# Optimizing a Trainium2 kernel written in Bass

```python
import numpy as np
import jax
import jax.numpy as jnp

def _softmax(x, axis=-1):
    return jax.nn.softmax(x, axis=axis)

def _gelu(x):
    return jax.nn.gelu(x, approximate=True)

def _silu(x):
    return jax.nn.silu(x)

def _sigmoid(x):
    return jax.nn.sigmoid(x)

def _layernorm(x, axis=-1, eps=1e-05):
    m = jnp.mean(x, axis=axis, keepdims=True)
    v = jnp.var(x, axis=axis, keepdims=True)
    return (x - m) / jnp.sqrt(v + eps)

def _scatter_add(tgt, idx, src, axis=0):
    return tgt.at[idx].add(src)

def _segment_sum(src, seg, n):
    return jax.ops.segment_sum(src, seg, n)
kernel_name = 'mk_gnn_preln_d2_gnn_r64_890c57'

def setup_inputs(seed: int=0):
    np.random.seed(seed)
    _w = jnp.asarray

    def _rec_inputs():
        import jax
        import jax.numpy as jnp
        _gk = jax.random.key(seed)
        x = -0.0003713 + 1 * jax.random.normal(jax.random.fold_in(_gk, 1), (50000, 256), jnp.float32)
        src = jax.random.randint(jax.random.fold_in(_gk, 2), (25000,), 0, 50000, jnp.int32)
        dst = jax.random.randint(jax.random.fold_in(_gk, 3), (25000,), 0, 50000, jnp.int32)
        _o = jnp.argsort(dst, stable=True)
        src = src[_o]
        dst = dst[_o]
        edge_attr_17 = jax.random.uniform(jax.random.fold_in(_gk, 11), (25000, 17), jnp.float32, 0.0, 1)
        return (x, src, dst, edge_attr_17)
    x, src, dst, edge_attr_17 = _rec_inputs()

    def _L0_gnn_setup():
        import jax, jax.numpy as jnp
        import numpy as np
        N, E = (50000, 12500)
        D_IN = 256
        D_HID = 128
        D_RAW = 16
        LN_EPS = 1e-05

        def _glorot(key, shape):
            fan_in, fan_out = (shape[0], shape[1])
            lim = float(np.sqrt(6.0 / (fan_in + fan_out)))
            return jax.random.uniform(key, shape, jnp.float32, -lim, lim)
        key = jax.random.key(seed)
        ks = jax.random.split(key, 12)
        x = jax.random.normal(ks[0], (N, D_IN), jnp.float32)
        edge_index = jax.random.randint(ks[1], (2, E), 0, N, jnp.int64)
        edge_attr = jax.random.uniform(ks[2], (E, 1 + D_RAW), jnp.float32)
        return {'x': x, 'edge_index': edge_index, 'edge_attr': edge_attr, 'ew1': _glorot(ks[3], (D_RAW, D_HID)), 'eb1': jnp.zeros((D_HID,), jnp.float32), 'ew2': _glorot(ks[4], (D_HID, D_HID)), 'eb2': jnp.zeros((D_HID,), jnp.float32), 'lew': _glorot(ks[5], (D_HID, D_IN)), 'leb': jnp.zeros((D_IN,), jnp.float32), 'w1': _glorot(ks[6], (D_IN, D_IN)), 'b1': jnp.zeros((D_IN,), jnp.float32), 'ln_g': jnp.ones((D_IN,), jnp.float32), 'ln_b': jnp.zeros((D_IN,), jnp.float32), 'w2': _glorot(ks[7], (D_IN, D_IN)), 'b2': jnp.zeros((D_IN,), jnp.float32)}
    _L0_gnn_all = _L0_gnn_setup()
    _L0_gnn_in = {k: v for k, v in _L0_gnn_all.items() if k in ('ew1', 'eb1', 'ew2', 'eb2', 'lew', 'leb', 'w1', 'b1', 'ln_g', 'ln_b', 'w2', 'b2')}
    del _L0_gnn_all

    def _L1_gnn_setup():
        import jax, jax.numpy as jnp
        import numpy as np
        N = 50000
        E = 25000
        D = 256
        H = 256
        EPS = 1e-05

        def _gnn_layer(x, row, col, W, b, g, beta):
            n = x.shape[0]
            neigh = x[col]
            agg = jax.ops.segment_sum(neigh, row, num_segments=n)
            deg = jax.ops.segment_sum(jnp.ones((row.shape[0],), x.dtype), row, num_segments=n)
            deg = jnp.maximum(deg, 1.0)[:, None]
            h = (x + agg / deg) @ W.T + b
            mu = jnp.mean(h, axis=-1, keepdims=True)
            var = jnp.mean(jnp.square(h - mu), axis=-1, keepdims=True)
            hn = (h - mu) * jax.lax.rsqrt(var + EPS) * g + beta
            return jax.nn.silu(hn)
        key = jax.random.key(seed)
        ks = jax.random.split(key, 12)
        x = jax.random.normal(ks[0], (N, D), dtype=jnp.float32)
        edge_index = jax.random.randint(ks[1], (2, E), 0, N, dtype=jnp.int32)
        s0 = 1.0 / np.sqrt(D)
        s1 = 1.0 / np.sqrt(H)
        W0 = jax.random.uniform(ks[2], (H, D), jnp.float32, -s0, s0)
        b0 = jax.random.uniform(ks[3], (H,), jnp.float32, -s0, s0)
        g0 = jnp.ones((H,), jnp.float32)
        beta0 = jnp.zeros((H,), jnp.float32)
        W1 = jax.random.uniform(ks[4], (H, H), jnp.float32, -s1, s1)
        b1 = jax.random.uniform(ks[5], (H,), jnp.float32, -s1, s1)
        g1 = jnp.ones((H,), jnp.float32)
        beta1 = jnp.zeros((H,), jnp.float32)
        return {'x': x, 'edge_index': edge_index, 'W0': W0, 'b0': b0, 'g0': g0, 'beta0': beta0, 'W1': W1, 'b1': b1, 'g1': g1, 'beta1': beta1}
    _L1_gnn_all = _L1_gnn_setup()
    _L1_gnn_in = {k: v for k, v in _L1_gnn_all.items() if k in ('W0', 'b0', 'g0', 'beta0', 'W1', 'b1', 'g1', 'beta1')}
    del _L1_gnn_all
    return {'x': x, 'src': src, 'dst': dst, 'edge_attr_17': edge_attr_17, 'L0_gnn_ew1': _L0_gnn_in['ew1'], 'L0_gnn_eb1': _L0_gnn_in['eb1'], 'L0_gnn_ew2': _L0_gnn_in['ew2'], 'L0_gnn_eb2': _L0_gnn_in['eb2'], 'L0_gnn_lew': _L0_gnn_in['lew'], 'L0_gnn_leb': _L0_gnn_in['leb'], 'L0_gnn_w1': _L0_gnn_in['w1'], 'L0_gnn_b1': _L0_gnn_in['b1'], 'L0_gnn_ln_g': _L0_gnn_in['ln_g'], 'L0_gnn_ln_b': _L0_gnn_in['ln_b'], 'L0_gnn_w2': _L0_gnn_in['w2'], 'L0_gnn_b2': _L0_gnn_in['b2'], 'L1_gnn_W0': _L1_gnn_in['W0'], 'L1_gnn_b0': _L1_gnn_in['b0'], 'L1_gnn_g0': _L1_gnn_in['g0'], 'L1_gnn_beta0': _L1_gnn_in['beta0'], 'L1_gnn_W1': _L1_gnn_in['W1'], 'L1_gnn_b1': _L1_gnn_in['b1'], 'L1_gnn_g1': _L1_gnn_in['g1'], 'L1_gnn_beta1': _L1_gnn_in['beta1']}

def reference(x, src, dst, edge_attr_17, L0_gnn_ew1, L0_gnn_eb1, L0_gnn_ew2, L0_gnn_eb2, L0_gnn_lew, L0_gnn_leb, L0_gnn_w1, L0_gnn_b1, L0_gnn_ln_g, L0_gnn_ln_b, L0_gnn_w2, L0_gnn_b2, L1_gnn_W0, L1_gnn_b0, L1_gnn_g0, L1_gnn_beta0, L1_gnn_W1, L1_gnn_b1, L1_gnn_g1, L1_gnn_beta1):
    import jax
    import jax.numpy as jnp

    def _L0_gnn_ref(x, edge_index, edge_attr, ew1, eb1, ew2, eb2, lew, leb, w1, b1, ln_g, ln_b, w2, b2):
        import jax, jax.numpy as jnp
        import numpy as np
        N, E = (50000, 12500)
        D_IN = 256
        D_HID = 128
        D_RAW = 16
        LN_EPS = 1e-05

        def _glorot(key, shape):
            fan_in, fan_out = (shape[0], shape[1])
            lim = float(np.sqrt(6.0 / (fan_in + fan_out)))
            return jax.random.uniform(key, shape, jnp.float32, -lim, lim)
        src, dst = (edge_index[0], edge_index[1])
        polarity = jnp.clip(edge_attr[:, 0:1], 0.0, 1.0)
        raw = edge_attr[:, 1:]
        e = jax.nn.relu(raw @ ew1 + eb1) @ ew2 + eb2
        gated = e * (polarity + 0.01)
        edge_emb = gated @ lew + leb
        msg = jax.nn.relu(x[src] + edge_emb)
        aggr = jax.ops.segment_sum(msg, dst, num_segments=x.shape[0])
        h = x + aggr
        h1 = h @ w1 + b1
        mu = jnp.mean(h1, axis=-1, keepdims=True)
        var = jnp.mean(jnp.square(h1 - mu), axis=-1, keepdims=True)
        h1 = (h1 - mu) * jax.lax.rsqrt(var + LN_EPS) * ln_g + ln_b
        return jax.nn.relu(h1) @ w2 + b2

    def _L1_gnn_ref(x, edge_index, W0, b0, g0, beta0, W1, b1, g1, beta1):
        import jax, jax.numpy as jnp
        import numpy as np
        N = 50000
        E = 25000
        D = 256
        H = 256
        EPS = 1e-05

        def _gnn_layer(x, row, col, W, b, g, beta):
            n = x.shape[0]
            neigh = x[col]
            agg = jax.ops.segment_sum(neigh, row, num_segments=n)
            deg = jax.ops.segment_sum(jnp.ones((row.shape[0],), x.dtype), row, num_segments=n)
            deg = jnp.maximum(deg, 1.0)[:, None]
            h = (x + agg / deg) @ W.T + b
            mu = jnp.mean(h, axis=-1, keepdims=True)
            var = jnp.mean(jnp.square(h - mu), axis=-1, keepdims=True)
            hn = (h - mu) * jax.lax.rsqrt(var + EPS) * g + beta
            return jax.nn.silu(hn)
        row, col = (edge_index[0], edge_index[1])
        x = _gnn_layer(x, row, col, W0, b0, g0, beta0)
        x = _gnn_layer(x, row, col, W1, b1, g1, beta1)
        return x
    edge_index = jnp.stack([src, dst])
    h = jnp.maximum(_layernorm(x, axis=-1), 0.0)
    x = x + _L0_gnn_ref(h, edge_index, edge_attr_17, L0_gnn_ew1, L0_gnn_eb1, L0_gnn_ew2, L0_gnn_eb2, L0_gnn_lew, L0_gnn_leb, L0_gnn_w1, L0_gnn_b1, L0_gnn_ln_g, L0_gnn_ln_b, L0_gnn_w2, L0_gnn_b2)
    h = jnp.maximum(_layernorm(x, axis=-1), 0.0)
    x = x + _L1_gnn_ref(h, edge_index, L1_gnn_W0, L1_gnn_b0, L1_gnn_g0, L1_gnn_beta0, L1_gnn_W1, L1_gnn_b1, L1_gnn_g1, L1_gnn_beta1)
    return x

_drawn_inputs = setup_inputs


def setup_inputs(seed=0):
    import zlib

    import numpy as np

    out = dict(_drawn_inputs(seed))
    spreads = {'L0_gnn_eb1': (0.0, 0.757),
     'L0_gnn_eb2': (0.0, 0.606),
     'L0_gnn_leb': (0.0, 0.304),
     'L0_gnn_b1': (0.0, 0.1),
     'L0_gnn_ln_g': (1.0, 0.2),
     'L0_gnn_ln_b': (0.0, 0.1),
     'L0_gnn_b2': (0.0, 0.1),
     'L1_gnn_g0': (1.0, 0.2),
     'L1_gnn_beta0': (0.0, 0.1),
     'L1_gnn_g1': (1.0, 0.2),
     'L1_gnn_beta1': (0.0, 0.1)}
    factors = {'edge_attr_17': 3.644}
    for name, (base, spread) in spreads.items():
        noise = np.random.default_rng([zlib.crc32(name.encode()), seed]).standard_normal(out[name].shape)
        drawn = base * np.exp(spread * noise) if base else spread * noise
        out[name] = jnp.asarray(drawn.astype(out[name].dtype))
    for name, factor in factors.items():
        out[name] = (out[name] * factor).astype(out[name].dtype)
    return out
```

```python
import concourse.bass as bass
from concourse import mybir
from contextlib import ExitStack

P = 128
D = 256
RAW = 16
EPS = 1e-5
NO_LANE = 512
NO_ROW = 1 << 20
NO_NODE = 1 << 23

F32 = mybir.dt.float32
BF16 = mybir.dt.bfloat16
I32 = mybir.dt.int32
ALU = mybir.AluOpType
ACT = mybir.ActivationFunctionType


def run_steps(eng, count, unroll, stages):
    deepest = max(lag for lag, _ in stages)
    first = deepest + unroll
    rounds = max(0, (count - 1 - first) // unroll)
    if rounds < 2:
        rounds = 0

    def outside(steps):
        for s in steps:
            for lag, body in stages:
                if 0 <= s - lag < count:
                    body(0, s - lag)

    outside(range(first))
    if rounds:
        with eng.Fori(0, rounds) as i:
            for u in range(unroll):
                for lag, body in stages:
                    body(i, first + u - lag)
    outside(range(first + rounds * unroll, count + deepest))


class Phase(ExitStack):

    def __init__(self, nc):
        super().__init__()
        self.nc, self.semaphores = nc, []
        self.callback(self.give_back)

    def sem(self, name):
        self.semaphores.append(self.nc.alloc_semaphore(name))
        return self.semaphores[-1]

    def give_back(self):
        self.nc.clear_and_free_semaphores(self.semaphores)
        self.nc.all_engine_barrier()


def anchor_on_pool(pool, tile):
    pool.tensor_tensor(tile[:, 0:1], tile[:, 1:2], tile[:, 1:2], ALU.mult)


def wait(eng, semaphore, value):
    if isinstance(value, int) and value <= 0:
        return
    eng.wait_ge(semaphore, value)


def program(nc, x, src, dst, attr, ew1, eb1, ew2, eb2, lew, leb, w1, b1, ln_g, ln_b, w2, b2,
            wt0, bb0, g0, beta0, wt1, bb1, g1, beta1, out):
    N = x.shape[0]
    E = src.shape[0]
    EC = -(-E // P)
    LAST = E - (P - 1) * EC
    assert 0 < LAST <= EC and EC % 4 == 0
    PAIRS = -(-N // 256)
    TAIL = (N - (PAIRS - 1) * 256) // 2
    assert N % 2 == 0
    NT = 2 * PAIRS

    MR = P * EC
    rows = nc.dram_tensor("rows", (MR + 2 * N, D), F32, kind="Internal").ap()
    msg_rows, h2_rows, y_rows = rows[0:MR, :], rows[MR:MR + N, :], rows[MR + N:, :]
    x1_rows = nc.dram_tensor("x1_rows", (N, D), F32, kind="Internal").ap()
    slots = {side: nc.dram_tensor(f"slots_{side}", (P * NT, 2), I32, kind="Internal").ap()
             for side in ("dst", "src")}

    whole = ExitStack()
    with whole:
        def keep(name, shape, dt):
            return whole.enter_context(nc.sbuf_tensor(name, shape, dt))

        iota = keep("iota", [P, max(NT, P)], F32)
        ident = keep("ident", [P, P], F32)
        ones16 = keep("ones16", [P, P], BF16)
        eps = keep("eps", [P, 1], F32)
        w_sb = {n: keep(n + "_sb", [P, 2, D], F32) for n in ("w1", "w2", "wt0", "wt1")}
        bias3 = {n: keep(n + "_3", [P, D], BF16) for n in ("b1", "b2", "bb0", "bb1")}
        lng_sb = keep("lng_sb", [P, 2], F32)
        lnb_sb = keep("lnb_sb", [P, 2], F32)
        wide = {n: keep(n + "_wide", [P, D], F32) for n in ("g0", "beta0", "g1", "beta1")}
        lane_of = {side: keep(f"lane_of_{side}", [P, NT], F32) for side in ("dst", "src")}
        row_of = {side: keep(f"row_of_{side}", [P, NT], I32) for side in ("dst", "src")}
        rdeg = keep("rdeg", [P, NT], F32)
        banks = [whole.enter_context(nc.psum_tensor(f"bank{n}", [P, 512], F32)) for n in range(8)]

        crowd = dict(
            key={side: keep(f"key_{side}", [P, EC], F32) for side in ("dst", "src")},
            entry={side: keep(f"entry_{side}", [P, EC, 2], I32) for side in ("dst", "src")},
            count={side: keep(f"crowded_{side}", [P, 1], I32) for side in ("dst", "src")},
            tiles={side: nc.dram_tensor(f"crowded_tiles_{side}", (2 * P, 1), I32, kind="Internal").ap()
                   for side in ("dst", "src")},
            lane=keep("lane", [P, 2], F32), most=max(1, min(E // (P + 1), NT)))
        assert E // (P + 1) <= 2 * P

        setup = dict(N=N, E=E, EC=EC, LAST=LAST, NT=NT)
        edges = ExitStack()
        with edges:
            def ek(name, shape, dt):
                return edges.enter_context(nc.sbuf_tensor(name, shape, dt))
            e = dict(
                ends={side: ek(f"ends_{side}", [P, EC], I32) for side in ("dst", "src")},
                tile={side: ek(f"tile_{side}", [P, EC], F32) for side in ("dst", "src")},
                entry=crowd["entry"], lane=crowd["lane"],
                place={side: ek(f"place_{side}", [P, EC], I32) for side in ("dst", "src")},
                before=ek("before", [P, P], BF16), rest=ek("rest", [P, P], BF16),
                attr=ek("attr_sb", [P, EC * 17], F32), gate=ek("gate", [P, EC], F32),
                xrow=ek("xrow_of_src", [P, EC], I32),
                ew1=ek("ew1_sb", [RAW, P], F32), ew2=ek("ew2_sb", [P, P], F32),
                lew=ek("lew_sb", [P, D], F32), eb1=ek("eb1_sb", [P, 1], F32),
                eb2=ek("eb2_sb", [P, 1], F32), leb=ek("leb_wide", [P, D], F32))
            load_and_prepare(nc, setup, e, iota, ident, ones16, eps, w_sb, bias3, lng_sb, lnb_sb, wide,
                             slots, dict(w1=w1, w2=w2, wt0=wt0, wt1=wt1, b1=b1, b2=b2, bb0=bb0, bb1=bb1,
                                         ln_g=ln_g, ln_b=ln_b, g0=g0, beta0=beta0, g1=g1, beta1=beta1,
                                         src=src, dst=dst, attr=attr, ew1=ew1, ew2=ew2, lew=lew,
                                         eb1=eb1, eb2=eb2, leb=leb))
            place_edges(nc, setup, e, iota, banks, crowd)
            messages(nc, setup, e, ident, eps, slots, x, msg_rows, banks)
        read_slots(nc, NT, slots, lane_of, row_of)
        crowded_tiles(nc, "A", "dst", EC, crowd, iota, lane_of, row_of, msg_rows, 0, banks)
        gated_block(nc, N, PAIRS, TAIL, iota, ident, ones16, eps, w_sb, bias3, lng_sb, lnb_sb,
                    lane_of["dst"], row_of["dst"], x, msg_rows, x1_rows, h2_rows, banks)
        crowded_tiles(nc, "B", "src", EC, crowd, iota, lane_of, row_of, rows[0:MR + N, :], 0, banks)
        mean_block(nc, "B", N, PAIRS, TAIL, iota, ident, ones16, eps, w_sb["wt0"], bias3["bb0"],
                   wide["g0"], wide["beta0"], lane_of["src"], row_of["src"], rdeg, h2_rows, rows[0:MR + N, :], None, y_rows, banks)
        name_rows_of_y(nc, MR, N, row_of["src"])
        crowded_tiles(nc, "C", "src", EC, crowd, iota, lane_of, row_of, rows, N, banks)
        mean_block(nc, "C", N, PAIRS, TAIL, iota, ident, ones16, eps, w_sb["wt1"], bias3["bb1"],
                   wide["g1"], wide["beta1"], lane_of["src"], row_of["src"], rdeg, y_rows, rows, x1_rows, out, banks)


def load_and_prepare(nc, dims, e, iota, ident, ones16, eps, w_sb, bias3, lng_sb, lnb_sb, wide, slots, a):
    N, EC, LAST, NT = dims["N"], dims["EC"], dims["LAST"], dims["NT"]
    own = Phase(nc)
    with own:
        def sb(name, shape, dt):
            return own.enter_context(nc.sbuf_tensor(name, shape, dt))

        def sem(name):
            return own.sem(name)

        empty = sb("empty", [P, NT, 2], I32)
        names = ("b1", "b2", "bb0", "bb1")
        raw = {n: sb(n + "_raw", [P, D], F32) for n in names}
        part = {n: sb(n + "_part", [P, D], BF16) for n in names}
        left = {n: sb(n + "_left", [P, D], F32) for n in names}
        odd = {s: sb(f"odd_{s}", [P, EC], F32) for s in ("dst", "src")}
        bit = {s: sb(f"bit_{s}", [P, EC], I32) for s in ("dst", "src")}
        high = {s: sb(f"high_{s}", [P, EC], I32) for s in ("dst", "src")}

        weights_in = sem("weights_in")
        biases_in = sem("biases_in")
        ends_in = sem("ends_in")
        attr_in = sem("attr_in")
        padded = sem("padded")
        empty_made = sem("empty_made")
        empty_out = sem("empty_out")
        made = sem("made")
        split = sem("split")
        ended = sem("ended")
        numbered = sem("numbered")

        sets = [(w_sb[n][:, :, :], a[n].rearrange("(c p) n -> p c n", p=P)) for n in ("w1", "w2", "wt0", "wt1")]
        sets += [(e["ew1"][:, :], a["ew1"]), (e["ew2"][:, :], a["ew2"]), (e["lew"][:, :], a["lew"]),
                 (lng_sb[:, :], a["ln_g"].rearrange("(c p) -> p c", p=P)),
                 (lnb_sb[:, :], a["ln_b"].rearrange("(c p) -> p c", p=P)),
                 (e["eb1"][:, :], a["eb1"].rearrange("(p c) -> p c", c=1)),
                 (e["eb2"][:, :], a["eb2"].rearrange("(p c) -> p c", c=1)),
                 (e["leb"][:, :], a["leb"].partition_broadcast(P))]
        sets += [(wide[n][:, :], a[n].partition_broadcast(P)) for n in ("g0", "beta0", "g1", "beta1")]
        parts = [(0, 112), (112, P - 1)]

        with nc.Block() as block:
            @block.sync
            def _(sp):
                sp.wait_ge(padded, 3)
                for side in ("dst", "src"):
                    v = a[side]
                    for lo, hi in parts:
                        sp.dma_start(e["ends"][side][lo:hi, :],
                                     v[lo * EC:hi * EC].rearrange("(p c) -> p c", c=EC)).then_inc(ends_in, 16)
                    sp.dma_start(e["ends"][side][P - 1:P, 0:LAST],
                                 v[(P - 1) * EC:].rearrange("(p c) -> p c", p=1)).then_inc(ends_in, 16)
                for lo, hi in parts:
                    sp.dma_start(e["attr"][lo:hi, :],
                                 a["attr"][lo * EC:hi * EC, :].rearrange("(p c) f -> p (c f)", c=EC)).then_inc(attr_in, 16)
                sp.dma_start(e["attr"][P - 1:P, 0:LAST * 17],
                             a["attr"][(P - 1) * EC:, :].rearrange("(p c) f -> p (c f)", p=1)).then_inc(attr_in, 16)
                sp.wait_ge(empty_made, 2)
                for side in ("dst", "src"):
                    sp.dma_start(slots[side].rearrange("(p t) w -> p (t w)", t=NT),
                                 empty[:, :, :].rearrange("p t w -> p (t w)")).then_inc(empty_out, 16)
                sp.wait_ge(empty_out, 32)
                sp.wait_ge(attr_in, 48)

            @block.scalar
            def _(act):
                for n in names:
                    for row in (0, 32, 64):
                        act.dma_start(raw[n][row:row + 1, :], a[n].rearrange("(p c) -> p c", p=1)).then_inc(biases_in, 16)
                with nc.allow_non_contiguous_dma(reason="per-feature scales, 256 numbers each"):
                    for to, of in sets:
                        act.dma_start(to, of).then_inc(weights_in, 16)
                act.wait_ge(weights_in, 16 * len(sets))

            @block.gpsimd
            def _(pool):
                pool.memset(e["ends"]["dst"][:, :], NO_NODE).then_inc(padded, 1)
                pool.memset(e["ends"]["src"][:, :], NO_NODE).then_inc(padded, 1)
                pool.memset(e["attr"][:, :], 0.0).then_inc(padded, 1)
                pool.memset(empty[:, :, 0], NO_LANE).then_inc(empty_made, 1)
                pool.memset(empty[:, :, 1], NO_ROW).then_inc(empty_made, 1)
                pool.memset(ident[:, :], 1.0).then_inc(made, 1)
                pool.memset(e["before"][:, :], 1.0).then_inc(made, 1)
                pool.memset(e["rest"][:, :], 1.0).then_inc(made, 1)
                pool.memset(ones16[:, :], 1.0)
                pool.memset(eps[:, :], EPS)
                pool.iota(iota[:, :], [[1, max(NT, P)]], base=0, channel_multiplier=0, allow_small_or_imprecise_dtypes=True)
                pool.iota(e["entry"]["dst"][:, :, 1], [[1, EC]], base=0, channel_multiplier=EC)
                pool.iota(e["lane"][:, :], [[P, 2]], base=0, channel_multiplier=1, allow_small_or_imprecise_dtypes=True)
                pool.wait_ge(made, 3)
                pool.affine_select(out=ident[:, :], in_=ident[:, :], compare_op=ALU.is_equal, fill=0.0,
                                   base=0, pattern=[[-1, P]], channel_multiplier=1)
                pool.affine_select(out=e["before"][:, :], in_=e["before"][:, :], compare_op=ALU.is_gt, fill=0.0,
                                   base=0, pattern=[[1, P]], channel_multiplier=-1)
                pool.affine_select(out=e["rest"][:, :], in_=e["rest"][:, :], compare_op=ALU.is_ge, fill=0.0,
                                   base=0, pattern=[[-1, P]], channel_multiplier=1)

            @block.vector
            def _(dve):
                for n in names:
                    dve.memset(bias3[n][:, :], 0.0).then_inc(split, 1)
                dve.wait_ge(ends_in, 96)
                for side in ("dst", "src"):
                    ends = e["ends"][side]
                    dve.tensor_scalar(high[side][:, :], ends[:, :], 8, None, ALU.logical_shift_right).then_inc(numbered, 1)
                    dve.tensor_scalar(bit[side][:, :], ends[:, :], 1, None, ALU.bitwise_and).then_inc(numbered, 1)
                    dve.tensor_scalar(e["entry"][side][:, :, 0], ends[:, :], 1, P - 1, ALU.logical_shift_right,
                                      ALU.bitwise_and).then_inc(ended, 1)
                dve.tensor_scalar(e["xrow"][:, :], e["ends"]["src"][:, :], NO_ROW, None, ALU.min)
                dve.tensor_scalar(e["entry"]["src"][:, :, 1], e["ends"]["dst"][:, :], float(P * EC), None, ALU.add)
                dve.wait_ge(numbered, 4)
                for side in ("dst", "src"):
                    dve.scalar_tensor_tensor(out=e["tile"][side][:, :], in0=high[side][:, :], scalar=2.0,
                                             in1=bit[side][:, :], op0=ALU.mult, op1=ALU.add)
                dve.wait_ge(biases_in, 16 * 3 * len(names))
                top = 65
                step = [4]

                def link(ins):
                    step[0] += 1
                    ins.then_inc(split, 1)
                for n in names:
                    for lane in (0, 32, 64):
                        row = slice(lane, lane + 1)
                        if lane == 0:
                            dve.wait_ge(split, step[0])
                            dve.tensor_copy(bias3[n][row, :], raw[n][row, :])
                            continue
                        link(dve.tensor_copy(part[n][row, :], raw[n][row, :]))
                        dve.wait_ge(split, step[0])
                        link(dve.tensor_tensor(left[n][row, :], raw[n][row, :], part[n][row, :], ALU.subtract))
                        dve.wait_ge(split, step[0])
                        if lane == 32:
                            dve.tensor_copy(bias3[n][row, :], left[n][row, :])
                            continue
                        link(dve.tensor_copy(part[n][row, :], left[n][row, :]))
                        dve.wait_ge(split, step[0])
                        link(dve.tensor_tensor(raw[n][row, :], left[n][row, :], part[n][row, :], ALU.subtract))
                        dve.wait_ge(split, step[0])
                        dve.tensor_copy(bias3[n][row, :], raw[n][row, :])
                dve.wait_ge(attr_in, 48)
                pol = e["attr"][:, :].rearrange("p (c f) -> p c f", f=17)[:, :, 0]
                link(dve.tensor_scalar(e["gate"][:, :], pol, 0.0, 1.0, ALU.max, ALU.min))
                dve.wait_ge(split, step[0])
                dve.tensor_scalar(e["gate"][:, :], e["gate"][:, :], 0.01, None, ALU.add)


def place_edges(nc, dims, e, iota, banks, crowd):
    EC, NT = dims["EC"], dims["NT"]
    U = 2
    own = Phase(nc)
    with own:
        def sb(name, shape, dt):
            return own.enter_context(nc.sbuf_tensor(name, shape, dt))

        def sem(name):
            return own.sem(name)
        sides = ("dst", "src")
        hot = {s: [sb(f"hot_{s}{n}", [P, NT], BF16) for n in range(U)] for s in sides}
        rank = {s: sb(f"rank_{s}", [P, EC], F32) for s in sides}
        picked = {s: [sb(f"picked_{s}{n}", [P, NT], BF16) for n in range(2)] for s in sides}
        counted = dict(zip(sides, banks))
        zero = sb("zero", [P, NT], BF16)
        over = {s: sb(f"over_{s}", [P, NT], F32) for s in sides}
        running = {s: sb(f"running_{s}", [P, NT], F32) for s in sides}
        below = {s: [sb(f"below_{s}{g}", [P, NT], F32) for g in range(2)] for s in sides}
        nth = {s: sb(f"nth_{s}", [P, 2], F32) for s in sides}
        nth_i = {s: sb(f"nth_i_{s}", [P, 2], I32) for s in sides}
        listed = sem("listed")
        list_out = sem("list_out")
        zeroed = sem("zeroed")
        hot_made = {s: sem(f"hot_made_{s}") for s in sides}
        added = {s: sem(f"added_{s}") for s in sides}
        ranked = {s: sem(f"ranked_{s}") for s in sides}
        totalled = {s: sem(f"totalled_{s}") for s in sides}

        with nc.Block() as block:
            @block.vector
            def _(dve):
                dve.memset(zero[:, :], 0.0).then_inc(zeroed, 1)

                def one_hot(i, c):
                    n = U * i + c
                    for s in sides:
                        wait(dve, totalled[s], n - U + 1)
                        dve.tensor_scalar(hot[s][c % U][:, :], iota[:, 0:NT], e["tile"][s][:, bass.ds(n, 1)], None,
                                          ALU.is_equal).then_inc(hot_made[s], 1)

                def read_rank(i, c):
                    n = U * i + c
                    for s in sides:
                        dve.wait_ge(added[s], n + 1)
                        wait(dve, ranked[s], n - 1)
                        dve.scalar_tensor_tensor(out=picked[s][c % 2][:, :], in0=iota[:, 0:NT],
                                                 scalar=e["tile"][s][:, bass.ds(n, 1)], in1=counted[s][:, 0:NT],
                                                 op0=ALU.is_equal, op1=ALU.mult,
                                                 accum_out=rank[s][:, bass.ds(n, 1)]).then_inc(ranked[s], 1)

                run_steps(dve, EC, U, [(0, one_hot), (1, read_rank)])
                for s in sides:
                    dve.wait_ge(ranked[s], EC)
                    dve.scalar_tensor_tensor(out=e["place"][s][:, :], in0=rank[s][:, :], scalar=float(NT),
                                             in1=e["tile"][s][:, :], op0=ALU.mult, op1=ALU.add)
                    dve.scalar_tensor_tensor(out=crowd["key"][s][:, :], in0=e["tile"][s][:, :], scalar=float(P),
                                             in1=e["entry"][s][:, :, 0], op0=ALU.mult, op1=ALU.add)
                    dve.wait_ge(totalled[s], EC)
                    dve.tensor_scalar(over[s][:, :], counted[s][:, 0:NT], float(P), None, ALU.is_gt).then_inc(listed, 1)
                    at = 5 * sides.index(s)
                    dve.wait_ge(listed, at + 1)
                    dve.tensor_tensor_scan(running[s][:, :], over[s][:, :], over[s][:, :], 0.0, ALU.add,
                                           ALU.bypass).then_inc(listed, 1)
                    dve.wait_ge(listed, at + 2)
                    dve.tensor_copy(crowd["count"][s][:, :], running[s][:, NT - 1:NT])
                    for g in range(2):
                        dve.tensor_scalar(below[s][g][:, :], running[s][:, :], crowd["lane"][:, g:g + 1], 0.0, ALU.is_le,
                                          ALU.add, accum_out=nth[s][:, g:g + 1]).then_inc(listed, 1)
                    dve.wait_ge(listed, at + 4)
                    dve.tensor_copy(nth_i[s][:, :], nth[s][:, :]).then_inc(listed, 1)

            @block.sync
            def _(sp):
                for n, s in enumerate(sides):
                    sp.wait_ge(listed, 5 * n + 5)
                    sp.dma_start(crowd["tiles"][s].rearrange("(g p) w -> p (g w)", p=P), nth_i[s][:, :],
                                 allow_slow_non_contiguous=True).then_inc(list_out, 16)
                sp.wait_ge(list_out, 32)

            @block.tensor
            def _(pe):
                pe.wait_ge(zeroed, 1)
                for s in sides:
                    pe.matmul(counted[s][:, 0:NT], e["before"][:, :], zero[:, :], start=True, stop=True)

                def add_earlier_lanes(i, c):
                    n = U * i + c
                    for s in sides:
                        pe.wait_ge(hot_made[s], n + 1)
                        pe.matmul(counted[s][:, 0:NT], e["before"][:, :], hot[s][c % U][:, :], start=False,
                                  stop=True, skip_group_check=True).then_inc(added[s], 1)

                def add_the_rest(i, c):
                    n = U * i + c
                    for s in sides:
                        pe.wait_ge(ranked[s], n + 1)
                        pe.matmul(counted[s][:, 0:NT], e["rest"][:, :], hot[s][c % U][:, :], start=False,
                                  stop=True, skip_group_check=True).then_inc(totalled[s], 1)

                run_steps(pe, EC, U, [(0, add_earlier_lanes), (0, add_the_rest)])


def messages(nc, dims, e, ident, eps, slots, x, msg_rows, banks):
    N, EC, NT = dims["N"], dims["EC"], dims["NT"]
    G = 4
    U = 4
    K = EC // G
    own = Phase(nc)
    with own:
        def sb(name, shape, dt):
            return own.enter_context(nc.sbuf_tensor(name, shape, dt))

        def sem(name):
            return own.sem(name)
        PADDED = G * 17 + P
        place_now = {s: [sb(f"place_now_{s}{n}", [P, G], I32) for n in range(2)] for s in slots}
        entry_now = {s: [sb(f"entry_now_{s}{n}", [P, G * 2], I32) for n in range(2)] for s in slots}
        attr_now = [sb(f"attr_now{n}", [P, PADDED], F32) for n in range(2)]
        row_now = [sb(f"row_now{n}", [P, G], I32) for n in range(4)]
        xg = [sb(f"xg{n}", [P, G, D], F32) for n in range(4)]
        raw_t = [sb(f"raw_t{n}", [RAW, G * P], F32) for n in range(2)]
        e1_t = [sb(f"e1_t{n}", [P, G * P], F32) for n in range(2)]
        e2_t = [sb(f"e2_t{n}", [P, G * P], F32) for n in range(2)]
        anchor = sb("e_anchor", [P, 1], F32)
        tick = sb("e_tick", [P, 2], F32)
        ticked = sem("ticked")
        stats = [sb(f"e_stats{n}", [P, G, 6], F32) for n in range(2)]
        mv = [sb(f"e_mv{n}", [P, G, 2], F32) for n in range(2)]
        std = [sb(f"e_std{n}", [P, G], F32) for n in range(2)]
        rstd = [sb(f"e_rstd{n}", [P, G], F32) for n in range(2)]
        nmr = [sb(f"e_nmr{n}", [P, G], F32) for n in range(2)]
        hs = [sb(f"hs{n}", [P, G, D], F32) for n in range(2)]
        emb = [sb(f"emb{n}", [P, G, D], F32) for n in range(2)]
        msg = [sb(f"msg{n}", [P, G, D], F32) for n in range(2)]
        raw_ps, e1_ps, e2_ps = banks[0:3]
        emb_ps = [banks[3:5], banks[5:7]]

        placed_now = {s: sem(f"placed_now_{s}") for s in slots}
        scattered = {s: [sem(f"scattered_{s}{n}") for n in range(2)] for s in slots}
        cleared = sem("cleared")
        attr_copied = sem("attr_copied")
        rows_copied = sem("rows_copied")
        gathered = [sem(f"x_gathered{n}") for n in range(4)]
        turned = sem("turned")
        raw_ready = sem("raw_ready")
        e1_done = sem("e1_done")
        e1_ready = sem("e1_ready")
        e2_done = sem("e2_done")
        e2_ready = sem("e2_ready")
        emb_done = sem("emb_done")
        stats_done = sem("e_stats_done")
        mv_done = sem("e_mv_done")
        std_done = sem("e_std_done")
        rstd_done = sem("e_rstd_done")
        nmr_done = sem("e_nmr_done")
        hs_ready = sem("hs_ready")
        emb_scaled = sem("emb_scaled")
        summed = sem("summed")
        msg_ready = sem("msg_ready")
        stored = [sem(f"msg_stored{n}") for n in range(2)]
        ROUNDS = 2 * K

        with nc.Block() as block:
            @block.gpsimd
            def _(pool):
                pool.memset(tick[:, :], 0.0).then_inc(ticked, 1)
                pool.wait_ge(ticked, 1)
                for b in attr_now:
                    pool.memset(b[:, :], 0.0).then_inc(cleared, 1)
                for b in xg:
                    pool.memset(b[:, :, :], 0.0).then_inc(cleared, 1)
                pool.wait_ge(cleared, 6)

                def scatter(side):
                    def body(i, c):
                        m = 2 * i + c
                        wait(pool, scattered[side][c % 2], 16 * G * (i + c // 2))
                        pool.tensor_copy(place_now[side][c % 2][:, :], e["place"][side][:, bass.ds(G * m, G)]).then_inc(placed_now[side], 1)
                        pool.tensor_copy(entry_now[side][c % 2][:, :],
                                         e["entry"][side][:, bass.ds(G * m, G), :].rearrange("p c w -> p (c w)")).then_inc(placed_now[side], 1)
                        pool.wait_ge(placed_now[side], 2 * m + 2)
                        anchor_on_pool(pool, tick)
                        for u in range(G):
                            pool.indirect_dma_start(
                                out=slots[side], out_offset=bass.IndirectOffsetOnAxis(ap=place_now[side][c % 2][:, u:u + 1], axis=0),
                                in_=entry_now[side][c % 2][:, 2 * u:2 * u + 2], in_offset=None,
                                bounds_check=P * NT - 1, oob_is_err=False).then_inc(scattered[side][c % 2], 16)
                    return body

                run_steps(pool, K, 2, [(0, scatter("dst"))])
                run_steps(pool, K, 2, [(0, scatter("src"))])

                def gather(i, c):
                    k = U * i + c
                    wait(pool, turned, k - 1)
                    pool.tensor_copy(attr_now[c % 2][:, 0:G * 17], e["attr"][:, bass.ds(G * 17 * k, G * 17)]).then_inc(attr_copied, 1)
                    wait(pool, gathered[c % 4], 16 * G * (i + c // 4))
                    pool.tensor_copy(row_now[c % 4][:, :], e["xrow"][:, bass.ds(G * k, G)]).then_inc(rows_copied, 1)
                    pool.wait_ge(rows_copied, k + 1)
                    wait(pool, hs_ready, k - 3)
                    anchor_on_pool(pool, tick)
                    for u in range(G):
                        pool.indirect_dma_start(
                            out=xg[c % 4][:, u, :], out_offset=None, in_=x,
                            in_offset=bass.IndirectOffsetOnAxis(ap=row_now[c % 4][:, u:u + 1], axis=0),
                            bounds_check=N - 1, oob_is_err=False).then_inc(gathered[c % 4], 16)

                run_steps(pool, K, U, [(0, gather)])
                for side in slots:
                    for n in range(2):
                        pool.wait_ge(scattered[side][n], 16 * G * ((K + 1 - n) // 2))

            @block.tensor
            def _(pe):
                def turn(i, c):
                    k = U * i + c
                    pe.wait_ge(attr_copied, k + 1)
                    wait(pe, raw_ready, k)
                    for u in range(G):
                        last = pe.matmul(raw_ps[:, u * P:(u + 1) * P], attr_now[c % 2][:, 17 * u + 1:17 * u + 1 + P],
                                         ident[:, :], is_transpose=True, start=True, stop=True)
                    last.then_inc(turned, 1)

                def first(i, c):
                    k = U * i + c
                    pe.wait_ge(raw_ready, k + 1)
                    wait(pe, e1_ready, k)
                    pe.matmul(e1_ps[:, :], e["ew1"][:, :], raw_t[c % 2][:, :], start=True, stop=True).then_inc(e1_done, 1)

                def second(i, c):
                    k = U * i + c
                    pe.wait_ge(e1_ready, k + 1)
                    wait(pe, e2_ready, k)
                    pe.matmul(e2_ps[:, :], e["ew2"][:, :], e1_t[c % 2][:, :], start=True, stop=True).then_inc(e2_done, 1)

                def embed(i, c):
                    k = U * i + c
                    pe.wait_ge(e2_ready, k + 1)
                    wait(pe, emb_scaled, k - 1)
                    for u in range(G):
                        last = pe.matmul(emb_ps[c % 2][u // 2][:, u % 2 * D:(u % 2 + 1) * D], e2_t[c % 2][:, u * P:(u + 1) * P],
                                         e["lew"][:, :], start=True, stop=True)
                    last.then_inc(emb_done, 1)

                run_steps(pe, K, U, [(0, turn), (1, first), (2, second), (3, embed)])

            @block.scalar
            def _(act):
                def raw_out(i, c):
                    k = U * i + c
                    wait(act, e1_done, k - 1)
                    act.wait_ge(turned, k + 1)
                    act.activation(raw_t[c % 2][:, :], raw_ps[0:RAW, :], ACT.Copy).then_inc(raw_ready, 1)

                def e1_out(i, c):
                    k = U * i + c
                    wait(act, e2_done, k - 1)
                    act.wait_ge(e1_done, k + 1)
                    act.activation(e1_t[c % 2][:, :], e1_ps[:, :], ACT.Relu, bias=e["eb1"][:, 0:1]).then_inc(e1_ready, 1)

                def e2_out(i, c):
                    k = U * i + c
                    wait(act, emb_done, k - 1)
                    act.wait_ge(e2_done, k + 1)
                    act.activation(e2_t[c % 2][:, :], e2_ps[:, :], ACT.Identity, bias=e["eb2"][:, 0:1]).then_inc(e2_ready, 1)

                def root(i, c):
                    k = U * i + c
                    wait(act, rstd_done, k - 1)
                    act.wait_ge(mv_done, k + 1)
                    act.activation(std[c % 2][:, :], mv[c % 2][:, :, 1], ACT.Sqrt, bias=eps[:, 0:1]).then_inc(std_done, 1)

                def normalise(i, c):
                    k = U * i + c
                    wait(act, summed, k - 1)
                    act.wait_ge(nmr_done, k + 1)
                    for u in range(G):
                        last = act.activation(hs[c % 2][:, u, :], xg[c % 4][:, u, :], ACT.Relu,
                                              bias=nmr[c % 2][:, u:u + 1], scale=rstd[c % 2][:, u:u + 1])
                    last.then_inc(hs_ready, 1)

                def message(i, c):
                    k = U * i + c
                    wait(act, stored[c % 2], 16 * (2 * i + c // 2))
                    act.wait_ge(summed, k + 1)
                    act.activation(msg[c % 2][:, :, :], emb[c % 2][:, :, :], ACT.Relu).then_inc(msg_ready, 1)

                run_steps(act, K, U, [(0, raw_out), (1, e1_out), (2, e2_out), (2, root), (3, normalise), (4, message)])

            @block.vector
            def _(dve):
                def take_stats(i, c):
                    k = U * i + c
                    wait(dve, mv_done, k - 1)
                    dve.wait_ge(gathered[c % 4], 16 * G * (i + c // 4 + 1))
                    for u in range(G):
                        last = dve.bn_stats(stats[c % 2][:, u, :], xg[c % 4][:, u, :])
                    last.then_inc(stats_done, 1)

                def add(i, c):
                    k = U * i + c
                    dve.wait_ge(emb_scaled, k + 1)
                    dve.wait_ge(hs_ready, k + 1)
                    dve.tensor_tensor(emb[c % 2][:, :, :], emb[c % 2][:, :, :], hs[c % 2][:, :, :], ALU.add).then_inc(summed, 1)

                def aggregate(i, c):
                    k = U * i + c
                    wait(dve, nmr_done, k - 1)
                    wait(dve, hs_ready, k - 1)
                    dve.wait_ge(stats_done, k + 1)
                    dve.tensor_copy(anchor[:, :], eps[:, :])
                    for u in range(G):
                        last = dve.bn_aggr(mv[c % 2][:, u, :], stats[c % 2][:, u, :])
                    last.then_inc(mv_done, 1)

                def scale(i, c):
                    k = U * i + c
                    wait(dve, msg_ready, k - 1)
                    dve.wait_ge(emb_done, k + 1)
                    for u in range(G):
                        last = dve.scalar_tensor_tensor(out=emb[c % 2][:, u, :], in0=emb_ps[c % 2][u // 2][:, u % 2 * D:(u % 2 + 1) * D],
                                                        scalar=e["gate"][:, bass.ds(G * k + u, 1)], in1=e["leb"][:, :],
                                                        op0=ALU.mult, op1=ALU.add)
                    last.then_inc(emb_scaled, 1)

                def factors(i, c):
                    k = U * i + c
                    wait(dve, hs_ready, k - 1)
                    dve.wait_ge(std_done, k + 1)
                    dve.reciprocal(rstd[c % 2][:, :], std[c % 2][:, :]).then_inc(rstd_done, 1)
                    dve.wait_ge(rstd_done, k + 1)
                    dve.scalar_tensor_tensor(out=nmr[c % 2][:, :], in0=mv[c % 2][:, :, 0], scalar=-1.0,
                                             in1=rstd[c % 2][:, :], op0=ALU.mult, op1=ALU.mult).then_inc(nmr_done, 1)

                run_steps(dve, K, U, [(2, take_stats), (4, add), (2, aggregate), (3, scale), (2, factors)])

            @block.sync
            def _(sp):
                rows = msg_rows[0:P * EC, :].rearrange("(p c) d -> p (c d)", c=EC)

                def store(i, c):
                    k = U * i + c
                    sp.wait_ge(msg_ready, k + 1)
                    sp.dma_start(rows[:, bass.ds(G * D * k, G * D)],
                                 msg[c % 2][:, :, :].rearrange("p g d -> p (g d)")).then_inc(stored[c % 2], 16)

                run_steps(sp, K, U, [(0, store)])
                sp.wait_ge(stored[0], 16 * ((K + 1) // 2))
                sp.wait_ge(stored[1], 16 * (K // 2))


def read_slots(nc, NT, slots, lane_of, row_of):
    own = Phase(nc)
    with own:
        both = {s: own.enter_context(nc.sbuf_tensor(f"both_{s}", [P, NT, 2], I32)) for s in slots}
        came = {s: own.sem(f"slots_in_{s}") for s in slots}
        with nc.Block() as block:
            @block.sync
            def _(sp):
                for s in slots:
                    sp.dma_start(both[s][:, :, :].rearrange("p t w -> p (t w)"),
                                 slots[s].rearrange("(p t) w -> p (t w)", t=NT)).then_inc(came[s], 16)

            @block.vector
            def _(dve):
                for s in slots:
                    dve.wait_ge(came[s], 16)
                    dve.tensor_copy(lane_of[s][:, :], both[s][:, :, 0])
                    dve.tensor_copy(row_of[s][:, :], both[s][:, :, 1])


def name_rows_of_y(nc, first, N, row_of):
    own = Phase(nc)
    with own:
        later = own.enter_context(nc.sbuf_tensor("later", list(row_of.shape), F32))
        compared = own.sem("compared")
        with nc.Block() as block:
            @block.vector
            def _(dve):
                dve.tensor_scalar(later[:, :], row_of[:, :], float(first), float(N), ALU.is_ge, ALU.mult).then_inc(compared, 1)
                dve.wait_ge(compared, 1)
                dve.tensor_tensor(row_of[:, :], row_of[:, :], later[:, :], ALU.add)


def crowded_tiles(nc, name, side, EC, crowd, iota, lane_of, row_of, table, shift, banks):
    own = Phase(nc)
    mean = name != "A"
    with own:
        def sb(n, shape, dt=F32):
            return own.enter_context(nc.sbuf_tensor(f"crowd{name}_{n}", shape, dt))

        def sem(n):
            return own.sem(f"crowd{name}_{n}")
        tile_i = sb("tile_i", [P, 1], I32)
        shift_i = sb("shift_i", [P, 1], I32)
        offset = sb("offset", [P, 1])
        place = sb("place", [P, 1])
        column = sb("column", [P, 1])
        anchor = sb("anchor", [P, 1])
        row_now = sb("row_now", [P, 1], I32)
        target = sb("target", [P, 1], I32)
        rows = sb("rows", [P, D])
        hot = sb("hot", [P, P])
        total = sb("total", [P, D])
        degree = sb("degree", [P, 2])
        ones = sb("ones", [P, 1])
        tick = sb("tick", [P, 2])
        sum_ps, deg_ps = banks[0], banks[1]
        ticked = sem("ticked")
        tile_free = sem("tile_free")
        tile_in = sem("tile_in")
        offset_ready = sem("offset_ready")
        column_ready = sem("column_ready")
        hot_made = sem("hot_made")
        row_copied = sem("row_copied")
        gathered = sem("gathered")
        product_done = sem("product_done")
        emptied = sem("emptied")
        added = sem("added")
        counted = sem("counted")
        ratio_ready = sem("ratio_ready")
        placed = sem("placed")
        target_copied = sem("target_copied")
        result_ready = sem("result_ready")
        result_out = sem("result_out")
        tiles = crowd["tiles"][side]
        most = crowd["most"]
        last_tile = lane_of[side].shape[1] - 1

        with nc.Block() as block:
            @block.scalar
            def _(act):
                count = act.value_load(crowd["count"][side][0:1, 0:1], min_val=0, max_val=most)
                with act.If(count > 0):
                    with act.Fori(0, count) as j:
                        act.wait_ge(tile_free, j + 1)
                        act.dma_start(tile_i[:, :], tiles[bass.ds(j, 1), :].partition_broadcast(P)
                                     .rearrange("p a b -> p (a b)")).then_inc(tile_in, 16)
                        if mean:
                            act.wait_ge(result_ready, j + 1)
                            act.dma_start(table[bass.ds(j * P, P), :], total[:, :]).then_inc(result_out, 16)

            @block.gpsimd
            def _(pool):
                pool.memset(tick[:, :], 0.0).then_inc(ticked, 1)
                pool.memset(rows[:, :], 0.0).then_inc(ticked, 1)
                pool.memset(shift_i[:, :], shift).then_inc(ticked, 1)
                pool.wait_ge(ticked, 3)
                count = pool.value_load(crowd["count"][side][0:1, 0:1], min_val=0, max_val=most)
                with pool.If(count > 0):
                    with pool.Fori(0, count) as j:
                        with pool.Fori(0, EC) as c:
                            n = j * EC + c
                            pool.tensor_tensor(row_now[:, :], crowd["entry"][side][:, bass.ds(c, 1), 1], shift_i[:, :],
                                               ALU.add).then_inc(row_copied, 1)
                            pool.wait_ge(row_copied, n + 1)
                            anchor_on_pool(pool, tick)
                            pool.indirect_dma_start(
                                out=rows[:, :], out_offset=None, in_=table,
                                in_offset=bass.IndirectOffsetOnAxis(ap=row_now[:, 0:1], axis=0),
                                bounds_check=table.shape[0] - 1, oob_is_err=False).then_inc(gathered, 16)
                            pool.wait_ge(product_done, n + 1)
                        if not mean:
                            t = pool.value_load(tiles[bass.ds(j, 1), :], min_val=0, max_val=last_tile)
                            pool.tensor_copy(target[:, :], row_of[side][:, bass.ds(t, 1)]).then_inc(target_copied, 1)
                            pool.wait_ge(target_copied, j + 1)
                            pool.wait_ge(result_ready, j + 1)
                            anchor_on_pool(pool, tick)
                            pool.indirect_dma_start(
                                out=table, out_offset=bass.IndirectOffsetOnAxis(ap=target[:, 0:1], axis=0),
                                in_=total[:, :], in_offset=None,
                                bounds_check=table.shape[0] - 1, oob_is_err=False).then_inc(result_out, 16)
                            pool.wait_ge(result_out, 16 * j + 16)

            @block.tensor
            def _(pe):
                count = pe.value_load(crowd["count"][side][0:1, 0:1], min_val=0, max_val=most)
                with pe.If(count > 0):
                    with pe.Fori(0, count) as j:
                        with pe.Fori(0, EC) as c:
                            n = j * EC + c
                            pe.wait_ge(hot_made, n + 1)
                            pe.wait_ge(gathered, 16 * n + 16)
                            pe.matmul(deg_ps[:, 0:1], hot[:, :], ones[:, 0:1], start=True, stop=True)
                            pe.matmul(sum_ps[:, 0:D], hot[:, :], rows[:, :], start=True, stop=True).then_inc(product_done, 1)
                            pe.wait_ge(added, n + 1)
                            pe.wait_ge(counted, n + 1)

            @block.vector
            def _(dve):
                dve.memset(ones[:, :], 1.0).then_inc(tile_free, 1)
                dve.tensor_copy(place[:, :], crowd["lane"][:, 0:1]).then_inc(placed, 1)
                count = dve.value_load(crowd["count"][side][0:1, 0:1], min_val=0, max_val=most)
                with dve.If(count > 0):
                    with dve.Fori(0, count) as j:
                        t = dve.value_load(tiles[bass.ds(j, 1), :], min_val=0, max_val=last_tile)
                        dve.wait_ge(tile_in, 16 * j + 16)
                        dve.tensor_scalar(offset[:, :], tile_i[:, :], float(P), None, ALU.mult).then_inc(offset_ready, 1)
                        dve.memset(total[:, :], 0.0).then_inc(emptied, 1)
                        dve.memset(degree[:, :], 0.0).then_inc(emptied, 1)
                        dve.wait_ge(offset_ready, j + 1)
                        dve.wait_ge(emptied, 2 * j + 2)
                        dve.tensor_copy(anchor[:, :], offset[:, :]).then_inc(tile_free, 1)
                        with dve.Fori(0, EC) as c:
                            n = j * EC + c
                            dve.tensor_tensor(column[:, :], crowd["key"][side][:, bass.ds(c, 1)], offset[:, :],
                                              ALU.subtract).then_inc(column_ready, 1)
                            dve.wait_ge(column_ready, n + 1)
                            dve.tensor_scalar(hot[:, :], iota[:, 0:P], column[:, 0:1], None, ALU.is_equal).then_inc(hot_made, 1)
                            dve.wait_ge(product_done, n + 1)
                            dve.tensor_tensor(degree[:, 0:1], deg_ps[:, 0:1], degree[:, 0:1], ALU.add).then_inc(counted, 1)
                            dve.tensor_tensor(total[:, :], sum_ps[:, 0:D], total[:, :], ALU.add).then_inc(added, 1)
                            dve.wait_ge(added, n + 1)
                            dve.wait_ge(counted, n + 1)
                        if mean:
                            dve.tensor_scalar(degree[:, 1:2], degree[:, 0:1], 1.0, None, ALU.max).then_inc(ratio_ready, 1)
                            dve.wait_ge(ratio_ready, 3 * j + 1)
                            dve.reciprocal(degree[:, 0:1], degree[:, 1:2]).then_inc(ratio_ready, 1)
                            dve.wait_ge(ratio_ready, 3 * j + 2)
                            dve.tensor_scalar(total[:, :], total[:, :], degree[:, 0:1], None, ALU.mult).then_inc(ratio_ready, 1)
                            dve.wait_ge(ratio_ready, 3 * j + 3)
                            dve.wait_ge(placed, j + 1)
                            dve.tensor_copy(row_of[side][:, bass.ds(t, 1)], place[:, :]).then_inc(target_copied, 1)
                            dve.wait_ge(target_copied, j + 1)
                            dve.tensor_scalar(place[:, :], place[:, :], float(P), None, ALU.add).then_inc(placed, 1)
                        dve.tensor_copy(lane_of[side][:, bass.ds(t, 1)], crowd["lane"][:, 0:1]).then_inc(result_ready, 1)
                        dve.wait_ge(result_out, 16 * j + 16)


def pair_rows(table, k):
    return table[bass.ds(256 * k, 256), :].rearrange("(p j) d -> p (j d)", j=2)


def last_rows(table, k, lanes):
    return table[256 * k:256 * k + 2 * lanes, :].rearrange("(p j) d -> p (j d)", j=2)


def gated_block(nc, N, K, TAIL, iota, ident, ones16, eps, w_sb, bias3, lng_sb, lnb_sb, lane_of, row_of,
                x, msg_rows, x1_rows, h2_rows, banks):
    U = 6
    own = Phase(nc)
    with own:
        def sb(name, shape, dt=F32):
            return own.enter_context(nc.sbuf_tensor(name, shape, dt))

        def ring(name, n, shape, dt=F32):
            return [sb(f"{name}{m}", shape, dt) for m in range(n)]

        def sem(name):
            return own.sem("A_" + name)
        xb = ring("xb", 6, [P, 512])
        mb = ring("mb", 6, [P, 2, D])
        rows_now = ring("rows_now", 6, [P, 2], I32)
        hot = ring("hotA", 2, [P, 2, P])
        h = ring("h", 2, [P, 512])
        ht = ring("ht", 2, [P, 2, 2, P])
        z = ring("z", 2, [P, 512])
        r = ring("r", 2, [P, 2, 2, P])
        x1 = ring("x1b", 6, [P, 512])
        h2 = ring("h2b", 6, [P, 512])
        anchor = sb("anchor", [P, 1])
        tick = sb("tick", [P, 2])
        ticked = sem("ticked")
        st = {g: ring(f"st{g}", 2, [P, 2, 6]) for g in "xhy"}
        mv = {g: ring(f"mv{g}", 2, [P, 2, 2]) for g in "xhy"}
        sd = {g: ring(f"sd{g}", 2, [P, 2]) for g in "xhy"}
        rs = {g: ring(f"rs{g}", 2, [P, 2]) for g in "xhy"}
        nm = {g: ring(f"nm{g}", 2, [P, 2]) for g in "xhy"}
        ht_ps, h1_ps, zt_ps, o_ps = banks[0:2], banks[2:4], banks[4:6], banks[6:8]

        x_in = [sem(f"x_in{m}") for m in range(6)]
        msg_in = [sem(f"msg_in{m}") for m in range(6)]
        stored = [sem(f"stored{m}") for m in range(6)]
        cleared = sem("cleared")
        rows_copied = sem("rows_copied")
        hot_made = sem("hot_made")
        st_done = {g: sem(f"st_done_{g}") for g in "xhy"}
        mv_done = {g: sem(f"mv_done_{g}") for g in "xhy"}
        sd_done = {g: sem(f"sd_done_{g}") for g in "xhy"}
        rs_done = {g: sem(f"rs_done_{g}") for g in "xhy"}
        nm_done = {g: sem(f"nm_done_{g}") for g in "xhy"}
        h_ready = sem("h_ready")
        ht_done = sem("ht_done")
        ht_ready = sem("ht_ready")
        h1_done = sem("h1_done")
        z_ready = sem("z_ready")
        zt_done = sem("zt_done")
        r_ready = sem("r_ready")
        o_done = sem("o_done")
        x1_ready = sem("x1_ready")
        h2_ready = sem("h2_ready")

        with nc.Block() as block:
            @block.sync
            def _(sp):
                def load(i, c):
                    k = U * i + c
                    wait(sp, x1_ready, k - 5)
                    full = not (isinstance(k, int) and k == K - 1)
                    lanes = P if full else TAIL
                    sp.dma_start(xb[c % 6][0:lanes, :], pair_rows(x, k) if full else last_rows(x, k, lanes)).then_inc(x_in[c % 6], 16)

                def store(i, c):
                    k = U * i + c
                    sp.wait_ge(h2_ready, k + 1)
                    full = not (isinstance(k, int) and k == K - 1)
                    lanes = P if full else TAIL
                    for table, b in ((x1_rows, x1), (h2_rows, h2)):
                        sp.dma_start(pair_rows(table, k) if full else last_rows(table, k, lanes),
                                     b[c % 6][0:lanes, :]).then_inc(stored[c % 6], 16)

                sp.wait_ge(cleared, 12)
                run_steps(sp, K, U, [(0, load), (6, store)])
                for m in range(6):
                    sp.wait_ge(stored[m], 32 * ((K - m + 5) // 6))

            @block.gpsimd
            def _(pool):
                pool.memset(tick[:, :], 0.0).then_inc(ticked, 1)
                pool.wait_ge(ticked, 1)
                for m in range(6):
                    pool.memset(mb[m][:, :, :], 0.0).then_inc(cleared, 1)
                    pool.memset(xb[m][:, :], 0.0).then_inc(cleared, 1)

                def gather(i, c):
                    k = U * i + c
                    wait(pool, msg_in[c % 6], 32 * (i + c // 6))
                    pool.tensor_copy(rows_now[c % 6][:, :], row_of[:, bass.ds(2 * k, 2)]).then_inc(rows_copied, 1)
                    wait(pool, ht_done, k - 5)
                    pool.wait_ge(rows_copied, k + 1)
                    anchor_on_pool(pool, tick)
                    for j in range(2):
                        pool.indirect_dma_start(
                            out=mb[c % 6][:, j, :], out_offset=None, in_=msg_rows,
                            in_offset=bass.IndirectOffsetOnAxis(ap=rows_now[c % 6][:, j:j + 1], axis=0),
                            bounds_check=msg_rows.shape[0] - 1, oob_is_err=False).then_inc(msg_in[c % 6], 16)

                run_steps(pool, K, U, [(0, gather)])

            @block.tensor
            def _(pe):
                def turn_and_sum(i, c):
                    k = U * i + c
                    pe.wait_ge(h_ready, k + 1)
                    pe.wait_ge(hot_made, k + 1)
                    pe.wait_ge(msg_in[c % 6], 32 * (i + c // 6 + 1))
                    wait(pe, ht_ready, k - 1)
                    for f in range(2):
                        for j in range(2):
                            to = ht_ps[c % 2][:, (2 * f + j) * P:(2 * f + j + 1) * P]
                            pe.matmul(to, h[c % 2][:, j * D + f * P:j * D + (f + 1) * P], ident[:, :],
                                      is_transpose=True, start=True, stop=False)
                            last = pe.matmul(to, mb[c % 6][:, j, f * P:(f + 1) * P], hot[c % 2][:, j, :],
                                             start=False, stop=True)
                    last.then_inc(ht_done, 1)

                def layer(i, c, ready, read, operand, w, bias, to, done):
                    k = U * i + c
                    pe.wait_ge(ready, k + 1)
                    wait(pe, read, k - 1)
                    for j in range(2):
                        part = to[c % 2][:, j * D:(j + 1) * D]
                        pe.matmul(part, ones16[:, :], bias[:, :], start=True, stop=False)
                        for f in range(2):
                            last = pe.matmul(part, operand[c % 2][:, f, j, :], w[:, f, :], start=False, stop=(f == 1))
                    last.then_inc(done, 1)

                def first(i, c):
                    layer(i, c, ht_ready, z_ready, ht, w_sb["w1"], bias3["b1"], h1_ps, h1_done)

                def turn(i, c):
                    k = U * i + c
                    pe.wait_ge(z_ready, k + 1)
                    wait(pe, r_ready, k - 1)
                    for f in range(2):
                        for j in range(2):
                            last = pe.matmul(zt_ps[c % 2][:, (2 * f + j) * P:(2 * f + j + 1) * P],
                                             z[c % 2][:, j * D + f * P:j * D + (f + 1) * P], ident[:, :],
                                             is_transpose=True, start=True, stop=True)
                    last.then_inc(zt_done, 1)

                def second(i, c):
                    layer(i, c, r_ready, x1_ready, r, w_sb["w2"], bias3["b2"], o_ps, o_done)

                run_steps(pe, K, U, [(1, turn_and_sum), (3, second), (2, turn), (1, first)])

            @block.scalar
            def _(act):
                def root(g):
                    def body(i, c):
                        k = U * i + c
                        wait(act, rs_done[g], k - 1)
                        act.wait_ge(mv_done[g], k + 1)
                        act.activation(sd[g][c % 2][:, :], mv[g][c % 2][:, :, 1], ACT.Sqrt, bias=eps[:, 0:1]).then_inc(sd_done[g], 1)
                    return body

                def normalise(i, c, g, func, to, slot, of, done):
                    k = U * i + c
                    act.wait_ge(nm_done[g], k + 1)
                    for j in range(2):
                        last = act.activation(to[slot][:, j * D:(j + 1) * D], of[:, j * D:(j + 1) * D], func,
                                              bias=nm[g][c % 2][:, j:j + 1], scale=rs[g][c % 2][:, j:j + 1])
                    last.then_inc(done, 1)

                def h_out(i, c):
                    wait(act, ht_done, U * i + c - 1)
                    normalise(i, c, "x", ACT.Relu, h, c % 2, xb[c % 6], h_ready)

                def ht_out(i, c):
                    k = U * i + c
                    wait(act, h1_done, k - 1)
                    act.wait_ge(ht_done, k + 1)
                    act.activation(ht[c % 2][:, :, :, :].rearrange("p f j n -> p (f j n)"), ht_ps[c % 2][:, :],
                                   ACT.Copy).then_inc(ht_ready, 1)

                def z_out(i, c):
                    wait(act, zt_done, U * i + c - 1)
                    normalise(i, c, "h", ACT.Identity, z, c % 2, h1_ps[c % 2], z_ready)

                def r_out(i, c):
                    k = U * i + c
                    wait(act, o_done, k - 1)
                    act.wait_ge(zt_done, k + 1)
                    for f in range(2):
                        last = act.activation(r[c % 2][:, f, :, :].rearrange("p j n -> p (j n)"),
                                              zt_ps[c % 2][:, f * D:(f + 1) * D], ACT.Relu,
                                              bias=lnb_sb[:, f:f + 1], scale=lng_sb[:, f:f + 1])
                    last.then_inc(r_ready, 1)

                def h2_out(i, c):
                    wait(act, stored[c % 6], 32 * (i + c // 6))
                    normalise(i, c, "y", ACT.Relu, h2, c % 6, x1[c % 6], h2_ready)

                run_steps(act, K, U, [(2, root("h")), (1, ht_out), (2, z_out), (0, root("x")), (2, r_out),
                                      (0, h_out), (4, h2_out), (3, root("y"))])

            @block.vector
            def _(dve):
                def take_stats(g, i, c, of):
                    k = U * i + c
                    wait(dve, mv_done[g], k - 1)
                    for j in range(2):
                        last = dve.bn_stats(st[g][c % 2][:, j, :], of[:, j * D:(j + 1) * D])
                    last.then_inc(st_done[g], 1)

                def stats_x(i, c):
                    dve.wait_ge(x_in[c % 6], 16 * (i + c // 6 + 1))
                    take_stats("x", i, c, xb[c % 6])

                def stats_h(i, c):
                    dve.wait_ge(h1_done, U * i + c + 1)
                    take_stats("h", i, c, h1_ps[c % 2])

                def stats_y(i, c):
                    dve.wait_ge(x1_ready, U * i + c + 1)
                    take_stats("y", i, c, x1[c % 6])

                reader = dict(x=h_ready, h=z_ready, y=h2_ready)

                def aggregate(g):
                    def body(i, c):
                        k = U * i + c
                        wait(dve, nm_done[g], k - 1)
                        wait(dve, sd_done[g], k - 1)
                        dve.wait_ge(st_done[g], k + 1)
                        dve.tensor_copy(anchor[:, :], eps[:, :])
                        for j in range(2):
                            last = dve.bn_aggr(mv[g][c % 2][:, j, :], st[g][c % 2][:, j, :])
                        last.then_inc(mv_done[g], 1)
                    return body

                def factors(g):
                    def body(i, c):
                        k = U * i + c
                        wait(dve, reader[g], k - 1)
                        dve.wait_ge(sd_done[g], k + 1)
                        dve.reciprocal(rs[g][c % 2][:, :], sd[g][c % 2][:, :]).then_inc(rs_done[g], 1)
                        dve.wait_ge(rs_done[g], k + 1)
                        dve.scalar_tensor_tensor(out=nm[g][c % 2][:, :], in0=mv[g][c % 2][:, :, 0], scalar=-1.0,
                                                 in1=rs[g][c % 2][:, :], op0=ALU.mult, op1=ALU.mult).then_inc(nm_done[g], 1)
                    return body

                def one_hot(i, c):
                    k = U * i + c
                    wait(dve, ht_done, k - 1)
                    for j in range(2):
                        last = dve.tensor_scalar(hot[c % 2][:, j, :], iota[:, 0:P], lane_of[:, bass.ds(2 * k + j, 1)], None,
                                                 ALU.is_equal)
                    last.then_inc(hot_made, 1)

                def residual(i, c):
                    k = U * i + c
                    wait(dve, stored[c % 6], 32 * (i + c // 6))
                    dve.wait_ge(o_done, k + 1)
                    dve.tensor_tensor(x1[c % 6][:, :], o_ps[c % 2][:, :], xb[c % 6][:, :], ALU.add).then_inc(x1_ready, 1)

                run_steps(dve, K, U, [(2, stats_h), (0, one_hot), (4, factors("y")), (2, aggregate("h")), (0, stats_x),
                                      (2, factors("h")), (0, aggregate("x")), (3, residual), (0, factors("x")),
                                      (3, stats_y), (3, aggregate("y"))])


def mean_block(nc, name, N, K, TAIL, iota, ident, ones16, eps, w, bias, g_wide, b_wide, lane_of, row_of, rdeg,
               own_rows, table, residual_rows, result, banks):
    U = 6
    last_layer = residual_rows is not None
    own = Phase(nc)
    with own:
        def sb(n, shape, dt=F32):
            return own.enter_context(nc.sbuf_tensor(f"{name}_{n}", shape, dt))

        def ring(n, count, shape, dt=F32):
            return [sb(f"{n}{m}", shape, dt) for m in range(count)]

        def sem(n):
            return own.sem(f"{name}_{n}")
        hb = ring("hb", 6, [P, 512])
        nb = ring("nb", 6, [P, 2, D])
        rows_now = ring("rows_now", 6, [P, 2], I32)
        hot = ring("hot", 2, [P, 2, P])
        hm = ring("hm", 2, [P, 512])
        ht = ring("ht", 2, [P, 2, 2, P])
        anchor = sb("anchor", [P, 1])
        tick = sb("tick", [P, 2])
        ticked = sem("ticked")
        st = ring("st", 2, [P, 2, 6])
        mv = ring("mv", 2, [P, 2, 2])
        sd = ring("sd", 2, [P, 2])
        rs = ring("rs", 2, [P, 2])
        u = ring("u", 2, [P, 512])
        v = ring("v", 2, [P, 512])
        y = ring("y", 6, [P, 512])
        dg = ring("dg", 2, [P, 2])
        ones = sb("ones", [P, 2])
        if last_layer:
            xb = ring("xb", 6, [P, 512])
            res = ring("res", 6, [P, 512])
        agg_ps, ht_ps, z_ps, deg_ps = banks[0:2], banks[2:4], banks[4:6], banks[6:7]

        h_in = [sem(f"h_in{m}") for m in range(6)]
        nb_in = [sem(f"nb_in{m}") for m in range(6)]
        stored = [sem(f"stored{m}") for m in range(6)]
        cleared = sem("cleared")
        rows_copied = sem("rows_copied")
        hot_made = sem("hot_made")
        agg_done = sem("agg_done")
        deg_raised = sem("deg_raised")
        rdeg_ready = sem("rdeg_ready")
        hm_ready = sem("hm_ready")
        ht_done = sem("ht_done")
        ht_ready = sem("ht_ready")
        z_done = sem("z_done")
        st_done = sem("st_done")
        mv_done = sem("mv_done")
        sd_done = sem("sd_done")
        rs_done = sem("rs_done")
        u_ready = sem("u_ready")
        v_ready = sem("v_ready")
        y_ready = sem("y_ready")
        if last_layer:
            x_in = [sem(f"x_in{m}") for m in range(6)]
            res_ready = sem("res_ready")
        CLEARED = 13 + (6 if last_layer else 0)

        with nc.Block() as block:
            @block.sync
            def _(sp):
                def load(i, c):
                    k = U * i + c
                    wait(sp, hm_ready, k - 5)
                    if last_layer:
                        wait(sp, res_ready, k - 5)
                    full = not (isinstance(k, int) and k == K - 1)
                    lanes = P if full else TAIL
                    sp.dma_start(hb[c % 6][0:lanes, :], pair_rows(own_rows, k) if full else last_rows(own_rows, k, lanes)).then_inc(h_in[c % 6], 16)
                    if last_layer:
                        sp.dma_start(xb[c % 6][0:lanes, :],
                                     pair_rows(residual_rows, k) if full else last_rows(residual_rows, k, lanes)).then_inc(x_in[c % 6], 16)

                def store(i, c):
                    k = U * i + c
                    full = not (isinstance(k, int) and k == K - 1)
                    lanes = P if full else TAIL
                    sp.wait_ge(res_ready if last_layer else y_ready, k + 1)
                    b = res if last_layer else y
                    sp.dma_start(pair_rows(result, k) if full else last_rows(result, k, lanes),
                                 b[c % 6][0:lanes, :]).then_inc(stored[c % 6], 16)

                sp.wait_ge(cleared, CLEARED)
                run_steps(sp, K, U, [(0, load), (6 if not last_layer else 7, store)] if not last_layer else [(0, load), (6, store)])
                for m in range(6):
                    sp.wait_ge(stored[m], 16 * ((K - m + 5) // 6))

            @block.gpsimd
            def _(pool):
                pool.memset(tick[:, :], 0.0).then_inc(ticked, 1)
                pool.wait_ge(ticked, 1)
                for m in range(6):
                    pool.memset(nb[m][:, :, :], 0.0).then_inc(cleared, 1)
                    pool.memset(hb[m][:, :], 0.0).then_inc(cleared, 1)
                    if last_layer:
                        pool.memset(xb[m][:, :], 0.0).then_inc(cleared, 1)
                pool.memset(ones[:, :], 1.0).then_inc(cleared, 1)

                def gather(i, c):
                    k = U * i + c
                    wait(pool, nb_in[c % 6], 32 * (i + c // 6))
                    pool.tensor_copy(rows_now[c % 6][:, :], row_of[:, bass.ds(2 * k, 2)]).then_inc(rows_copied, 1)
                    wait(pool, agg_done, k - 5)
                    pool.wait_ge(rows_copied, k + 1)
                    anchor_on_pool(pool, tick)
                    for j in range(2):
                        pool.indirect_dma_start(
                            out=nb[c % 6][:, j, :], out_offset=None, in_=table,
                            in_offset=bass.IndirectOffsetOnAxis(ap=rows_now[c % 6][:, j:j + 1], axis=0),
                            bounds_check=table.shape[0] - 1, oob_is_err=False).then_inc(nb_in[c % 6], 16)

                def add_residual(i, c):
                    k = U * i + c
                    pool.wait_ge(y_ready, k + 1)
                    pool.wait_ge(x_in[c % 6], 16 * (i + c // 6 + 1))
                    wait(pool, stored[c % 6], 16 * (i + c // 6))
                    pool.tensor_tensor(res[c % 6][:, :], y[c % 6][:, :], xb[c % 6][:, :], ALU.add).then_inc(res_ready, 1)

                run_steps(pool, K, U, [(0, gather)] + ([(5, add_residual)] if last_layer else []))

            @block.tensor
            def _(pe):
                def aggregate(i, c):
                    k = U * i + c
                    pe.wait_ge(hot_made, k + 1)
                    pe.wait_ge(nb_in[c % 6], 32 * (i + c // 6 + 1))
                    wait(pe, hm_ready, k - 1)
                    if not last_layer:
                        wait(pe, deg_raised, k)
                        for j in range(2):
                            pe.matmul(deg_ps[0][:, 2 * j:2 * j + 1], hot[c % 2][:, j, :], ones[:, 0:1], start=True, stop=True)
                    for j in range(2):
                        last = pe.matmul(agg_ps[c % 2][:, j * D:(j + 1) * D], hot[c % 2][:, j, :], nb[c % 6][:, j, :],
                                         start=True, stop=True)
                    last.then_inc(agg_done, 1)

                def turn(i, c):
                    k = U * i + c
                    pe.wait_ge(hm_ready, k + 1)
                    wait(pe, ht_ready, k - 1)
                    for f in range(2):
                        for j in range(2):
                            last = pe.matmul(ht_ps[c % 2][:, (2 * f + j) * P:(2 * f + j + 1) * P],
                                             hm[c % 2][:, j * D + f * P:j * D + (f + 1) * P], ident[:, :],
                                             is_transpose=True, start=True, stop=True)
                    last.then_inc(ht_done, 1)

                def layer(i, c):
                    k = U * i + c
                    pe.wait_ge(ht_ready, k + 1)
                    wait(pe, u_ready, k - 1)
                    for j in range(2):
                        part = z_ps[c % 2][:, j * D:(j + 1) * D]
                        pe.matmul(part, ones16[:, :], bias[:, :], start=True, stop=False)
                        for f in range(2):
                            last = pe.matmul(part, ht[c % 2][:, f, j, :], w[:, f, :], start=False, stop=(f == 1))
                    last.then_inc(z_done, 1)

                run_steps(pe, K, U, [(1, aggregate), (2, layer), (1, turn)])

            @block.scalar
            def _(act):
                def root(i, c):
                    k = U * i + c
                    wait(act, rs_done, k - 1)
                    act.wait_ge(mv_done, k + 1)
                    act.activation(sd[c % 2][:, :], mv[c % 2][:, :, 1], ACT.Sqrt, bias=eps[:, 0:1]).then_inc(sd_done, 1)

                def ht_out(i, c):
                    k = U * i + c
                    wait(act, z_done, k - 1)
                    act.wait_ge(ht_done, k + 1)
                    act.activation(ht[c % 2][:, :, :, :].rearrange("p f j n -> p (f j n)"), ht_ps[c % 2][:, :],
                                   ACT.Copy).then_inc(ht_ready, 1)

                def silu(i, c):
                    k = U * i + c
                    if last_layer:
                        wait(act, res_ready, k - 5)
                    else:
                        wait(act, stored[c % 6], 16 * (i + c // 6))
                    act.wait_ge(v_ready, k + 1)
                    act.activation(y[c % 6][:, :], v[c % 2][:, :], ACT.Silu).then_inc(y_ready, 1)

                run_steps(act, K, U, [(3, root), (1, ht_out), (4, silu)])

            @block.vector
            def _(dve):
                def one_hot(i, c):
                    k = U * i + c
                    wait(dve, agg_done, k - 1)
                    for j in range(2):
                        last = dve.tensor_scalar(hot[c % 2][:, j, :], iota[:, 0:P], lane_of[:, bass.ds(2 * k + j, 1)], None,
                                                 ALU.is_equal)
                    last.then_inc(hot_made, 1)

                def stats(i, c):
                    k = U * i + c
                    wait(dve, mv_done, k - 1)
                    dve.wait_ge(z_done, k + 1)
                    for j in range(2):
                        last = dve.bn_stats(st[c % 2][:, j, :], z_ps[c % 2][:, j * D:(j + 1) * D])
                    last.then_inc(st_done, 1)

                def degree(i, c):
                    k = U * i + c
                    dve.wait_ge(agg_done, k + 1)
                    wait(dve, rdeg_ready, k - 1)
                    dve.tensor_scalar(dg[c % 2][:, :], deg_ps[0][:, 0:4:2], 1.0, None, ALU.max).then_inc(deg_raised, 1)
                    dve.wait_ge(deg_raised, k + 1)
                    dve.reciprocal(rdeg[:, bass.ds(2 * k, 2)], dg[c % 2][:, :]).then_inc(rdeg_ready, 1)

                def mean(i, c):
                    k = U * i + c
                    dve.wait_ge(agg_done, k + 1)
                    dve.wait_ge(h_in[c % 6], 16 * (i + c // 6 + 1))
                    wait(dve, ht_done, k - 1)
                    if not last_layer:
                        dve.wait_ge(rdeg_ready, k + 1)
                    for j in range(2):
                        half = slice(j * D, (j + 1) * D)
                        last = dve.scalar_tensor_tensor(out=hm[c % 2][:, half], in0=agg_ps[c % 2][:, half],
                                                        scalar=rdeg[:, bass.ds(2 * k + j, 1)], in1=hb[c % 6][:, half],
                                                        op0=ALU.mult, op1=ALU.add)
                    last.then_inc(hm_ready, 1)

                def aggregate(i, c):
                    k = U * i + c
                    wait(dve, u_ready, k - 1)
                    wait(dve, sd_done, k - 1)
                    dve.wait_ge(st_done, k + 1)
                    dve.tensor_copy(anchor[:, :], eps[:, :])
                    for j in range(2):
                        last = dve.bn_aggr(mv[c % 2][:, j, :], st[c % 2][:, j, :])
                    last.then_inc(mv_done, 1)

                def centre(i, c):
                    k = U * i + c
                    wait(dve, v_ready, k - 1)
                    dve.wait_ge(mv_done, k + 1)
                    for j in range(2):
                        half = slice(j * D, (j + 1) * D)
                        last = dve.scalar_tensor_tensor(out=u[c % 2][:, half], in0=z_ps[c % 2][:, half],
                                                        scalar=mv[c % 2][:, j, 0:1], in1=g_wide[:, :],
                                                        op0=ALU.subtract, op1=ALU.mult)
                    last.then_inc(u_ready, 1)

                def invert(i, c):
                    k = U * i + c
                    wait(dve, v_ready, k - 1)
                    dve.wait_ge(sd_done, k + 1)
                    dve.reciprocal(rs[c % 2][:, :], sd[c % 2][:, :]).then_inc(rs_done, 1)

                def scale(i, c):
                    k = U * i + c
                    wait(dve, y_ready, k - 1)
                    dve.wait_ge(u_ready, k + 1)
                    dve.wait_ge(rs_done, k + 1)
                    for j in range(2):
                        half = slice(j * D, (j + 1) * D)
                        last = dve.scalar_tensor_tensor(out=v[c % 2][:, half], in0=u[c % 2][:, half],
                                                        scalar=rs[c % 2][:, j:j + 1], in1=b_wide[:, :],
                                                        op0=ALU.mult, op1=ALU.add)
                    last.then_inc(v_ready, 1)

                stages = [(0, one_hot), (3, stats)] + ([] if last_layer else [(1, degree)])
                run_steps(dve, K, U, stages + [(1, mean), (3, aggregate), (3, centre), (3, invert), (3, scale)])


_INS = ['x', 'src', 'dst', 'edge_attr_17', 'L0_gnn_ew1', 'L0_gnn_eb1', 'L0_gnn_ew2', 'L0_gnn_eb2', 'L0_gnn_lew',
        'L0_gnn_leb', 'L0_gnn_w1', 'L0_gnn_b1', 'L0_gnn_ln_g', 'L0_gnn_ln_b', 'L0_gnn_w2', 'L0_gnn_b2',
        'L1_gnn_W0', 'L1_gnn_b0', 'L1_gnn_g0', 'L1_gnn_beta0', 'L1_gnn_W1', 'L1_gnn_b1', 'L1_gnn_g1', 'L1_gnn_beta1']


def kernel(**inputs):
    import numpy as _np
    import concourse.bacc as _bacc
    from concourse import mybir as _mybir
    from concourse.bass_utils import run_bass_kernel_spmd as _run

    nc = _bacc.Bacc("TRN2", target_bir_lowering=False, num_devices=1)
    arrays, args = {}, []
    for name in _INS:
        a = _np.asarray(inputs[name])
        if name in ('L1_gnn_W0', 'L1_gnn_W1'):
            a = a.T
        a = _np.ascontiguousarray(a)
        arrays[f"in_{name}_dram"] = a
        args.append(nc.dram_tensor(f"in_{name}_dram", a.shape, _mybir.dt.from_np(a.dtype), kind="ExternalInput").ap())
    shape = _np.asarray(inputs['x']).shape
    args.append(nc.dram_tensor("out_0_dram", shape, _mybir.dt.from_np(_np.dtype('float32')), kind="ExternalOutput").ap())
    program(nc, *args)
    r = _run(nc, [arrays], core_ids=[0])
    return r.results[0]["out_0_dram"]
```

```python
import concourse.bass as bass
from concourse import mybir
from contextlib import ExitStack

P = 128
D = 256
RAW = 16
EPS = 1e-5
NO_LANE = 512
SC = 10
NO_ROW = 1 << 20
NO_NODE = 1 << 23

F32 = mybir.dt.float32
BF16 = mybir.dt.bfloat16
I32 = mybir.dt.int32
ALU = mybir.AluOpType
ACT = mybir.ActivationFunctionType


def run_steps(eng, count, unroll, stages):
    stages = [(*stage, count)[:3] for stage in stages]
    deepest = max(lag for lag, _, _ in stages)
    first = deepest + unroll
    rounds = max(0, (count - 1 - first) // unroll)
    if rounds < 2:
        rounds = 0

    def outside(steps):
        for s in steps:
            for lag, body, items in stages:
                if 0 <= s - lag < items:
                    body(0, s - lag)

    outside(range(first))
    if rounds:
        with eng.Fori(0, rounds) as i:
            for u in range(unroll):
                for lag, body, _ in stages:
                    body(i, first + u - lag)
    outside(range(first + rounds * unroll, max(lag + items for lag, _, items in stages)))


class Phase(ExitStack):

    def __init__(self, nc):
        super().__init__()
        self.nc, self.semaphores = nc, []
        self.callback(self.give_back)

    def sem(self, name):
        self.semaphores.append(self.nc.alloc_semaphore(name))
        return self.semaphores[-1]

    def give_back(self):
        self.nc.clear_and_free_semaphores(self.semaphores)
        self.nc.all_engine_barrier()


def anchor_on_pool(pool, tile):
    pool.tensor_tensor(tile[:, 0:1], tile[:, 1:2], tile[:, 1:2], ALU.mult)


def wait(eng, semaphore, value):
    if isinstance(value, int) and value <= 0:
        return
    eng.wait_ge(semaphore, value)


def program(nc, x, src, dst, attr, ew1, eb1, ew2, eb2, lew, leb, w1, b1, ln_g, ln_b, w2, b2,
            wt0, bb0, g0, beta0, wt1, bb1, g1, beta1, out):
    N = x.shape[0]
    E = src.shape[0]
    EC = -(-E // P)
    LAST = E - (P - 1) * EC
    assert 0 < LAST <= EC and EC % 4 == 0
    PAIRS = -(-N // 256)
    TAIL = (N - (PAIRS - 1) * 256) // 2
    assert N % 2 == 0
    NT = 2 * PAIRS

    MR = P * EC
    rows = nc.dram_tensor("rows", (MR + 2 * N, D), F32, kind="Internal").ap()
    msg_rows, h2_rows, y_rows = rows[0:MR, :], rows[MR:MR + N, :], rows[MR + N:, :]
    x1_rows = nc.dram_tensor("x1_rows", (N, D), F32, kind="Internal").ap()
    slots = {side: nc.dram_tensor(f"slots_{side}", (P * NT, 2), I32, kind="Internal").ap()
             for side in ("dst", "src")}

    whole = ExitStack()
    with whole:
        def keep(name, shape, dt):
            return whole.enter_context(nc.sbuf_tensor(name, shape, dt))

        iota = keep("iota", [P, max(NT, P)], F32)
        ident = keep("ident", [P, P], F32)
        ones16 = keep("ones16", [P, P], BF16)
        eps = keep("eps", [P, 1], F32)
        w_sb = {n: keep(n + "_sb", [P, 2, D], F32) for n in ("w1", "w2", "wt0", "wt1")}
        bias3 = {n: keep(n + "_3", [P, D], BF16) for n in ("b1", "b2", "bb0", "bb1")}
        lng_sb = keep("lng_sb", [P, 2], F32)
        lnb_sb = keep("lnb_sb", [P, 2], F32)
        wide = {n: keep(n + "_wide", [P, (2 if n[0] == "g" else 1) * D], F32) for n in ("g0", "beta0", "g1", "beta1")}
        lane_of = {side: keep(f"lane_of_{side}", [P, NT], F32) for side in ("dst", "src")}
        row_of = {side: keep(f"row_of_{side}", [P, NT], I32) for side in ("dst", "src")}
        rdeg = keep("rdeg", [P, NT], F32)
        banks = [whole.enter_context(nc.psum_tensor(f"bank{n}", [P, 512], F32)) for n in range(8)]

        crowd = dict(
            key={side: keep(f"key_{side}", [P, EC], F32) for side in ("dst", "src")},
            entry={side: keep(f"entry_{side}", [P, EC, 2], I32) for side in ("dst", "src")},
            count={side: keep(f"crowded_{side}", [P, 1], I32) for side in ("dst", "src")},
            tiles={side: nc.dram_tensor(f"crowded_tiles_{side}", (2 * P, 1), I32, kind="Internal").ap()
                   for side in ("dst", "src")},
            lane=keep("lane", [P, 2], F32), most=max(1, min(E // (P + 1), NT)))
        assert E // (P + 1) <= 2 * P

        setup = dict(N=N, E=E, EC=EC, LAST=LAST, NT=NT)
        edges = ExitStack()
        with edges:
            def ek(name, shape, dt):
                return edges.enter_context(nc.sbuf_tensor(name, shape, dt))
            e = dict(
                ends={side: ek(f"ends_{side}", [P, EC], I32) for side in ("dst", "src")},
                tile={side: ek(f"tile_{side}", [P, EC], F32) for side in ("dst", "src")},
                entry=crowd["entry"], lane=crowd["lane"],
                place={side: ek(f"place_{side}", [P, EC], I32) for side in ("dst", "src")},
                before=ek("before", [P, P], BF16), rest=ek("rest", [P, P], BF16),
                attr=ek("attr_sb", [P, EC * 17], F32), gate=ek("gate", [P, EC], F32),
                xrow=ek("xrow_of_src", [P, EC], I32),
                ew1=ek("ew1_sb", [RAW, P], F32), ew2=ek("ew2_sb", [P, P], F32),
                lew=ek("lew_sb", [P, D], F32), eb1=ek("eb1_sb", [P, 1], F32),
                eb2=ek("eb2_sb", [P, 1], F32), leb=ek("leb_wide", [P, D], F32))
            load_and_prepare(nc, setup, e, iota, ident, ones16, eps, w_sb, bias3, lng_sb, lnb_sb, wide,
                             slots, dict(w1=w1, w2=w2, wt0=wt0, wt1=wt1, b1=b1, b2=b2, bb0=bb0, bb1=bb1,
                                         ln_g=ln_g, ln_b=ln_b, g0=g0, beta0=beta0, g1=g1, beta1=beta1,
                                         src=src, dst=dst, attr=attr, ew1=ew1, ew2=ew2, lew=lew,
                                         eb1=eb1, eb2=eb2, leb=leb))
            place_edges(nc, setup, e, iota, banks, crowd)
            messages(nc, setup, e, ident, eps, slots, x, msg_rows, banks)
        read_slots(nc, NT, slots, lane_of, row_of)
        crowded_tiles(nc, "A", "dst", EC, crowd, iota, lane_of, row_of, msg_rows, 0, banks)
        gated_block(nc, N, PAIRS, TAIL, iota, ident, ones16, eps, w_sb, bias3, lng_sb, lnb_sb,
                    lane_of["dst"], row_of["dst"], x, msg_rows, x1_rows, h2_rows, banks)
        crowded_tiles(nc, "B", "src", EC, crowd, iota, lane_of, row_of, rows[0:MR + N, :], 0, banks)
        mean_block(nc, "B", N, PAIRS, TAIL, iota, ident, ones16, eps, w_sb["wt0"], bias3["bb0"],
                   wide["g0"], wide["beta0"], lane_of["src"], row_of["src"], rdeg, h2_rows, rows[0:MR + N, :], None, y_rows, banks)
        name_rows_of_y(nc, MR, N, row_of["src"])
        crowded_tiles(nc, "C", "src", EC, crowd, iota, lane_of, row_of, rows, N, banks)
        mean_block(nc, "C", N, PAIRS, TAIL, iota, ident, ones16, eps, w_sb["wt1"], bias3["bb1"],
                   wide["g1"], wide["beta1"], lane_of["src"], row_of["src"], rdeg, y_rows, rows, x1_rows, out, banks)


def load_and_prepare(nc, dims, e, iota, ident, ones16, eps, w_sb, bias3, lng_sb, lnb_sb, wide, slots, a):
    N, EC, LAST, NT = dims["N"], dims["EC"], dims["LAST"], dims["NT"]
    own = Phase(nc)
    with own:
        def sb(name, shape, dt):
            return own.enter_context(nc.sbuf_tensor(name, shape, dt))

        def sem(name):
            return own.sem(name)

        empty = sb("empty", [P, NT, 2], I32)
        names = ("b1", "b2", "bb0", "bb1")
        raw = {n: sb(n + "_raw", [P, D], F32) for n in names}
        part = {n: sb(n + "_part", [P, D], BF16) for n in names}
        left = {n: sb(n + "_left", [P, D], F32) for n in names}
        odd = {s: sb(f"odd_{s}", [P, EC], F32) for s in ("dst", "src")}
        bit = {s: sb(f"bit_{s}", [P, EC], I32) for s in ("dst", "src")}
        high = {s: sb(f"high_{s}", [P, EC], I32) for s in ("dst", "src")}

        weights_in = sem("weights_in")
        biases_in = sem("biases_in")
        ends_in = sem("ends_in")
        attr_in = sem("attr_in")
        padded = sem("padded")
        empty_made = sem("empty_made")
        empty_out = sem("empty_out")
        made = sem("made")
        split = sem("split")
        raw_cleared = sem("raw_cleared")
        summed = sem("rows_summed")
        averaged = sem("rows_averaged")
        taken_off = sem("means_taken_off")
        ended = sem("ended")
        numbered = sem("numbered")

        sets = [(w_sb[n][:, :, :], a[n].rearrange("(c p) n -> p c n", p=P)) for n in ("w1", "w2", "wt0", "wt1")]
        sets += [(e["ew1"][:, :], a["ew1"]), (e["ew2"][:, :], a["ew2"]), (e["lew"][:, :], a["lew"]),
                 (lng_sb[:, :], a["ln_g"].rearrange("(c p) -> p c", p=P)),
                 (lnb_sb[:, :], a["ln_b"].rearrange("(c p) -> p c", p=P)),
                 (e["eb1"][:, :], a["eb1"].rearrange("(p c) -> p c", c=1)),
                 (e["eb2"][:, :], a["eb2"].rearrange("(p c) -> p c", c=1)),
                 (e["leb"][:, :], a["leb"].partition_broadcast(P))]
        sets += [(wide[n][:, j * D:(j + 1) * D], a[n].partition_broadcast(P))
                 for n, j in (("g0", 0), ("g0", 1), ("beta0", 0), ("g1", 0), ("g1", 1), ("beta1", 0))]
        parts = [(0, 112), (112, P - 1)]
        centred = [(w_sb[n][:, f, :], f"{n}_{f}") for n in ("wt0", "wt1") for f in range(2)]
        centred_biases = [(raw[n][:, :], n) for n in ("bb0", "bb1")]
        sums = {n: sb("sums_" + n, [P, 6], F32) for _, n in centred + centred_biases}
        means = {n: sb("means_" + n, [P, 2], F32) for _, n in centred + centred_biases}

        with nc.Block() as block:
            @block.sync
            def _(sp):
                sp.wait_ge(padded, 3)
                for side in ("dst", "src"):
                    v = a[side]
                    for lo, hi in parts:
                        sp.dma_start(e["ends"][side][lo:hi, :],
                                     v[lo * EC:hi * EC].rearrange("(p c) -> p c", c=EC)).then_inc(ends_in, 16)
                    sp.dma_start(e["ends"][side][P - 1:P, 0:LAST],
                                 v[(P - 1) * EC:].rearrange("(p c) -> p c", p=1)).then_inc(ends_in, 16)
                for lo, hi in parts:
                    sp.dma_start(e["attr"][lo:hi, :],
                                 a["attr"][lo * EC:hi * EC, :].rearrange("(p c) f -> p (c f)", c=EC)).then_inc(attr_in, 16)
                sp.dma_start(e["attr"][P - 1:P, 0:LAST * 17],
                             a["attr"][(P - 1) * EC:, :].rearrange("(p c) f -> p (c f)", p=1)).then_inc(attr_in, 16)
                sp.wait_ge(empty_made, 2)
                for side in ("dst", "src"):
                    sp.dma_start(slots[side].rearrange("(p t) w -> p (t w)", t=NT),
                                 empty[:, :, :].rearrange("p t w -> p (t w)")).then_inc(empty_out, 16)
                sp.wait_ge(empty_out, 32)
                sp.wait_ge(attr_in, 48)

            @block.scalar
            def _(act):
                act.wait_ge(raw_cleared, len(names))
                for n in names:
                    for row in (0, 32, 64):
                        act.dma_start(raw[n][row:row + 1, :], a[n].rearrange("(p c) -> p c", p=1)).then_inc(biases_in, 16)
                with nc.allow_non_contiguous_dma(reason="per-feature scales, 256 numbers each"):
                    for to, of in sets:
                        act.dma_start(to, of).then_inc(weights_in, 16)
                act.wait_ge(weights_in, 16 * len(sets))

            @block.gpsimd
            def _(pool):
                for n in names:
                    pool.memset(raw[n][:, :], 0.0).then_inc(raw_cleared, 1)
                pool.memset(e["ends"]["dst"][:, :], NO_NODE).then_inc(padded, 1)
                pool.memset(e["ends"]["src"][:, :], NO_NODE).then_inc(padded, 1)
                pool.memset(e["attr"][:, :], 0.0).then_inc(padded, 1)
                pool.memset(empty[:, :, 0], NO_LANE).then_inc(empty_made, 1)
                pool.memset(empty[:, :, 1], NO_ROW).then_inc(empty_made, 1)
                pool.memset(ident[:, :], 1.0).then_inc(made, 1)
                pool.memset(e["before"][:, :], 1.0).then_inc(made, 1)
                pool.memset(e["rest"][:, :], 1.0).then_inc(made, 1)
                pool.memset(ones16[:, :], 1.0)
                pool.memset(eps[:, :], EPS)
                pool.iota(iota[:, :], [[1, max(NT, P)]], base=0, channel_multiplier=0, allow_small_or_imprecise_dtypes=True)
                pool.iota(e["entry"]["dst"][:, :, 1], [[1, EC]], base=0, channel_multiplier=EC)
                pool.iota(e["lane"][:, :], [[P, 2]], base=0, channel_multiplier=1, allow_small_or_imprecise_dtypes=True)
                pool.wait_ge(made, 3)
                pool.affine_select(out=ident[:, :], in_=ident[:, :], compare_op=ALU.is_equal, fill=0.0,
                                   base=0, pattern=[[-1, P]], channel_multiplier=1)
                pool.affine_select(out=e["before"][:, :], in_=e["before"][:, :], compare_op=ALU.is_gt, fill=0.0,
                                   base=0, pattern=[[1, P]], channel_multiplier=-1)
                pool.affine_select(out=e["rest"][:, :], in_=e["rest"][:, :], compare_op=ALU.is_ge, fill=0.0,
                                   base=0, pattern=[[-1, P]], channel_multiplier=1)

            @block.vector
            def _(dve):
                for n in names:
                    dve.memset(bias3[n][:, :], 0.0).then_inc(split, 1)
                dve.wait_ge(ends_in, 96)
                for side in ("dst", "src"):
                    ends = e["ends"][side]
                    dve.tensor_scalar(high[side][:, :], ends[:, :], 8, None, ALU.logical_shift_right).then_inc(numbered, 1)
                    dve.tensor_scalar(bit[side][:, :], ends[:, :], 1, None, ALU.bitwise_and).then_inc(numbered, 1)
                    dve.tensor_scalar(e["entry"][side][:, :, 0], ends[:, :], 1, P - 1, ALU.logical_shift_right,
                                      ALU.bitwise_and).then_inc(ended, 1)
                dve.tensor_scalar(e["xrow"][:, :], e["ends"]["src"][:, :], NO_ROW, None, ALU.min)
                dve.tensor_scalar(e["entry"]["src"][:, :, 1], e["ends"]["dst"][:, :], float(P * EC), None, ALU.add)
                dve.wait_ge(numbered, 4)
                for side in ("dst", "src"):
                    dve.scalar_tensor_tensor(out=e["tile"][side][:, :], in0=high[side][:, :], scalar=2.0,
                                             in1=bit[side][:, :], op0=ALU.mult, op1=ALU.add)
                dve.wait_ge(biases_in, 16 * 3 * len(names))
                dve.wait_ge(weights_in, 16 * len(sets))
                for of, n in centred + centred_biases:
                    dve.bn_stats(sums[n][:, :], of).then_inc(summed, 1)
                dve.wait_ge(summed, len(centred + centred_biases))
                for _, n in centred + centred_biases:
                    dve.bn_aggr(means[n][:, :], sums[n][:, :]).then_inc(averaged, 1)
                dve.wait_ge(averaged, len(centred + centred_biases))
                for of, n in centred + centred_biases:
                    dve.tensor_scalar(of, of, means[n][:, 0:1], None, ALU.subtract).then_inc(taken_off, 1)
                dve.wait_ge(taken_off, len(centred + centred_biases))
                step = [4]

                def link(ins):
                    step[0] += 1
                    ins.then_inc(split, 1)
                for n in names:
                    for lane in (0, 32, 64):
                        row = slice(lane, lane + 1)
                        if lane == 0:
                            dve.wait_ge(split, step[0])
                            dve.tensor_copy(bias3[n][row, :], raw[n][row, :])
                            continue
                        link(dve.tensor_copy(part[n][row, :], raw[n][row, :]))
                        dve.wait_ge(split, step[0])
                        link(dve.tensor_tensor(left[n][row, :], raw[n][row, :], part[n][row, :], ALU.subtract))
                        dve.wait_ge(split, step[0])
                        if lane == 32:
                            dve.tensor_copy(bias3[n][row, :], left[n][row, :])
                            continue
                        link(dve.tensor_copy(part[n][row, :], left[n][row, :]))
                        dve.wait_ge(split, step[0])
                        link(dve.tensor_tensor(raw[n][row, :], left[n][row, :], part[n][row, :], ALU.subtract))
                        dve.wait_ge(split, step[0])
                        dve.tensor_copy(bias3[n][row, :], raw[n][row, :])
                dve.wait_ge(attr_in, 48)
                pol = e["attr"][:, :].rearrange("p (c f) -> p c f", f=17)[:, :, 0]
                link(dve.tensor_scalar(e["gate"][:, :], pol, 0.0, 1.0, ALU.max, ALU.min))
                dve.wait_ge(split, step[0])
                dve.tensor_scalar(e["gate"][:, :], e["gate"][:, :], 0.01, None, ALU.add)


def place_edges(nc, dims, e, iota, banks, crowd):
    EC, NT = dims["EC"], dims["NT"]
    U = 2
    own = Phase(nc)
    with own:
        def sb(name, shape, dt):
            return own.enter_context(nc.sbuf_tensor(name, shape, dt))

        def sem(name):
            return own.sem(name)
        sides = ("dst", "src")
        hot = {s: [sb(f"hot_{s}{n}", [P, NT], BF16) for n in range(U)] for s in sides}
        rank = {s: sb(f"rank_{s}", [P, EC], F32) for s in sides}
        picked = {s: [sb(f"picked_{s}{n}", [P, NT], BF16) for n in range(2)] for s in sides}
        counted = dict(zip(sides, banks))
        zero = sb("zero", [P, NT], BF16)
        over = {s: sb(f"over_{s}", [P, NT], F32) for s in sides}
        running = {s: sb(f"running_{s}", [P, NT], F32) for s in sides}
        below = {s: [sb(f"below_{s}{g}", [P, NT], F32) for g in range(2)] for s in sides}
        nth = {s: sb(f"nth_{s}", [P, 2], F32) for s in sides}
        nth_i = {s: sb(f"nth_i_{s}", [P, 2], I32) for s in sides}
        listed = sem("listed")
        list_out = sem("list_out")
        zeroed = sem("zeroed")
        hot_made = {s: sem(f"hot_made_{s}") for s in sides}
        added = {s: sem(f"added_{s}") for s in sides}
        ranked = {s: sem(f"ranked_{s}") for s in sides}
        totalled = {s: sem(f"totalled_{s}") for s in sides}

        with nc.Block() as block:
            @block.vector
            def _(dve):
                dve.memset(zero[:, :], 0.0).then_inc(zeroed, 1)

                def one_hot(i, c):
                    n = U * i + c
                    for s in sides:
                        wait(dve, totalled[s], n - U + 1)
                        dve.tensor_scalar(hot[s][c % U][:, :], iota[:, 0:NT], e["tile"][s][:, bass.ds(n, 1)], None,
                                          ALU.is_equal).then_inc(hot_made[s], 1)

                def read_rank(i, c):
                    n = U * i + c
                    for s in sides:
                        dve.wait_ge(added[s], n + 1)
                        wait(dve, ranked[s], n - 1)
                        dve.scalar_tensor_tensor(out=picked[s][c % 2][:, :], in0=iota[:, 0:NT],
                                                 scalar=e["tile"][s][:, bass.ds(n, 1)], in1=counted[s][:, 0:NT],
                                                 op0=ALU.is_equal, op1=ALU.mult,
                                                 accum_out=rank[s][:, bass.ds(n, 1)]).then_inc(ranked[s], 1)

                run_steps(dve, EC, U, [(0, one_hot), (1, read_rank)])
                for s in sides:
                    dve.wait_ge(ranked[s], EC)
                    dve.scalar_tensor_tensor(out=e["place"][s][:, :], in0=rank[s][:, :], scalar=float(NT),
                                             in1=e["tile"][s][:, :], op0=ALU.mult, op1=ALU.add)
                    dve.scalar_tensor_tensor(out=crowd["key"][s][:, :], in0=e["tile"][s][:, :], scalar=float(P),
                                             in1=e["entry"][s][:, :, 0], op0=ALU.mult, op1=ALU.add)
                    dve.wait_ge(totalled[s], EC)
                    dve.tensor_scalar(over[s][:, :], counted[s][:, 0:NT], float(P), None, ALU.is_gt).then_inc(listed, 1)
                    at = 5 * sides.index(s)
                    dve.wait_ge(listed, at + 1)
                    dve.tensor_tensor_scan(running[s][:, :], over[s][:, :], over[s][:, :], 0.0, ALU.add,
                                           ALU.bypass).then_inc(listed, 1)
                    dve.wait_ge(listed, at + 2)
                    dve.tensor_copy(crowd["count"][s][:, :], running[s][:, NT - 1:NT])
                    for g in range(2):
                        dve.tensor_scalar(below[s][g][:, :], running[s][:, :], crowd["lane"][:, g:g + 1], 0.0, ALU.is_le,
                                          ALU.add, accum_out=nth[s][:, g:g + 1]).then_inc(listed, 1)
                    dve.wait_ge(listed, at + 4)
                    dve.tensor_copy(nth_i[s][:, :], nth[s][:, :]).then_inc(listed, 1)

            @block.sync
            def _(sp):
                for n, s in enumerate(sides):
                    sp.wait_ge(listed, 5 * n + 5)
                    sp.dma_start(crowd["tiles"][s].rearrange("(g p) w -> p (g w)", p=P), nth_i[s][:, :],
                                 allow_slow_non_contiguous=True).then_inc(list_out, 16)
                sp.wait_ge(list_out, 32)

            @block.tensor
            def _(pe):
                pe.wait_ge(zeroed, 1)
                for s in sides:
                    pe.matmul(counted[s][:, 0:NT], e["before"][:, :], zero[:, :], start=True, stop=True)

                def add_earlier_lanes(i, c):
                    n = U * i + c
                    for s in sides:
                        pe.wait_ge(hot_made[s], n + 1)
                        pe.matmul(counted[s][:, 0:NT], e["before"][:, :], hot[s][c % U][:, :], start=False,
                                  stop=True, skip_group_check=True).then_inc(added[s], 1)

                def add_the_rest(i, c):
                    n = U * i + c
                    for s in sides:
                        pe.wait_ge(ranked[s], n + 1)
                        pe.matmul(counted[s][:, 0:NT], e["rest"][:, :], hot[s][c % U][:, :], start=False,
                                  stop=True, skip_group_check=True).then_inc(totalled[s], 1)

                run_steps(pe, EC, U, [(0, add_earlier_lanes), (0, add_the_rest)])


def messages(nc, dims, e, ident, eps, slots, x, msg_rows, banks):
    N, EC, NT = dims["N"], dims["EC"], dims["NT"]
    G = 4
    U = 4
    K = EC // G
    own = Phase(nc)
    with own:
        def sb(name, shape, dt):
            return own.enter_context(nc.sbuf_tensor(name, shape, dt))

        def sem(name):
            return own.sem(name)
        PADDED = G * 17 + P
        place_now = {s: [sb(f"place_now_{s}{n}", [P, G], I32) for n in range(2)] for s in slots}
        entry_now = {s: [sb(f"entry_now_{s}{n}", [P, G * 2], I32) for n in range(2)] for s in slots}
        attr_now = [sb(f"attr_now{n}", [P, PADDED], F32) for n in range(2)]
        row_now = [sb(f"row_now{n}", [P, G], I32) for n in range(4)]
        xg = [sb(f"xg{n}", [P, G, D], F32) for n in range(4)]
        raw_t = [sb(f"raw_t{n}", [RAW, G * P], F32) for n in range(2)]
        e1_t = [sb(f"e1_t{n}", [P, G * P], F32) for n in range(2)]
        e2_t = [sb(f"e2_t{n}", [P, G * P], F32) for n in range(2)]
        anchor = sb("e_anchor", [P, 1], F32)
        tick = sb("e_tick", [P, 2], F32)
        ticked = sem("ticked")
        stats = [sb(f"e_stats{n}", [P, G, 6], F32) for n in range(2)]
        mv = [sb(f"e_mv{n}", [P, G, 2], F32) for n in range(2)]
        std = [sb(f"e_std{n}", [P, G], F32) for n in range(2)]
        rstd = [sb(f"e_rstd{n}", [P, G], F32) for n in range(2)]
        nmr = [sb(f"e_nmr{n}", [P, G], F32) for n in range(2)]
        hs = [sb(f"hs{n}", [P, G, D], F32) for n in range(2)]
        emb = [sb(f"emb{n}", [P, G, D], F32) for n in range(2)]
        msg = [sb(f"msg{n}", [P, G, D], F32) for n in range(2)]
        raw_ps, e1_ps, e2_ps = banks[0:3]
        emb_ps = [banks[3:5], banks[5:7]]

        placed_now = {s: sem(f"placed_now_{s}") for s in slots}
        scattered = {s: [sem(f"scattered_{s}{n}") for n in range(2)] for s in slots}
        cleared = sem("cleared")
        attr_copied = sem("attr_copied")
        rows_copied = sem("rows_copied")
        gathered = [sem(f"x_gathered{n}") for n in range(4)]
        turned = sem("turned")
        raw_ready = sem("raw_ready")
        e1_done = sem("e1_done")
        e1_ready = sem("e1_ready")
        e2_done = sem("e2_done")
        e2_ready = sem("e2_ready")
        emb_done = sem("emb_done")
        stats_done = sem("e_stats_done")
        mv_done = sem("e_mv_done")
        std_done = sem("e_std_done")
        rstd_done = sem("e_rstd_done")
        nmr_done = sem("e_nmr_done")
        hs_ready = sem("hs_ready")
        emb_scaled = sem("emb_scaled")
        summed = sem("summed")
        msg_ready = sem("msg_ready")
        stored = [sem(f"msg_stored{n}") for n in range(2)]
        ROUNDS = 2 * K

        with nc.Block() as block:
            @block.gpsimd
            def _(pool):
                pool.memset(tick[:, :], 0.0).then_inc(ticked, 1)
                pool.wait_ge(ticked, 1)
                for b in attr_now:
                    pool.memset(b[:, :], 0.0).then_inc(cleared, 1)
                for b in xg:
                    pool.memset(b[:, :, :], 0.0).then_inc(cleared, 1)
                pool.wait_ge(cleared, 6)

                def scatter(side):
                    def body(i, c):
                        m = 2 * i + c
                        wait(pool, scattered[side][c % 2], 16 * G * (i + c // 2))
                        pool.tensor_copy(place_now[side][c % 2][:, :], e["place"][side][:, bass.ds(G * m, G)]).then_inc(placed_now[side], 1)
                        pool.tensor_copy(entry_now[side][c % 2][:, :],
                                         e["entry"][side][:, bass.ds(G * m, G), :].rearrange("p c w -> p (c w)")).then_inc(placed_now[side], 1)
                        pool.wait_ge(placed_now[side], 2 * m + 2)
                        anchor_on_pool(pool, tick)
                        for u in range(G):
                            pool.indirect_dma_start(
                                out=slots[side], out_offset=bass.IndirectOffsetOnAxis(ap=place_now[side][c % 2][:, u:u + 1], axis=0),
                                in_=entry_now[side][c % 2][:, 2 * u:2 * u + 2], in_offset=None,
                                bounds_check=P * NT - 1, oob_is_err=False).then_inc(scattered[side][c % 2], 16)
                    return body

                run_steps(pool, K, 2, [(0, scatter("dst"))])
                run_steps(pool, K, 2, [(0, scatter("src"))])

                def gather(i, c):
                    k = U * i + c
                    wait(pool, turned, k - 1)
                    pool.tensor_copy(attr_now[c % 2][:, 0:G * 17], e["attr"][:, bass.ds(G * 17 * k, G * 17)]).then_inc(attr_copied, 1)
                    wait(pool, gathered[c % 4], 16 * G * (i + c // 4))
                    pool.tensor_copy(row_now[c % 4][:, :], e["xrow"][:, bass.ds(G * k, G)]).then_inc(rows_copied, 1)
                    pool.wait_ge(rows_copied, k + 1)
                    wait(pool, hs_ready, k - 3)
                    anchor_on_pool(pool, tick)
                    for u in range(G):
                        pool.indirect_dma_start(
                            out=xg[c % 4][:, u, :], out_offset=None, in_=x,
                            in_offset=bass.IndirectOffsetOnAxis(ap=row_now[c % 4][:, u:u + 1], axis=0),
                            bounds_check=N - 1, oob_is_err=False).then_inc(gathered[c % 4], 16)

                run_steps(pool, K, U, [(0, gather)])
                for side in slots:
                    for n in range(2):
                        pool.wait_ge(scattered[side][n], 16 * G * ((K + 1 - n) // 2))

            @block.tensor
            def _(pe):
                def turn(i, c):
                    k = U * i + c
                    pe.wait_ge(attr_copied, k + 1)
                    wait(pe, raw_ready, k)
                    for u in range(G):
                        last = pe.matmul(raw_ps[:, u * P:(u + 1) * P], attr_now[c % 2][:, 17 * u + 1:17 * u + 1 + P],
                                         ident[:, :], is_transpose=True, start=True, stop=True)
                    last.then_inc(turned, 1)

                def first(i, c):
                    k = U * i + c
                    pe.wait_ge(raw_ready, k + 1)
                    wait(pe, e1_ready, k)
                    pe.matmul(e1_ps[:, :], e["ew1"][:, :], raw_t[c % 2][:, :], start=True, stop=True).then_inc(e1_done, 1)

                def second(i, c):
                    k = U * i + c
                    pe.wait_ge(e1_ready, k + 1)
                    wait(pe, e2_ready, k)
                    pe.matmul(e2_ps[:, :], e["ew2"][:, :], e1_t[c % 2][:, :], start=True, stop=True).then_inc(e2_done, 1)

                def embed(i, c):
                    k = U * i + c
                    pe.wait_ge(e2_ready, k + 1)
                    wait(pe, emb_scaled, k - 1)
                    for u in range(G):
                        last = pe.matmul(emb_ps[c % 2][u // 2][:, u % 2 * D:(u % 2 + 1) * D], e2_t[c % 2][:, u * P:(u + 1) * P],
                                         e["lew"][:, :], start=True, stop=True)
                    last.then_inc(emb_done, 1)

                run_steps(pe, K, U, [(0, turn), (1, first), (2, second), (3, embed)])

            @block.scalar
            def _(act):
                def raw_out(i, c):
                    k = U * i + c
                    wait(act, e1_done, k - 1)
                    act.wait_ge(turned, k + 1)
                    act.activation(raw_t[c % 2][:, :], raw_ps[0:RAW, :], ACT.Copy).then_inc(raw_ready, 1)

                def e1_out(i, c):
                    k = U * i + c
                    wait(act, e2_done, k - 1)
                    act.wait_ge(e1_done, k + 1)
                    act.activation(e1_t[c % 2][:, :], e1_ps[:, :], ACT.Relu, bias=e["eb1"][:, 0:1]).then_inc(e1_ready, 1)

                def e2_out(i, c):
                    k = U * i + c
                    wait(act, emb_done, k - 1)
                    act.wait_ge(e2_done, k + 1)
                    act.activation(e2_t[c % 2][:, :], e2_ps[:, :], ACT.Identity, bias=e["eb2"][:, 0:1]).then_inc(e2_ready, 1)

                def root(i, c):
                    k = U * i + c
                    wait(act, rstd_done, k - 1)
                    act.wait_ge(mv_done, k + 1)
                    act.activation(std[c % 2][:, :], mv[c % 2][:, :, 1], ACT.Sqrt, bias=eps[:, 0:1]).then_inc(std_done, 1)

                def normalise(i, c):
                    k = U * i + c
                    wait(act, summed, k - 1)
                    act.wait_ge(nmr_done, k + 1)
                    for u in range(G):
                        last = act.activation(hs[c % 2][:, u, :], xg[c % 4][:, u, :], ACT.Relu,
                                              bias=nmr[c % 2][:, u:u + 1], scale=rstd[c % 2][:, u:u + 1])
                    last.then_inc(hs_ready, 1)

                def message(i, c):
                    k = U * i + c
                    wait(act, stored[c % 2], 16 * (2 * i + c // 2))
                    act.wait_ge(summed, k + 1)
                    act.activation(msg[c % 2][:, :, :], emb[c % 2][:, :, :], ACT.Relu).then_inc(msg_ready, 1)

                run_steps(act, K, U, [(0, raw_out), (1, e1_out), (2, e2_out), (2, root), (3, normalise), (4, message)])

            @block.vector
            def _(dve):
                def take_stats(i, c):
                    k = U * i + c
                    wait(dve, mv_done, k - 1)
                    dve.wait_ge(gathered[c % 4], 16 * G * (i + c // 4 + 1))
                    for u in range(G):
                        last = dve.bn_stats(stats[c % 2][:, u, :], xg[c % 4][:, u, :])
                    last.then_inc(stats_done, 1)

                def add(i, c):
                    k = U * i + c
                    dve.wait_ge(emb_scaled, k + 1)
                    dve.wait_ge(hs_ready, k + 1)
                    dve.tensor_tensor(emb[c % 2][:, :, :], emb[c % 2][:, :, :], hs[c % 2][:, :, :], ALU.add).then_inc(summed, 1)

                def aggregate(i, c):
                    k = U * i + c
                    wait(dve, nmr_done, k - 1)
                    wait(dve, hs_ready, k - 1)
                    dve.wait_ge(stats_done, k + 1)
                    dve.tensor_copy(anchor[:, :], eps[:, :])
                    for u in range(G):
                        last = dve.bn_aggr(mv[c % 2][:, u, :], stats[c % 2][:, u, :])
                    last.then_inc(mv_done, 1)

                def scale(i, c):
                    k = U * i + c
                    wait(dve, msg_ready, k - 1)
                    dve.wait_ge(emb_done, k + 1)
                    for u in range(G):
                        last = dve.scalar_tensor_tensor(out=emb[c % 2][:, u, :], in0=emb_ps[c % 2][u // 2][:, u % 2 * D:(u % 2 + 1) * D],
                                                        scalar=e["gate"][:, bass.ds(G * k + u, 1)], in1=e["leb"][:, :],
                                                        op0=ALU.mult, op1=ALU.add)
                    last.then_inc(emb_scaled, 1)

                def factors(i, c):
                    k = U * i + c
                    wait(dve, hs_ready, k - 1)
                    dve.wait_ge(std_done, k + 1)
                    dve.reciprocal(rstd[c % 2][:, :], std[c % 2][:, :]).then_inc(rstd_done, 1)
                    dve.wait_ge(rstd_done, k + 1)
                    dve.scalar_tensor_tensor(out=nmr[c % 2][:, :], in0=mv[c % 2][:, :, 0], scalar=-1.0,
                                             in1=rstd[c % 2][:, :], op0=ALU.mult, op1=ALU.mult).then_inc(nmr_done, 1)

                run_steps(dve, K, U, [(2, take_stats), (4, add), (2, aggregate), (3, scale), (2, factors)])

            @block.sync
            def _(sp):
                rows = msg_rows[0:P * EC, :].rearrange("(p c) d -> p (c d)", c=EC)

                def store(i, c):
                    k = U * i + c
                    sp.wait_ge(msg_ready, k + 1)
                    sp.dma_start(rows[:, bass.ds(G * D * k, G * D)],
                                 msg[c % 2][:, :, :].rearrange("p g d -> p (g d)")).then_inc(stored[c % 2], 16)

                run_steps(sp, K, U, [(0, store)])
                sp.wait_ge(stored[0], 16 * ((K + 1) // 2))
                sp.wait_ge(stored[1], 16 * (K // 2))


def read_slots(nc, NT, slots, lane_of, row_of):
    own = Phase(nc)
    with own:
        both = {s: own.enter_context(nc.sbuf_tensor(f"both_{s}", [P, NT, 2], I32)) for s in slots}
        came = {s: own.sem(f"slots_in_{s}") for s in slots}
        with nc.Block() as block:
            @block.sync
            def _(sp):
                for s in slots:
                    sp.dma_start(both[s][:, :, :].rearrange("p t w -> p (t w)"),
                                 slots[s].rearrange("(p t) w -> p (t w)", t=NT)).then_inc(came[s], 16)

            @block.vector
            def _(dve):
                for s in slots:
                    dve.wait_ge(came[s], 16)
                    dve.tensor_copy(lane_of[s][:, :], both[s][:, :, 0])
                    dve.tensor_copy(row_of[s][:, :], both[s][:, :, 1])


def name_rows_of_y(nc, first, N, row_of):
    own = Phase(nc)
    with own:
        later = own.enter_context(nc.sbuf_tensor("later", list(row_of.shape), F32))
        compared = own.sem("compared")
        with nc.Block() as block:
            @block.vector
            def _(dve):
                dve.tensor_scalar(later[:, :], row_of[:, :], float(first), float(N), ALU.is_ge, ALU.mult).then_inc(compared, 1)
                dve.wait_ge(compared, 1)
                dve.tensor_tensor(row_of[:, :], row_of[:, :], later[:, :], ALU.add)


def crowded_tiles(nc, name, side, EC, crowd, iota, lane_of, row_of, table, shift, banks):
    own = Phase(nc)
    mean = name != "A"
    with own:
        def sb(n, shape, dt=F32):
            return own.enter_context(nc.sbuf_tensor(f"crowd{name}_{n}", shape, dt))

        def sem(n):
            return own.sem(f"crowd{name}_{n}")
        tile_i = sb("tile_i", [P, 1], I32)
        shift_i = sb("shift_i", [P, 1], I32)
        offset = sb("offset", [P, 1])
        place = sb("place", [P, 1])
        column = sb("column", [P, 1])
        anchor = sb("anchor", [P, 1])
        row_now = sb("row_now", [P, 1], I32)
        target = sb("target", [P, 1], I32)
        rows = sb("rows", [P, D])
        hot = sb("hot", [P, P])
        total = sb("total", [P, D])
        degree = sb("degree", [P, 2])
        ones = sb("ones", [P, 1])
        tick = sb("tick", [P, 2])
        sum_ps, deg_ps = banks[0], banks[1]
        ticked = sem("ticked")
        tile_free = sem("tile_free")
        tile_in = sem("tile_in")
        offset_ready = sem("offset_ready")
        column_ready = sem("column_ready")
        hot_made = sem("hot_made")
        row_copied = sem("row_copied")
        gathered = sem("gathered")
        product_done = sem("product_done")
        emptied = sem("emptied")
        added = sem("added")
        counted = sem("counted")
        ratio_ready = sem("ratio_ready")
        placed = sem("placed")
        target_copied = sem("target_copied")
        result_ready = sem("result_ready")
        result_out = sem("result_out")
        tiles = crowd["tiles"][side]
        most = crowd["most"]
        last_tile = lane_of[side].shape[1] - 1

        with nc.Block() as block:
            @block.scalar
            def _(act):
                count = act.value_load(crowd["count"][side][0:1, 0:1], min_val=0, max_val=most)
                with act.If(count > 0):
                    with act.Fori(0, count) as j:
                        act.wait_ge(tile_free, j + 1)
                        act.dma_start(tile_i[:, :], tiles[bass.ds(j, 1), :].partition_broadcast(P)
                                     .rearrange("p a b -> p (a b)")).then_inc(tile_in, 16)
                        if mean:
                            act.wait_ge(result_ready, j + 1)
                            act.dma_start(table[bass.ds(j * P, P), :], total[:, :]).then_inc(result_out, 16)

            @block.gpsimd
            def _(pool):
                pool.memset(tick[:, :], 0.0).then_inc(ticked, 1)
                pool.memset(rows[:, :], 0.0).then_inc(ticked, 1)
                pool.memset(shift_i[:, :], shift).then_inc(ticked, 1)
                pool.wait_ge(ticked, 3)
                count = pool.value_load(crowd["count"][side][0:1, 0:1], min_val=0, max_val=most)
                with pool.If(count > 0):
                    with pool.Fori(0, count) as j:
                        with pool.Fori(0, EC) as c:
                            n = j * EC + c
                            pool.tensor_tensor(row_now[:, :], crowd["entry"][side][:, bass.ds(c, 1), 1], shift_i[:, :],
                                               ALU.add).then_inc(row_copied, 1)
                            pool.wait_ge(row_copied, n + 1)
                            anchor_on_pool(pool, tick)
                            pool.indirect_dma_start(
                                out=rows[:, :], out_offset=None, in_=table,
                                in_offset=bass.IndirectOffsetOnAxis(ap=row_now[:, 0:1], axis=0),
                                bounds_check=table.shape[0] - 1, oob_is_err=False).then_inc(gathered, 16)
                            pool.wait_ge(product_done, n + 1)
                        if not mean:
                            t = pool.value_load(tiles[bass.ds(j, 1), :], min_val=0, max_val=last_tile)
                            pool.tensor_copy(target[:, :], row_of[side][:, bass.ds(t, 1)]).then_inc(target_copied, 1)
                            pool.wait_ge(target_copied, j + 1)
                            pool.wait_ge(result_ready, j + 1)
                            anchor_on_pool(pool, tick)
                            pool.indirect_dma_start(
                                out=table, out_offset=bass.IndirectOffsetOnAxis(ap=target[:, 0:1], axis=0),
                                in_=total[:, :], in_offset=None,
                                bounds_check=table.shape[0] - 1, oob_is_err=False).then_inc(result_out, 16)
                            pool.wait_ge(result_out, 16 * j + 16)

            @block.tensor
            def _(pe):
                count = pe.value_load(crowd["count"][side][0:1, 0:1], min_val=0, max_val=most)
                with pe.If(count > 0):
                    with pe.Fori(0, count) as j:
                        with pe.Fori(0, EC) as c:
                            n = j * EC + c
                            pe.wait_ge(hot_made, n + 1)
                            pe.wait_ge(gathered, 16 * n + 16)
                            pe.matmul(deg_ps[:, 0:1], hot[:, :], ones[:, 0:1], start=True, stop=True)
                            pe.matmul(sum_ps[:, 0:D], hot[:, :], rows[:, :], start=True, stop=True).then_inc(product_done, 1)
                            pe.wait_ge(added, n + 1)
                            pe.wait_ge(counted, n + 1)

            @block.vector
            def _(dve):
                dve.memset(ones[:, :], 1.0).then_inc(tile_free, 1)
                dve.tensor_copy(place[:, :], crowd["lane"][:, 0:1]).then_inc(placed, 1)
                count = dve.value_load(crowd["count"][side][0:1, 0:1], min_val=0, max_val=most)
                with dve.If(count > 0):
                    with dve.Fori(0, count) as j:
                        t = dve.value_load(tiles[bass.ds(j, 1), :], min_val=0, max_val=last_tile)
                        dve.wait_ge(tile_in, 16 * j + 16)
                        dve.tensor_scalar(offset[:, :], tile_i[:, :], float(P), None, ALU.mult).then_inc(offset_ready, 1)
                        dve.memset(total[:, :], 0.0).then_inc(emptied, 1)
                        dve.memset(degree[:, :], 0.0).then_inc(emptied, 1)
                        dve.wait_ge(offset_ready, j + 1)
                        dve.wait_ge(emptied, 2 * j + 2)
                        dve.tensor_copy(anchor[:, :], offset[:, :]).then_inc(tile_free, 1)
                        with dve.Fori(0, EC) as c:
                            n = j * EC + c
                            dve.tensor_tensor(column[:, :], crowd["key"][side][:, bass.ds(c, 1)], offset[:, :],
                                              ALU.subtract).then_inc(column_ready, 1)
                            dve.wait_ge(column_ready, n + 1)
                            dve.tensor_scalar(hot[:, :], iota[:, 0:P], column[:, 0:1], None, ALU.is_equal).then_inc(hot_made, 1)
                            dve.wait_ge(product_done, n + 1)
                            dve.tensor_tensor(degree[:, 0:1], deg_ps[:, 0:1], degree[:, 0:1], ALU.add).then_inc(counted, 1)
                            dve.tensor_tensor(total[:, :], sum_ps[:, 0:D], total[:, :], ALU.add).then_inc(added, 1)
                            dve.wait_ge(added, n + 1)
                            dve.wait_ge(counted, n + 1)
                        if mean:
                            dve.tensor_scalar(degree[:, 1:2], degree[:, 0:1], 1.0, None, ALU.max).then_inc(ratio_ready, 1)
                            dve.wait_ge(ratio_ready, 3 * j + 1)
                            dve.reciprocal(degree[:, 0:1], degree[:, 1:2]).then_inc(ratio_ready, 1)
                            dve.wait_ge(ratio_ready, 3 * j + 2)
                            dve.tensor_scalar(total[:, :], total[:, :], degree[:, 0:1], None, ALU.mult).then_inc(ratio_ready, 1)
                            dve.wait_ge(ratio_ready, 3 * j + 3)
                            dve.wait_ge(placed, j + 1)
                            dve.tensor_copy(row_of[side][:, bass.ds(t, 1)], place[:, :]).then_inc(target_copied, 1)
                            dve.wait_ge(target_copied, j + 1)
                            dve.tensor_scalar(place[:, :], place[:, :], float(P), None, ALU.add).then_inc(placed, 1)
                        dve.tensor_copy(lane_of[side][:, bass.ds(t, 1)], crowd["lane"][:, 0:1]).then_inc(result_ready, 1)
                        dve.wait_ge(result_out, 16 * j + 16)


def pair_rows(table, k):
    return table[bass.ds(256 * k, 256), :].rearrange("(p j) d -> p (j d)", j=2)


def last_rows(table, k, lanes):
    return table[256 * k:256 * k + 2 * lanes, :].rearrange("(p j) d -> p (j d)", j=2)


def gated_block(nc, N, K, TAIL, iota, ident, ones16, eps, w_sb, bias3, lng_sb, lnb_sb, lane_of, row_of,
                x, msg_rows, x1_rows, h2_rows, banks):
    U = 8
    NT = 2 * K
    own = Phase(nc)
    with own:
        def sb(name, shape, dt=F32):
            return own.enter_context(nc.sbuf_tensor(name, shape, dt))

        def ring(name, n, shape, dt=F32):
            return [sb(f"{name}{m}", shape, dt) for m in range(n)]

        def sem(name):
            return own.sem("A_" + name)
        xb = ring("xb", 8, [P, 512])
        mb = ring("mb", 8, [P, 2, D])
        rows_now = ring("rows_now", 8, [P, 2], I32)
        hot = ring("hotA", 2, [P, 2, P])
        h = ring("h", 2, [P, 512])
        ht = ring("ht", 2, [P, 2, 2, P])
        z = ring("z", 2, [P, 512])
        r = ring("r", 2, [P, 2, 2, P])
        x1 = ring("x1b", 4, [P, 512])
        h2 = ring("h2b", 4, [P, 512])
        tick = sb("tick", [P, 2])
        GX, GH, GY = 0, 1, 2
        st = ring("st", 2, [P, 6, 6])
        mv = ring("mv", 2, [P, 6, 2])
        sd = ring("sd", 2, [P, 6])
        rs = ring("rs", 2, [P, 6])
        nm = ring("nm", 2, [P, 6])
        LX, LH, LY = 0, 3, 6
        STEPS = K + LY
        ht_ps, h1_ps, o_ps, zt_ps, counted = banks[0:2], banks[2:4], banks[4:6], banks[6], banks[7]
        place_now = ring("place_nowA", 4, [P, 1], I32)
        entry_now = ring("entry_nowA", 4, [P, 2], I32)

        x_in = [sem(f"x_in{m}") for m in range(8)]
        msg_in = [sem(f"msg_in{m}") for m in range(8)]
        stored = [sem(f"stored{m}") for m in range(4)]
        scattered = [sem(f"scattered{m}") for m in range(4)]
        cleared = sem("cleared")
        rows_copied = sem("rows_copied")
        entry_copied = sem("entry_copied")
        hot_made = sem("hot_made")
        st_done = {g: sem(f"st_done{g}") for g in (GX, GH, GY)}
        mv_set = sem("mv_set")
        mv_done = sem("mv_done")
        sd_done = sem("sd_done")
        rs_done = sem("rs_done")
        nm_done = sem("nm_done")
        h_ready = sem("h_ready")
        ht_done = sem("ht_done")
        ht_ready = sem("ht_ready")
        h1_done = sem("h1_done")
        z_ready = sem("z_ready")
        zt_done = sem("zt_done")
        r_ready = sem("r_ready")
        o_done = sem("o_done")
        x1_ready = sem("x1_ready")
        h2_ready = sem("h2_ready")
        rank_sems = dict(hot_made=sem("rank_hot_made"), added=sem("added"), ranked=sem("ranked"),
                         totalled=sem("totalled"))
        placed = sem("placed")

        with nc.Block() as block:
            @block.sync
            def _(sp):
                def load(i, c):
                    k = U * i + c
                    wait(sp, x1_ready, k - 7)
                    full = not (isinstance(k, int) and k == K - 1)
                    lanes = P if full else TAIL
                    sp.dma_start(xb[c % 8][0:lanes, :], pair_rows(x, k) if full else last_rows(x, k, lanes)).then_inc(x_in[c % 8], 16)

                def store(i, c):
                    k = U * i + c
                    sp.wait_ge(h2_ready, k + 1)
                    full = not (isinstance(k, int) and k == K - 1)
                    lanes = P if full else TAIL
                    for table, b in ((x1_rows, x1), (h2_rows, h2)):
                        sp.dma_start(pair_rows(table, k) if full else last_rows(table, k, lanes),
                                     b[c % 4][0:lanes, :]).then_inc(stored[c % 4], 16)

                sp.wait_ge(cleared, 17)
                run_steps(sp, K, U, [(0, load), (8, store)])
                for m in range(4):
                    sp.wait_ge(stored[m], 32 * ((K - m + 3) // 4))

            @block.gpsimd
            def _(pool):
                pool.memset(tick[:, :], 0.0).then_inc(cleared, 1)
                for m in range(8):
                    pool.memset(mb[m][:, :, :], 0.0).then_inc(cleared, 1)
                    pool.memset(xb[m][:, :], 0.0).then_inc(cleared, 1)
                pool.wait_ge(cleared, 17)

                def copy_rows(i, c):
                    k = U * i + c
                    wait(pool, msg_in[c % 8], 32 * (i + c // 8))
                    pool.tensor_copy(rows_now[c % 8][:, :], row_of[:, bass.ds(2 * k, 2)]).then_inc(rows_copied, 1)

                def copy_entry(i, c):
                    n = U * i + c
                    wait(pool, scattered[c % 4], 16 * (2 * i + c // 4))
                    pool.tensor_copy(entry_now[c % 4][:, :],
                                     entry[:, bass.ds(n, 1), :].rearrange("p c w -> p (c w)")).then_inc(entry_copied, 1)

                def ready(i, c):
                    pool.wait_ge(placed, U * i + c + 1)
                    pool.wait_ge(entry_copied, U * i + c + 1)

                def gather(i, c):
                    k = U * i + c
                    wait(pool, ht_done, k - 7)
                    pool.wait_ge(rows_copied, k + 1)
                    anchor_on_pool(pool, tick)
                    for j in range(2):
                        pool.indirect_dma_start(
                            out=mb[c % 8][:, j, :], out_offset=None, in_=msg_rows,
                            in_offset=bass.IndirectOffsetOnAxis(ap=rows_now[c % 8][:, j:j + 1], axis=0),
                            bounds_check=msg_rows.shape[0] - 1, oob_is_err=False).then_inc(msg_in[c % 8], 16)

                def scatter(i, c):
                    pool.indirect_dma_start(
                        out=slots, out_offset=bass.IndirectOffsetOnAxis(ap=place_now[c % 4][:, 0:1], axis=0),
                        in_=entry_now[c % 4][:, :], in_offset=None,
                        bounds_check=P * NT - 1, oob_is_err=False).then_inc(scattered[c % 4], 16)

                run_steps(pool, K, U, [(0, copy_rows), (0, gather)])

            @block.tensor
            def _(pe):
                def turn_and_sum(i, c):
                    k = U * i + c
                    pe.wait_ge(h_ready, k + 1)
                    pe.wait_ge(hot_made, k + 1)
                    pe.wait_ge(msg_in[c % 8], 32 * (i + c // 8 + 1))
                    wait(pe, ht_ready, k - 1)
                    for f in range(2):
                        for j in range(2):
                            to = ht_ps[c % 2][:, (2 * f + j) * P:(2 * f + j + 1) * P]
                            pe.matmul(to, h[c % 2][:, j * D + f * P:j * D + (f + 1) * P], ident[:, :],
                                      is_transpose=True, start=True, stop=False)
                            last = pe.matmul(to, mb[c % 8][:, j, f * P:(f + 1) * P], hot[c % 2][:, j, :],
                                             start=False, stop=True)
                    last.then_inc(ht_done, 1)

                def layer(i, c, ready, read, operand, w, bias, to, done):
                    k = U * i + c
                    pe.wait_ge(ready, k + 1)
                    wait(pe, read, k - 1)
                    for j in range(2):
                        part = to[c % 2][:, j * D:(j + 1) * D]
                        pe.matmul(part, ones16[:, :], bias[:, :], start=True, stop=False)
                        for f in range(2):
                            last = pe.matmul(part, operand[c % 2][:, f, j, :], w[:, f, :], start=False, stop=(f == 1))
                    last.then_inc(done, 1)

                def first(i, c):
                    layer(i, c, ht_ready, z_ready, ht, w_sb["w1"], bias3["b1"], h1_ps, h1_done)

                def turn(i, c):
                    k = U * i + c
                    pe.wait_ge(z_ready, k + 1)
                    wait(pe, r_ready, k)
                    for f in range(2):
                        for j in range(2):
                            last = pe.matmul(zt_ps[:, (2 * f + j) * P:(2 * f + j + 1) * P],
                                             z[c % 2][:, j * D + f * P:j * D + (f + 1) * P], ident[:, :],
                                             is_transpose=True, start=True, stop=True)
                    last.then_inc(zt_done, 1)

                def second(i, c):
                    layer(i, c, r_ready, x1_ready, r, w_sb["w2"], bias3["b2"], o_ps, o_done)

                run_steps(pe, K, U, [(2, turn_and_sum), (5, second), (4, turn), (2, first)])

            @block.scalar
            def _(act):
                def root(i, c):
                    s = U * i + c
                    wait(act, rs_done, s - 1)
                    act.wait_ge(mv_done, s + 1)
                    act.activation(sd[c % 2][:, :], mv[c % 2][:, :, 1], ACT.Sqrt, bias=eps[:, 0:1]).then_inc(sd_done, 1)

                def normalise(i, c, group, lag, func, to, of, done):
                    s = c + lag
                    act.wait_ge(nm_done, U * i + s + 1)
                    for j in range(2):
                        m = 2 * group + j
                        last = act.activation(to[:, j * D:(j + 1) * D], of[:, j * D:(j + 1) * D], func,
                                              bias=nm[s % 2][:, m:m + 1], scale=rs[s % 2][:, m:m + 1])
                    last.then_inc(done, 1)

                def h_out(i, c):
                    wait(act, ht_done, U * i + c - 1)
                    normalise(i, c, GX, LX, ACT.Relu, h[c % 2], xb[c % 8], h_ready)

                def ht_out(i, c):
                    k = U * i + c
                    wait(act, h1_done, k - 1)
                    act.wait_ge(ht_done, k + 1)
                    act.activation(ht[c % 2][:, :, :, :].rearrange("p f j n -> p (f j n)"), ht_ps[c % 2][:, :],
                                   ACT.Copy).then_inc(ht_ready, 1)

                def z_out(i, c):
                    wait(act, zt_done, U * i + c - 1)
                    normalise(i, c, GH, LH, ACT.Identity, z[c % 2], h1_ps[c % 2], z_ready)

                def r_out(i, c):
                    k = U * i + c
                    wait(act, o_done, k - 1)
                    act.wait_ge(zt_done, k + 1)
                    for f in range(2):
                        last = act.activation(r[c % 2][:, f, :, :].rearrange("p j n -> p (j n)"),
                                              zt_ps[:, f * D:(f + 1) * D], ACT.Relu,
                                              bias=lnb_sb[:, f:f + 1], scale=lng_sb[:, f:f + 1])
                    last.then_inc(r_ready, 1)

                def h2_out(i, c):
                    wait(act, stored[c % 4], 32 * (2 * i + c // 4))
                    normalise(i, c, GY, LY, ACT.Relu, h2[c % 4], x1[c % 4], h2_ready)

                run_steps(act, K, U, [(4, z_out), (1, h_out), (2, ht_out), (7, h2_out), (4, r_out), (0, root, STEPS)])

            @block.vector
            def _(dve):
                for m in range(2):
                    dve.memset(mv[m][:, :, :], 1.0).then_inc(mv_set, 1)
                dve.wait_ge(mv_set, 2)

                def take_stats(i, c, group, lag, of):
                    for j in range(2):
                        last = dve.bn_stats(st[(c + lag) % 2][:, 2 * group + j, :], of[:, j * D:(j + 1) * D])
                    last.then_inc(st_done[group], 1)

                def stats_x(i, c):
                    dve.wait_ge(x_in[c % 8], 16 * (i + c // 8 + 1))
                    take_stats(i, c, GX, LX, xb[c % 8])

                def stats_h(i, c):
                    wait(dve, mv_done, U * i + c + LH - 1)
                    dve.wait_ge(h1_done, U * i + c + 1)
                    take_stats(i, c, GH, LH, h1_ps[c % 2])

                def stats_y(i, c):
                    dve.wait_ge(x1_ready, U * i + c + 1)
                    take_stats(i, c, GY, LY, x1[c % 4])

                def one_hot(i, c):
                    k = U * i + c
                    wait(dve, ht_done, k - 1)
                    for j in range(2):
                        if j == 1:
                            if isinstance(k, int):
                                for group, lag in ((GX, LX), (GH, LH), (GY, LY)):
                                    wait(dve, st_done[group], min(k + 1 - lag + 1, K))
                            else:
                                dve.wait_ge(st_done[GY], k + 1 - LY + 1)
                            wait(dve, nm_done, k + 1 - 1)
                        last = dve.tensor_scalar(hot[c % 2][:, j, :], iota[:, 0:P], lane_of[:, bass.ds(2 * k + j, 1)], None,
                                                 ALU.is_equal)
                    last.then_inc(hot_made, 1)

                def aggregate(i, c):
                    s = U * i + c
                    groups = [(g, lag) for g, lag in ((GX, LX), (GH, LH), (GY, LY))
                              if not isinstance(s, int) or 0 <= s - lag < K]
                    if isinstance(s, int):
                        for g, lag in groups:
                            dve.wait_ge(st_done[g], s - lag + 1)
                        wait(dve, nm_done, s - 1)
                    for g, _ in groups:
                        for j in range(2):
                            last = dve.bn_aggr(mv[c % 2][:, 2 * g + j, :], st[c % 2][:, 2 * g + j, :])
                    last.then_inc(mv_done, 1)

                def factors(i, c):
                    s = U * i + c
                    if isinstance(s, int):
                        for done, lag in ((h_ready, LX), (z_ready, LH), (h2_ready, LY)):
                            wait(dve, done, min(s - 1 - lag, K))
                    else:
                        dve.wait_ge(h2_ready, s - 1 - LY)
                        dve.wait_ge(h_ready, s - 1 - LX)
                        dve.wait_ge(z_ready, s - 1 - LH)
                    dve.wait_ge(sd_done, s + 1)
                    dve.reciprocal(rs[c % 2][:, :], sd[c % 2][:, :]).then_inc(rs_done, 1)
                    dve.wait_ge(rs_done, s + 1)
                    dve.scalar_tensor_tensor(out=nm[c % 2][:, :], in0=mv[c % 2][:, :, 0], scalar=-1.0,
                                             in1=rs[c % 2][:, :], op0=ALU.mult, op1=ALU.mult).then_inc(nm_done, 1)

                def residual(i, c):
                    k = U * i + c
                    wait(dve, stored[c % 4], 32 * (2 * i + c // 4))
                    wait(dve, h2_ready, k - 3)
                    dve.wait_ge(o_done, k + 1)
                    dve.tensor_tensor(x1[c % 4][:, :], o_ps[c % 2][:, :], xb[c % 8][:, :], ALU.add).then_inc(x1_ready, 1)


                def place(i, c):
                    n = U * i + c
                    wait(dve, scattered[c % 4], 16 * (2 * i + c // 4))
                    dve.wait_ge(rank_sems["ranked"], n + 1)
                    dve.scalar_tensor_tensor(out=place_now[c % 4][:, :], in0=ranks.rank["src"][:, bass.ds(n, 1)],
                                             scalar=float(NT), in1=ranks.tile["src"][:, bass.ds(n, 1)],
                                             op0=ALU.mult, op1=ALU.add).then_inc(placed, 1)

                run_steps(dve, K, U, [(LH, stats_h), (6, residual), (LX, stats_x), (LY, stats_y),
                                      (1, one_hot), (0, aggregate, STEPS), (0, factors, STEPS)])


def mean_block(nc, name, N, K, TAIL, iota, ident, ones16, eps, w, bias, g_wide, b_wide, lane_of, row_of, rdeg,
               own_rows, table, residual_rows, result, banks):
    U = 6
    last_layer = residual_rows is not None
    own = Phase(nc)
    with own:
        def sb(n, shape, dt=F32):
            return own.enter_context(nc.sbuf_tensor(f"{name}_{n}", shape, dt))

        def ring(n, count, shape, dt=F32):
            return [sb(f"{n}{m}", shape, dt) for m in range(count)]

        def sem(n):
            return own.sem(f"{name}_{n}")
        hb = ring("hb", 6, [P, 512])
        nb = ring("nb", 6, [P, 2, D])
        rows_now = ring("rows_now", 6, [P, 2], I32)
        hot = ring("hot", 2, [P, 2, P])
        hm = ring("hm", 2, [P, 512])
        ht = ring("ht", 2, [P, 2, 2, P])
        tick = sb("tick", [P, 2])
        squares = ring("squares", 2, [P, 512])
        ss = ring("ss", 2, [P, 6])
        sd = ring("sd", 2, [P, 6])
        rs = ring("rs", 2, [P, 6])
        u = ring("u", 6, [P, 512])
        v = ring("v", 2, [P, 512])
        y = ring("y", 6, [P, 512])
        dg = ring("dg", 2, [P, 2])
        ones = sb("ones", [P, 2])
        if last_layer:
            xb = ring("xb", 6, [P, 512])
            res = ring("res", 6, [P, 512])
        agg_ps, ht_ps, z_ps, deg_ps = banks[0:2], banks[2:4], banks[4:6], banks[6:8]

        h_in = [sem(f"h_in{m}") for m in range(6)]
        nb_in = [sem(f"nb_in{m}") for m in range(6)]
        stored = [sem(f"stored{m}") for m in range(6)]
        cleared = sem("cleared")
        rows_copied = sem("rows_copied")
        hot_made = sem("hot_made")
        agg_done = sem("agg_done")
        deg_raised = sem("deg_raised")
        rdeg_ready = sem("rdeg_ready")
        hm_ready = sem("hm_ready")
        ht_done = sem("ht_done")
        ht_ready = sem("ht_ready")
        z_done = sem("z_done")
        ss_set = sem("ss_set")
        ss_done = sem("ss_done")
        sd_done = sem("sd_done")
        rs_done = sem("rs_done")
        u_ready = sem("u_ready")
        v_ready = sem("v_ready")
        y_ready = sem("y_ready")
        if last_layer:
            x_in = [sem(f"x_in{m}") for m in range(6)]
            res_ready = sem("res_ready")
        CLEARED = 14 + (6 if last_layer else 0)

        with nc.Block() as block:
            @block.sync
            def _(sp):
                def load(i, c):
                    k = U * i + c
                    wait(sp, hm_ready, k - 5)
                    full = not (isinstance(k, int) and k == K - 1)
                    lanes = P if full else TAIL
                    sp.dma_start(hb[c % 6][0:lanes, :], pair_rows(own_rows, k) if full else last_rows(own_rows, k, lanes)).then_inc(h_in[c % 6], 16)

                def load_residual(i, c):
                    k = U * i + c
                    wait(sp, res_ready, k - 5)
                    full = not (isinstance(k, int) and k == K - 1)
                    lanes = P if full else TAIL
                    sp.dma_start(xb[c % 6][0:lanes, :],
                                 pair_rows(residual_rows, k) if full else last_rows(residual_rows, k, lanes)).then_inc(x_in[c % 6], 16)

                def store(i, c):
                    k = U * i + c
                    full = not (isinstance(k, int) and k == K - 1)
                    lanes = P if full else TAIL
                    sp.wait_ge(res_ready if last_layer else y_ready, k + 1)
                    b = res if last_layer else y
                    sp.dma_start(pair_rows(result, k) if full else last_rows(result, k, lanes),
                                 b[c % 6][0:lanes, :]).then_inc(stored[c % 6], 16)

                sp.wait_ge(cleared, CLEARED)
                if last_layer:
                    run_steps(sp, K, U, [(0, load), (9, load_residual), (15, store)])
                else:
                    run_steps(sp, K, U, [(0, load), (14, store)])
                for m in range(6):
                    sp.wait_ge(stored[m], 16 * ((K - m + 5) // 6))

            @block.gpsimd
            def _(pool):
                pool.memset(tick[:, :], 0.0).then_inc(cleared, 1)
                for m in range(6):
                    pool.memset(nb[m][:, :, :], 0.0).then_inc(cleared, 1)
                    pool.memset(hb[m][:, :], 0.0).then_inc(cleared, 1)
                    if last_layer:
                        pool.memset(xb[m][:, :], 0.0).then_inc(cleared, 1)
                pool.memset(ones[:, :], 1.0).then_inc(cleared, 1)
                pool.wait_ge(cleared, CLEARED)

                def copy_rows(i, c):
                    k = U * i + c
                    wait(pool, nb_in[c % 6], 32 * (i + c // 6))
                    pool.tensor_copy(rows_now[c % 6][:, :], row_of[:, bass.ds(2 * k, 2)]).then_inc(rows_copied, 1)

                def gather(i, c):
                    k = U * i + c
                    wait(pool, agg_done, k - 5)
                    pool.wait_ge(rows_copied, k + 1)
                    anchor_on_pool(pool, tick)
                    for j in range(2):
                        pool.indirect_dma_start(
                            out=nb[c % 6][:, j, :], out_offset=None, in_=table,
                            in_offset=bass.IndirectOffsetOnAxis(ap=rows_now[c % 6][:, j:j + 1], axis=0),
                            bounds_check=table.shape[0] - 1, oob_is_err=False).then_inc(nb_in[c % 6], 16)

                run_steps(pool, K, U, [(0, copy_rows), (0, gather)])

            @block.tensor
            def _(pe):
                def aggregate(i, c):
                    k = U * i + c
                    pe.wait_ge(hot_made, k + 1)
                    pe.wait_ge(nb_in[c % 6], 32 * (i + c // 6 + 1))
                    wait(pe, hm_ready, k - 1)
                    if not last_layer:
                        wait(pe, deg_raised, k - 1)
                        for j in range(2):
                            pe.matmul(deg_ps[c % 2][:, 2 * j:2 * j + 1], hot[c % 2][:, j, :], ones[:, 0:1], start=True, stop=True)
                    for j in range(2):
                        last = pe.matmul(agg_ps[c % 2][:, j * D:(j + 1) * D], hot[c % 2][:, j, :], nb[c % 6][:, j, :],
                                         start=True, stop=True)
                    last.then_inc(agg_done, 1)

                def turn(i, c):
                    k = U * i + c
                    pe.wait_ge(hm_ready, k + 1)
                    wait(pe, ht_ready, k - 1)
                    for f in range(2):
                        for j in range(2):
                            last = pe.matmul(ht_ps[c % 2][:, (2 * f + j) * P:(2 * f + j + 1) * P],
                                             hm[c % 2][:, j * D + f * P:j * D + (f + 1) * P], ident[:, :],
                                             is_transpose=True, start=True, stop=True)
                    last.then_inc(ht_done, 1)

                def layer(i, c):
                    k = U * i + c
                    pe.wait_ge(ht_ready, k + 1)
                    wait(pe, ss_done, k - 1)
                    for j in range(2):
                        part = z_ps[c % 2][:, j * D:(j + 1) * D]
                        pe.matmul(part, ones16[:, :], bias[:, :], start=True, stop=False)
                        for f in range(2):
                            last = pe.matmul(part, ht[c % 2][:, f, j, :], w[:, f, :], start=False, stop=(f == 1))
                    last.then_inc(z_done, 1)

                run_steps(pe, K, U, [(1, aggregate), (3, turn), (5, layer)])

            @block.scalar
            def _(act):
                def root(i, c):
                    k = U * i + c
                    if c % 3 != 2 and not (isinstance(k, int) and k == K - 1):
                        return
                    group = (U // 3) * i + c // 3
                    wait(act, rs_done, group - 1)
                    act.wait_ge(ss_done, k + 1)
                    act.activation(sd[c // 3 % 2][:, :], ss[c // 3 % 2][:, :], ACT.Sqrt, bias=eps[:, 0:1],
                                   scale=1.0 / D).then_inc(sd_done, 1)

                def square(i, c):
                    k = U * i + c
                    act.wait_ge(u_ready, k + 1)
                    wait(act, ss_done, k - 1)
                    wait(act, sd_done, (U // 3) * i + c // 3 - 1)
                    for j in range(2):
                        half = slice(j * D, (j + 1) * D)
                        m = 2 * (c % 3) + j
                        last = act.activation(squares[c % 2][:, half], z_ps[c % 2][:, half], ACT.Square,
                                              accum_out=ss[c // 3 % 2][:, m:m + 1])
                    last.then_inc(ss_done, 1)

                def ht_out(i, c):
                    k = U * i + c
                    wait(act, z_done, k - 1)
                    act.wait_ge(ht_done, k + 1)
                    act.activation(ht[c % 2][:, :, :, :].rearrange("p f j n -> p (f j n)"), ht_ps[c % 2][:, :],
                                   ACT.Copy).then_inc(ht_ready, 1)

                def silu(i, c):
                    k = U * i + c
                    if last_layer:
                        wait(act, res_ready, k - 5)
                    else:
                        wait(act, stored[c % 6], 16 * (i + c // 6))
                    act.wait_ge(v_ready, k + 1)
                    act.activation(y[c % 6][:, :], v[c % 2][:, :], ACT.Silu).then_inc(y_ready, 1)

                run_steps(act, K, U, [(4, ht_out), (SC + 1, silu), (7, root), (6, square)])

            @block.vector
            def _(dve):
                for m in range(2):
                    dve.memset(ss[m][:, :], 1.0).then_inc(ss_set, 1)

                def one_hot(i, c):
                    k = U * i + c
                    wait(dve, agg_done, k - 1)
                    for j in range(2):
                        last = dve.tensor_scalar(hot[c % 2][:, j, :], iota[:, 0:P], lane_of[:, bass.ds(2 * k + j, 1)], None,
                                                 ALU.is_equal)
                    last.then_inc(hot_made, 1)

                def degree(i, c):
                    k = U * i + c
                    dve.wait_ge(agg_done, k + 1)
                    wait(dve, rdeg_ready, k - 1)
                    dve.tensor_scalar(dg[c % 2][:, :], deg_ps[c % 2][:, 0:4:2], 1.0, None, ALU.max).then_inc(deg_raised, 1)

                def invert_degree(i, c):
                    k = U * i + c
                    dve.wait_ge(deg_raised, k + 1)
                    dve.reciprocal(rdeg[:, bass.ds(2 * k, 2)], dg[c % 2][:, :]).then_inc(rdeg_ready, 1)

                def mean(i, c):
                    k = U * i + c
                    dve.wait_ge(agg_done, k + 1)
                    dve.wait_ge(h_in[c % 6], 16 * (i + c // 6 + 1))
                    wait(dve, ht_done, k - 1)
                    if not last_layer:
                        dve.wait_ge(rdeg_ready, k + 1)
                    for j in range(2):
                        half = slice(j * D, (j + 1) * D)
                        last = dve.scalar_tensor_tensor(out=hm[c % 2][:, half], in0=agg_ps[c % 2][:, half],
                                                        scalar=rdeg[:, bass.ds(2 * k + j, 1)], in1=hb[c % 6][:, half],
                                                        op0=ALU.mult, op1=ALU.add)
                    last.then_inc(hm_ready, 1)

                def by_gain(i, c):
                    k = U * i + c
                    wait(dve, v_ready, k - 5)
                    dve.wait_ge(z_done, k + 1)
                    dve.tensor_tensor(u[c % 6][:, :], z_ps[c % 2][:, :], g_wide[:, :], ALU.mult).then_inc(u_ready, 1)

                def invert(i, c):
                    k = U * i + c
                    if c % 3 != 2 and not (isinstance(k, int) and k == K - 1):
                        return
                    group = (U // 3) * i + c // 3
                    wait(dve, v_ready, 3 * (group - 1))
                    dve.wait_ge(sd_done, group + 1)
                    dve.reciprocal(rs[c // 3 % 2][:, :], sd[c // 3 % 2][:, :]).then_inc(rs_done, 1)

                def scale(i, c):
                    k = U * i + c
                    wait(dve, y_ready, k - 1)
                    dve.wait_ge(u_ready, k + 1)
                    dve.wait_ge(rs_done, (U // 3) * i + c // 3 + 1)
                    for j in range(2):
                        half = slice(j * D, (j + 1) * D)
                        m = 2 * (c % 3) + j
                        last = dve.scalar_tensor_tensor(out=v[c % 2][:, half], in0=u[c % 6][:, half],
                                                        scalar=rs[c // 3 % 2][:, m:m + 1], in1=b_wide[:, :],
                                                        op0=ALU.mult, op1=ALU.add)
                    last.then_inc(v_ready, 1)

                def residual(i, c):
                    k = U * i + c
                    dve.wait_ge(y_ready, k + 1)
                    dve.wait_ge(x_in[c % 6], 16 * (i + c // 6 + 1))
                    wait(dve, stored[c % 6], 16 * (i + c // 6))
                    dve.tensor_tensor(res[c % 6][:, :], y[c % 6][:, :], xb[c % 6][:, :], ALU.add).then_inc(res_ready, 1)

                stages = [(6, by_gain)] + ([(2, degree)] if not last_layer else [(SC + 2, residual)])
                stages += [(0, one_hot), (8, invert)] + ([] if last_layer else [(2, invert_degree)])
                run_steps(dve, K, U, stages + [(2, mean), (SC, scale)])


_INS = ['x', 'src', 'dst', 'edge_attr_17', 'L0_gnn_ew1', 'L0_gnn_eb1', 'L0_gnn_ew2', 'L0_gnn_eb2', 'L0_gnn_lew',
        'L0_gnn_leb', 'L0_gnn_w1', 'L0_gnn_b1', 'L0_gnn_ln_g', 'L0_gnn_ln_b', 'L0_gnn_w2', 'L0_gnn_b2',
        'L1_gnn_W0', 'L1_gnn_b0', 'L1_gnn_g0', 'L1_gnn_beta0', 'L1_gnn_W1', 'L1_gnn_b1', 'L1_gnn_g1', 'L1_gnn_beta1']


def kernel(**inputs):
    import numpy as _np
    import concourse.bacc as _bacc
    from concourse import mybir as _mybir
    from concourse.bass_utils import run_bass_kernel_spmd as _run

    nc = _bacc.Bacc("TRN2", target_bir_lowering=False, num_devices=1)
    arrays, args = {}, []
    for name in _INS:
        a = _np.asarray(inputs[name])
        if name in ('L1_gnn_W0', 'L1_gnn_W1'):
            a = a.T
        a = _np.ascontiguousarray(a)
        arrays[f"in_{name}_dram"] = a
        args.append(nc.dram_tensor(f"in_{name}_dram", a.shape, _mybir.dt.from_np(a.dtype), kind="ExternalInput").ap())
    shape = _np.asarray(inputs['x']).shape
    args.append(nc.dram_tensor("out_0_dram", shape, _mybir.dt.from_np(_np.dtype('float32')), kind="ExternalOutput").ap())
    program(nc, *args)
    r = _run(nc, [arrays], core_ids=[0])
    return r.results[0]["out_0_dram"]
```

```python
import concourse.bass as bass
from concourse import mybir
from contextlib import ExitStack

P = 128
D = 256
RAW = 16
EPS = 1e-5
NO_LANE = 512
SC = 10
NO_ROW = 1 << 20
NO_NODE = 1 << 23

F32 = mybir.dt.float32
BF16 = mybir.dt.bfloat16
I32 = mybir.dt.int32
ALU = mybir.AluOpType
ACT = mybir.ActivationFunctionType


def run_steps(eng, count, unroll, stages):
    stages = [(*stage, count)[:3] for stage in stages]
    deepest = max(lag for lag, _, _ in stages)
    first = deepest + unroll
    rounds = max(0, (count - 1 - first) // unroll)
    if rounds < 2:
        rounds = 0

    def outside(steps):
        for s in steps:
            for lag, body, items in stages:
                if 0 <= s - lag < items:
                    body(0, s - lag)

    outside(range(first))
    if rounds:
        with eng.Fori(0, rounds) as i:
            for u in range(unroll):
                for lag, body, _ in stages:
                    body(i, first + u - lag)
    outside(range(first + rounds * unroll, max(lag + items for lag, _, items in stages)))


class Phase(ExitStack):

    def __init__(self, nc):
        super().__init__()
        self.nc, self.semaphores = nc, []
        self.callback(self.give_back)

    def sem(self, name):
        self.semaphores.append(self.nc.alloc_semaphore(name))
        return self.semaphores[-1]

    def give_back(self):
        self.nc.clear_and_free_semaphores(self.semaphores)
        self.nc.all_engine_barrier()


def anchor_on_pool(pool, tile, at=0):
    pool.tensor_tensor(tile[:, 2 * at:2 * at + 1], tile[:, 1:2], tile[:, 1:2], ALU.mult)


def wait(eng, semaphore, value):
    if isinstance(value, int) and value <= 0:
        return
    eng.wait_ge(semaphore, value)


def program(nc, x, src, dst, attr, ew1, eb1, ew2, eb2, lew, leb, w1, b1, ln_g, ln_b, w2, b2,
            wt0, bb0, g0, beta0, wt1, bb1, g1, beta1, out):
    N = x.shape[0]
    E = src.shape[0]
    EC = -(-E // P)
    LAST = E - (P - 1) * EC
    assert 0 < LAST <= EC and EC % 4 == 0
    PAIRS = -(-N // 256)
    assert PAIRS > 8
    assert EC == PAIRS
    TAIL = (N - (PAIRS - 1) * 256) // 2
    assert N % 2 == 0
    NT = 2 * PAIRS

    MR = P * EC
    rows = nc.dram_tensor("rows", (MR + 2 * N, D), F32, kind="Internal").ap()
    msg_rows, h2_rows, y_rows = rows[0:MR, :], rows[MR:MR + N, :], rows[MR + N:, :]
    x1_rows = nc.dram_tensor("x1_rows", (N, D), F32, kind="Internal").ap()
    slots = {side: nc.dram_tensor(f"slots_{side}", (P * NT, 2), I32, kind="Internal").ap()
             for side in ("dst", "src")}

    whole = ExitStack()
    with whole:
        def keep(name, shape, dt):
            return whole.enter_context(nc.sbuf_tensor(name, shape, dt))

        iota = keep("iota", [P, max(NT, P)], F32)
        ident = keep("ident", [P, P], F32)
        ones16 = keep("ones16", [P, P], BF16)
        eps = keep("eps", [P, 1], F32)
        w_sb = {n: keep(n + "_sb", [P, 2, D], F32) for n in ("w1", "w2", "wt0", "wt1")}
        bias3 = {n: keep(n + "_3", [P, D], BF16) for n in ("b1", "bb0", "bb1")}
        lng_sb = keep("lng_sb", [P, 2], F32)
        lnb_sb = keep("lnb_sb", [P, 2], F32)
        wide = {n: keep(n + "_wide", [P, (1 if n[0:4] == "beta" else 2) * D], F32)
                for n in ("g0", "beta0", "g1", "beta1", "b2")}
        lane_of = {side: keep(f"lane_of_{side}", [P, NT], F32) for side in ("dst", "src")}
        row_of = {side: keep(f"row_of_{side}", [P, NT], I32) for side in ("dst", "src")}
        rdeg = keep("rdeg", [P, NT], F32)
        tile = {side: keep(f"tile_{side}", [P, EC], F32) for side in ("dst", "src")}
        before = keep("before", [P, P], BF16)
        rest = keep("rest", [P, P], BF16)
        banks = [whole.enter_context(nc.psum_tensor(f"bank{n}", [P, 512], F32)) for n in range(8)]

        counted = banks[7]

        crowd = dict(
            key={side: keep(f"key_{side}", [P, EC], F32) for side in ("dst", "src")},
            entry={side: keep(f"entry_{side}", [P, EC, 2], I32) for side in ("dst", "src")},
            count={side: keep(f"crowded_{side}", [P, 1], I32) for side in ("dst", "src")},
            tiles={side: nc.dram_tensor(f"crowded_tiles_{side}", (2 * P, 1), I32, kind="Internal").ap()
                   for side in ("dst", "src")},
            lane=keep("lane", [P, 2], F32), most=max(1, min(E // (P + 1), NT)))
        assert E // (P + 1) <= 2 * P

        setup = dict(N=N, E=E, EC=EC, LAST=LAST, NT=NT)
        edges = ExitStack()
        with edges:
            def ek(name, shape, dt):
                return edges.enter_context(nc.sbuf_tensor(name, shape, dt))
            e = dict(
                ends={side: ek(f"ends_{side}", [P, EC], I32) for side in ("dst", "src")},
                tile=tile, before=before, rest=rest,
                entry=crowd["entry"], lane=crowd["lane"],
                attr=ek("attr_sb", [P, EC * 17], F32), gate=ek("gate", [P, EC], F32),
                xrow=ek("xrow_of_src", [P, EC], I32),
                ew1=ek("ew1_sb", [RAW, P], F32), ew2=ek("ew2_sb", [P, P], F32),
                lew=ek("lew_sb", [P, D], F32), eb1=ek("eb1_sb", [P, 1], F32),
                eb2=ek("eb2_sb", [P, 1], F32), leb=ek("leb_wide", [P, D], F32))
            load_and_prepare(nc, setup, e, iota, ident, ones16, eps, w_sb, bias3, lng_sb, lnb_sb, wide,
                             slots, dict(w1=w1, w2=w2, wt0=wt0, wt1=wt1, b1=b1, b2=b2, bb0=bb0, bb1=bb1,
                                         ln_g=ln_g, ln_b=ln_b, g0=g0, beta0=beta0, g1=g1, beta1=beta1,
                                         src=src, dst=dst, attr=attr, ew1=ew1, ew2=ew2, lew=lew,
                                         eb1=eb1, eb2=eb2, leb=leb))
            messages(nc, setup, e, iota, ident, eps, slots["dst"], x, msg_rows, banks, counted)
        read_slots(nc, setup, e, "dst", counted, crowd, slots["dst"], lane_of["dst"], row_of["dst"])
        crowded_tiles(nc, "A", "dst", EC, crowd, iota, lane_of, row_of, msg_rows, 0, banks)
        gated_block(nc, N, PAIRS, TAIL, iota, ident, ones16, eps, w_sb, bias3, wide["b2"], lng_sb, lnb_sb,
                    lane_of["dst"], row_of["dst"], x, msg_rows, x1_rows, h2_rows, banks, e, slots["src"], counted)
        read_slots(nc, setup, e, "src", counted, crowd, slots["src"], lane_of["src"], row_of["src"])
        crowded_tiles(nc, "B", "src", EC, crowd, iota, lane_of, row_of, rows[0:MR + N, :], 0, banks)
        mean_block(nc, "B", N, PAIRS, TAIL, iota, ident, ones16, eps, w_sb["wt0"], bias3["bb0"],
                   wide["g0"], wide["beta0"], lane_of["src"], row_of["src"], rdeg, h2_rows, rows[0:MR + N, :], None, y_rows, banks)
        name_rows_of_y(nc, MR, N, row_of["src"])
        crowded_tiles(nc, "C", "src", EC, crowd, iota, lane_of, row_of, rows, N, banks)
        mean_block(nc, "C", N, PAIRS, TAIL, iota, ident, ones16, eps, w_sb["wt1"], bias3["bb1"],
                   wide["g1"], wide["beta1"], lane_of["src"], row_of["src"], rdeg, y_rows, rows, x1_rows, out, banks)


def load_and_prepare(nc, dims, e, iota, ident, ones16, eps, w_sb, bias3, lng_sb, lnb_sb, wide, slots, a):
    N, EC, LAST, NT = dims["N"], dims["EC"], dims["LAST"], dims["NT"]
    own = Phase(nc)
    with own:
        def sb(name, shape, dt):
            return own.enter_context(nc.sbuf_tensor(name, shape, dt))

        def sem(name):
            return own.sem(name)

        empty = sb("empty", [P, NT, 2], I32)
        names = ("b1", "bb0", "bb1")
        raw = {n: sb(n + "_raw", [P, D], F32) for n in names}
        part = {n: sb(n + "_part", [P, D], BF16) for n in names}
        part2 = {n: sb(n + "_part2", [P, D], BF16) for n in names}
        left = {n: sb(n + "_left", [P, D], F32) for n in names}
        bit = {s: sb(f"bit_{s}", [P, EC], I32) for s in ("dst", "src")}
        high = {s: sb(f"high_{s}", [P, EC], I32) for s in ("dst", "src")}

        weights_in = sem("weights_in")
        biases_in = sem("biases_in")
        ends_in = sem("ends_in")
        attr_in = sem("attr_in")
        padded = sem("padded")
        empty_made = sem("empty_made")
        empty_out = sem("empty_out")
        made = sem("made")
        split = sem("split")
        raw_cleared = sem("raw_cleared")
        summed = sem("rows_summed")
        averaged = sem("rows_averaged")
        taken_off = sem("means_taken_off")
        ended = sem("ended")
        numbered = sem("numbered")

        sets = [(w_sb[n][:, :, :], a[n].rearrange("(c p) n -> p c n", p=P)) for n in ("w1", "w2", "wt0", "wt1")]
        sets += [(e["ew1"][:, :], a["ew1"]), (e["ew2"][:, :], a["ew2"]), (e["lew"][:, :], a["lew"]),
                 (lng_sb[:, :], a["ln_g"].rearrange("(c p) -> p c", p=P)),
                 (lnb_sb[:, :], a["ln_b"].rearrange("(c p) -> p c", p=P)),
                 (e["eb1"][:, :], a["eb1"].rearrange("(p c) -> p c", c=1)),
                 (e["eb2"][:, :], a["eb2"].rearrange("(p c) -> p c", c=1)),
                 (e["leb"][:, :], a["leb"].partition_broadcast(P))]
        sets += [(wide[n][:, j * D:(j + 1) * D], a[n].partition_broadcast(P))
                 for n, j in (("g0", 0), ("g0", 1), ("beta0", 0), ("g1", 0), ("g1", 1), ("beta1", 0),
                              ("b2", 0), ("b2", 1))]
        parts = [(0, 112), (112, P - 1)]
        centred = [(w_sb[n][:, f, :], f"{n}_{f}") for n in ("wt0", "wt1") for f in range(2)]
        centred_biases = [(raw[n][:, :], n) for n in ("bb0", "bb1")]
        sums = {n: sb("sums_" + n, [P, 6], F32) for _, n in centred + centred_biases}
        means = {n: sb("means_" + n, [P, 2], F32) for _, n in centred + centred_biases}

        with nc.Block() as block:
            @block.sync
            def _(sp):
                sp.wait_ge(padded, 3)
                for side in ("dst", "src"):
                    v = a[side]
                    for lo, hi in parts:
                        sp.dma_start(e["ends"][side][lo:hi, :],
                                     v[lo * EC:hi * EC].rearrange("(p c) -> p c", c=EC)).then_inc(ends_in, 16)
                    sp.dma_start(e["ends"][side][P - 1:P, 0:LAST],
                                 v[(P - 1) * EC:].rearrange("(p c) -> p c", p=1)).then_inc(ends_in, 16)
                for lo, hi in parts:
                    sp.dma_start(e["attr"][lo:hi, :],
                                 a["attr"][lo * EC:hi * EC, :].rearrange("(p c) f -> p (c f)", c=EC)).then_inc(attr_in, 16)
                sp.dma_start(e["attr"][P - 1:P, 0:LAST * 17],
                             a["attr"][(P - 1) * EC:, :].rearrange("(p c) f -> p (c f)", p=1)).then_inc(attr_in, 16)
                sp.wait_ge(empty_made, 2)
                for side in ("dst", "src"):
                    sp.dma_start(slots[side].rearrange("(p t) w -> p (t w)", t=NT),
                                 empty[:, :, :].rearrange("p t w -> p (t w)")).then_inc(empty_out, 16)
                sp.wait_ge(empty_out, 32)
                sp.wait_ge(attr_in, 48)

            @block.scalar
            def _(act):
                act.wait_ge(raw_cleared, len(names))
                for n in names:
                    act.dma_start(raw[n][0:65:32, :], a[n].partition_broadcast(3)).then_inc(biases_in, 16)
                with nc.allow_non_contiguous_dma(reason="per-feature scales, 256 numbers each"):
                    for to, of in sets:
                        act.dma_start(to, of).then_inc(weights_in, 16)
                act.wait_ge(weights_in, 16 * len(sets))

            @block.gpsimd
            def _(pool):
                for n in names:
                    pool.memset(raw[n][:, :], 0.0).then_inc(raw_cleared, 1)
                pool.memset(e["ends"]["dst"][:, :], NO_NODE).then_inc(padded, 1)
                pool.memset(e["ends"]["src"][:, :], NO_NODE).then_inc(padded, 1)
                pool.memset(e["attr"][:, :], 0.0).then_inc(padded, 1)
                pool.memset(empty[:, :, 0], NO_LANE).then_inc(empty_made, 1)
                pool.memset(empty[:, :, 1], NO_ROW).then_inc(empty_made, 1)
                pool.memset(ident[:, :], 1.0).then_inc(made, 1)
                pool.memset(e["before"][:, :], 1.0).then_inc(made, 1)
                pool.memset(e["rest"][:, :], 1.0).then_inc(made, 1)
                pool.memset(ones16[:, :], 1.0)
                pool.memset(eps[:, :], EPS)
                pool.iota(iota[:, :], [[1, max(NT, P)]], base=0, channel_multiplier=0, allow_small_or_imprecise_dtypes=True)
                pool.iota(e["entry"]["dst"][:, :, 1], [[1, EC]], base=0, channel_multiplier=EC)
                pool.iota(e["lane"][:, :], [[P, 2]], base=0, channel_multiplier=1, allow_small_or_imprecise_dtypes=True)
                pool.wait_ge(made, 3)
                pool.affine_select(out=ident[:, :], in_=ident[:, :], compare_op=ALU.is_equal, fill=0.0,
                                   base=0, pattern=[[-1, P]], channel_multiplier=1)
                pool.affine_select(out=e["before"][:, :], in_=e["before"][:, :], compare_op=ALU.is_gt, fill=0.0,
                                   base=0, pattern=[[1, P]], channel_multiplier=-1)
                pool.affine_select(out=e["rest"][:, :], in_=e["rest"][:, :], compare_op=ALU.is_ge, fill=0.0,
                                   base=0, pattern=[[-1, P]], channel_multiplier=1)

            @block.vector
            def _(dve):
                for n in names:
                    dve.memset(bias3[n][:, :], 0.0).then_inc(split, 1)
                dve.wait_ge(ends_in, 96)
                for side in ("dst", "src"):
                    ends = e["ends"][side]
                    dve.tensor_scalar(high[side][:, :], ends[:, :], 8, None, ALU.logical_shift_right).then_inc(numbered, 1)
                    dve.tensor_scalar(bit[side][:, :], ends[:, :], 1, None, ALU.bitwise_and).then_inc(numbered, 1)
                    dve.tensor_scalar(e["entry"][side][:, :, 0], ends[:, :], 1, P - 1, ALU.logical_shift_right,
                                      ALU.bitwise_and).then_inc(ended, 1)
                dve.tensor_scalar(e["xrow"][:, :], e["ends"]["src"][:, :], NO_ROW, None, ALU.min)
                dve.tensor_scalar(e["entry"]["src"][:, :, 1], e["ends"]["dst"][:, :], float(P * EC), None, ALU.add)
                dve.wait_ge(numbered, 4)
                for side in ("dst", "src"):
                    dve.scalar_tensor_tensor(out=e["tile"][side][:, :], in0=high[side][:, :], scalar=2.0,
                                             in1=bit[side][:, :], op0=ALU.mult, op1=ALU.add)
                dve.wait_ge(biases_in, 16 * len(names))
                dve.wait_ge(weights_in, 16 * len(sets))
                for of, n in centred + centred_biases:
                    dve.bn_stats(sums[n][:, :], of).then_inc(summed, 1)
                dve.wait_ge(summed, len(centred + centred_biases))
                for _, n in centred + centred_biases:
                    dve.bn_aggr(means[n][:, :], sums[n][:, :]).then_inc(averaged, 1)
                dve.wait_ge(averaged, len(centred + centred_biases))
                for of, n in centred + centred_biases:
                    dve.tensor_scalar(of, of, means[n][:, 0:1], None, ALU.subtract).then_inc(taken_off, 1)
                dve.wait_ge(taken_off, len(centred + centred_biases))
                dve.wait_ge(split, len(names))
                for n in names:
                    dve.tensor_copy(part[n][:, :], raw[n][:, :]).then_inc(split, 1)
                dve.wait_ge(split, 2 * len(names))
                for n in names:
                    dve.tensor_tensor(left[n][:, :], raw[n][:, :], part[n][:, :], ALU.subtract).then_inc(split, 1)
                dve.wait_ge(split, 3 * len(names))
                for n in names:
                    dve.tensor_copy(part2[n][:, :], left[n][:, :]).then_inc(split, 1)
                dve.wait_ge(split, 4 * len(names))
                for n in names:
                    dve.tensor_tensor(raw[n][:, :], left[n][:, :], part2[n][:, :], ALU.subtract).then_inc(split, 1)
                dve.wait_ge(split, 5 * len(names))
                for n in names:
                    for lane, of in ((0, part), (32, part2), (64, raw)):
                        dve.tensor_copy(bias3[n][lane:lane + 1, :], of[n][lane:lane + 1, :])
                dve.wait_ge(attr_in, 48)
                pol = e["attr"][:, :].rearrange("p (c f) -> p c f", f=17)[:, :, 0]
                dve.tensor_scalar(e["gate"][:, :], pol, 0.0, 1.0, ALU.max, ALU.min).then_inc(split, 1)
                dve.wait_ge(split, 5 * len(names) + 1)
                dve.tensor_scalar(e["gate"][:, :], e["gate"][:, :], 0.01, None, ALU.add)


def read_slots(nc, dims, e, side, counted, crowd, slots, lane_of, row_of):
    EC, NT = dims["EC"], dims["NT"]
    own = Phase(nc)
    with own:
        def sb(name, shape, dt):
            return own.enter_context(nc.sbuf_tensor(f"{name}_{side}", shape, dt))
        both = sb("both", [P, NT, 2], I32)
        over = sb("over", [P, NT], F32)
        running = sb("running", [P, NT], F32)
        below = [sb(f"below{g}", [P, NT], F32) for g in range(2)]
        nth = sb("nth", [P, 2], F32)
        nth_i = sb("nth_i", [P, 2], I32)
        slots_in = own.sem(f"slots_in_{side}")
        listed = own.sem(f"listed_{side}")
        list_out = own.sem(f"list_out_{side}")

        with nc.Block() as block:
            @block.sync
            def _(sp):
                sp.dma_start(both[:, :, :].rearrange("p t w -> p (t w)"),
                             slots.rearrange("(p t) w -> p (t w)", t=NT)).then_inc(slots_in, 16)
                sp.wait_ge(listed, 5)
                sp.dma_start(crowd["tiles"][side].rearrange("(g p) w -> p (g w)", p=P), nth_i[:, :],
                             allow_slow_non_contiguous=True).then_inc(list_out, 16)
                sp.wait_ge(list_out, 16)

            @block.vector
            def _(dve):
                dve.tensor_scalar(over[:, :], counted[:, 0:NT], float(P), None, ALU.is_gt).then_inc(listed, 1)
                dve.wait_ge(listed, 1)
                dve.tensor_tensor_scan(running[:, :], over[:, :], over[:, :], 0.0, ALU.add,
                                       ALU.bypass).then_inc(listed, 1)
                dve.wait_ge(listed, 2)
                dve.tensor_copy(crowd["count"][side][:, :], running[:, NT - 1:NT])
                for g in range(2):
                    dve.tensor_scalar(below[g][:, :], running[:, :], crowd["lane"][:, g:g + 1], 0.0, ALU.is_le,
                                      ALU.add, accum_out=nth[:, g:g + 1]).then_inc(listed, 1)
                dve.wait_ge(listed, 4)
                dve.tensor_copy(nth_i[:, :], nth[:, :]).then_inc(listed, 1)
                dve.scalar_tensor_tensor(out=crowd["key"][side][:, :], in0=e["tile"][side][:, :], scalar=float(P),
                                         in1=e["entry"][side][:, :, 0], op0=ALU.mult, op1=ALU.add)
                dve.wait_ge(slots_in, 16)
                dve.tensor_copy(lane_of[:, :], both[:, :, 0])
                dve.tensor_copy(row_of[:, :], both[:, :, 1])


def messages(nc, dims, e, iota, ident, eps, slots, x, msg_rows, banks, counted):
    N, EC, NT = dims["N"], dims["EC"], dims["NT"]
    G = 4
    U = 6
    K = EC // G
    own = Phase(nc)
    with own:
        def sb(name, shape, dt):
            return own.enter_context(nc.sbuf_tensor(name, shape, dt))

        def sem(name):
            return own.sem(name)
        PADDED = G * 17 + P
        hot = [[sb(f"hot_dst{n}_{u}", [P, NT], BF16) for u in range(G)] for n in range(2)]
        rank = sb("rank_dst", [P, EC], F32)
        picked = [sb(f"picked_dst{n}", [P, NT], BF16) for n in range(2)]
        place_now = [sb(f"place_now_dst{n}", [P, G], I32) for n in range(2)]
        entry_now = [sb(f"entry_now_dst{n}", [P, G * 2], I32) for n in range(2)]
        attr_now = [sb(f"attr_now{n}", [P, PADDED], F32) for n in range(2)]
        row_now = [sb(f"row_now{n}", [P, G], I32) for n in range(6)]
        xg = [sb(f"xg{n}", [P, G, D], F32) for n in range(6)]
        raw_t = [sb(f"raw_t{n}", [RAW, G * P], F32) for n in range(2)]
        e1_t = [sb(f"e1_t{n}", [P, G * P], F32) for n in range(2)]
        e2_t = [sb(f"e2_t{n}", [P, G * P], F32) for n in range(2)]
        anchor = sb("e_anchor", [P, 1], F32)
        tick = sb("e_tick", [P, 3], F32)
        ticked = sem("ticked")
        stats = [sb(f"e_stats{n}", [P, G, 6], F32) for n in range(2)]
        mv = [sb(f"e_mv{n}", [P, G, 2], F32) for n in range(2)]
        std = [sb(f"e_std{n}", [P, G], F32) for n in range(2)]
        rstd = [sb(f"e_rstd{n}", [P, G], F32) for n in range(2)]
        nmr = [sb(f"e_nmr{n}", [P, G], F32) for n in range(2)]
        hs = [sb(f"hs{n}", [P, G, D], F32) for n in range(3)]
        emb = [sb(f"emb{n}", [P, G, D], F32) for n in range(3)]
        msg = [sb(f"msg{n}", [P, G, D], F32) for n in range(2)]
        raw_ps, e1_ps, e2_ps = banks[0:3]
        emb_ps = [banks[3:5], banks[5:7]]

        zero = sb("zero_dst", [P, NT], BF16)
        zeroed = sem("zeroed_dst")
        hot_made = sem("hot_made_dst")
        added = sem("added_dst")
        ranked = sem("ranked_dst")
        totalled = sem("totalled_dst")
        placed = sem("placed_dst")
        entries_copied = sem("entries_copied")
        scattered = [sem(f"scattered_dst{n}") for n in range(2)]
        cleared = sem("cleared")
        xg_cleared = sem("xg_cleared")
        attr_copied = sem("attr_copied")
        rows_copied = sem("rows_copied")
        gathered = [sem(f"x_gathered{n}") for n in range(6)]
        turned = sem("turned")
        raw_ready = sem("raw_ready")
        e1_done = sem("e1_done")
        e1_ready = sem("e1_ready")
        e2_done = sem("e2_done")
        e2_ready = sem("e2_ready")
        emb_done = sem("emb_done")
        stats_done = sem("e_stats_done")
        mv_done = sem("e_mv_done")
        std_done = sem("e_std_done")
        rstd_done = sem("e_rstd_done")
        nmr_done = sem("e_nmr_done")
        hs_ready = sem("hs_ready")
        emb_scaled = sem("emb_scaled")
        summed = sem("summed")
        msg_ready = sem("msg_ready")
        stored = [sem(f"msg_stored{n}") for n in range(2)]
        with nc.Block() as block:
            @block.gpsimd
            def _(pool):
                pool.memset(tick[:, :], 0.0).then_inc(ticked, 1)
                pool.wait_ge(ticked, 1)
                for b in attr_now:
                    pool.memset(b[:, :], 0.0).then_inc(cleared, 1)

                def copy_entries(i, c):
                    k = U * i + c
                    wait(pool, scattered[c % 2], 16 * G * (3 * i + c // 2))
                    pool.tensor_copy(entry_now[c % 2][:, :],
                                     e["entry"]["dst"][:, bass.ds(G * k, G), :].rearrange("p c w -> p (c w)")).then_inc(entries_copied, 1)

                def scatter(i, c):
                    k = U * i + c
                    pool.wait_ge(placed, k + 1)
                    pool.wait_ge(entries_copied, k + 1)
                    anchor_on_pool(pool, tick, 1)
                    for u in range(G):
                        pool.indirect_dma_start(
                            out=slots, out_offset=bass.IndirectOffsetOnAxis(ap=place_now[c % 2][:, u:u + 1], axis=0),
                            in_=entry_now[c % 2][:, 2 * u:2 * u + 2], in_offset=None,
                            bounds_check=P * NT - 1, oob_is_err=False).then_inc(scattered[c % 2], 16)

                def gather(i, c):
                    k = U * i + c
                    wait(pool, gathered[c % 6], 16 * G * (i + c // 6))
                    pool.tensor_copy(row_now[c % 6][:, :], e["xrow"][:, bass.ds(G * k, G)]).then_inc(rows_copied, 1)
                    pool.wait_ge(rows_copied, k + 1)
                    wait(pool, hs_ready, k - 5)
                    if isinstance(k, int) and k < 6:
                        pool.memset(xg[c][:, :, :], 0.0).then_inc(xg_cleared, 1)
                        pool.wait_ge(xg_cleared, k + 1)
                    anchor_on_pool(pool, tick)
                    for u in range(G):
                        pool.indirect_dma_start(
                            out=xg[c % 6][:, u, :], out_offset=None, in_=x,
                            in_offset=bass.IndirectOffsetOnAxis(ap=row_now[c % 6][:, u:u + 1], axis=0),
                            bounds_check=N - 1, oob_is_err=False).then_inc(gathered[c % 6], 16)

                run_steps(pool, K, U, [(2, copy_entries), (0, gather), (2, scatter)])
                for n in range(2):
                    pool.wait_ge(scattered[n], 16 * G * ((K + 1 - n) // 2))

            @block.tensor
            def _(pe):
                def turn(i, c):
                    k = U * i + c
                    pe.wait_ge(attr_copied, k + 1)
                    wait(pe, raw_ready, k)
                    for u in range(G):
                        last = pe.matmul(raw_ps[:, u * P:(u + 1) * P], attr_now[c % 2][:, 17 * u + 1:17 * u + 1 + P],
                                         ident[:, :], is_transpose=True, start=True, stop=True)
                    last.then_inc(turned, 1)

                def first(i, c):
                    k = U * i + c
                    pe.wait_ge(raw_ready, k + 1)
                    wait(pe, e1_ready, k)
                    pe.matmul(e1_ps[:, :], e["ew1"][:, :], raw_t[c % 2][:, :], start=True, stop=True).then_inc(e1_done, 1)

                def second(i, c):
                    k = U * i + c
                    pe.wait_ge(e1_ready, k + 1)
                    wait(pe, e2_ready, k)
                    pe.matmul(e2_ps[:, :], e["ew2"][:, :], e1_t[c % 2][:, :], start=True, stop=True).then_inc(e2_done, 1)

                def embed(i, c):
                    k = U * i + c
                    pe.wait_ge(e2_ready, k + 1)
                    wait(pe, emb_scaled, k - 1)
                    for u in range(G):
                        last = pe.matmul(emb_ps[c % 2][u // 2][:, u % 2 * D:(u % 2 + 1) * D], e2_t[c % 2][:, u * P:(u + 1) * P],
                                         e["lew"][:, :], start=True, stop=True)
                    last.then_inc(emb_done, 1)

                def count_earlier_lanes(u):
                    def body(i, c):
                        n = G * (U * i + c) + u
                        pe.wait_ge(hot_made, U * i + c + 1)
                        pe.matmul(counted[:, 0:NT], e["before"][:, :], hot[c % 2][u][:, :], start=False,
                                  stop=True, skip_group_check=True).then_inc(added, 1)
                    return body

                def count_the_rest(u):
                    def body(i, c):
                        n = G * (U * i + c) + u
                        pe.wait_ge(ranked, n + 1)
                        pe.matmul(counted[:, 0:NT], e["rest"][:, :], hot[c % 2][u][:, :], start=False,
                                  stop=True, skip_group_check=True).then_inc(totalled, 1)
                    return body

                pe.wait_ge(zeroed, 1)
                pe.matmul(counted[:, 0:NT], e["before"][:, :], zero[:, :], start=True, stop=True)
                run_steps(pe, K, U, [(1, turn), (1, count_earlier_lanes(0)), (1, count_the_rest(0)),
                                     (1, count_earlier_lanes(1)), (2, first), (1, count_the_rest(1)),
                                     (1, count_earlier_lanes(2)), (3, second), (1, count_the_rest(2)),
                                     (1, count_earlier_lanes(3)), (4, embed), (1, count_the_rest(3))])

            @block.scalar
            def _(act):
                act.wait_ge(cleared, 2)

                def copy_attr(i, c):
                    k = U * i + c
                    wait(act, turned, k - 1)
                    act.activation(attr_now[c % 2][:, 0:G * 17], e["attr"][:, bass.ds(G * 17 * k, G * 17)],
                                   ACT.Copy).then_inc(attr_copied, 1)

                def raw_out(i, c):
                    k = U * i + c
                    wait(act, e1_done, k - 1)
                    act.wait_ge(turned, k + 1)
                    act.activation(raw_t[c % 2][:, :], raw_ps[0:RAW, :], ACT.Copy).then_inc(raw_ready, 1)

                def e1_out(i, c):
                    k = U * i + c
                    wait(act, e2_done, k - 1)
                    act.wait_ge(e1_done, k + 1)
                    act.activation(e1_t[c % 2][:, :], e1_ps[:, :], ACT.Relu, bias=e["eb1"][:, 0:1]).then_inc(e1_ready, 1)

                def e2_out(i, c):
                    k = U * i + c
                    wait(act, emb_done, k - 1)
                    act.wait_ge(e2_done, k + 1)
                    act.activation(e2_t[c % 2][:, :], e2_ps[:, :], ACT.Identity, bias=e["eb2"][:, 0:1]).then_inc(e2_ready, 1)

                def root(i, c):
                    k = U * i + c
                    wait(act, rstd_done, k - 1)
                    act.wait_ge(mv_done, k + 1)
                    act.activation(std[c % 2][:, :], mv[c % 2][:, :, 1], ACT.Sqrt, bias=eps[:, 0:1]).then_inc(std_done, 1)

                def normalise(i, c):
                    k = U * i + c
                    wait(act, summed, k - 2)
                    act.wait_ge(nmr_done, k + 1)
                    for u in range(G):
                        last = act.activation(hs[c % 3][:, u, :], xg[c % 6][:, u, :], ACT.Relu,
                                              bias=nmr[c % 2][:, u:u + 1], scale=rstd[c % 2][:, u:u + 1])
                    last.then_inc(hs_ready, 1)

                def message(i, c):
                    k = U * i + c
                    wait(act, stored[c % 2], 16 * (3 * i + c // 2))
                    act.wait_ge(summed, k + 1)
                    act.activation(msg[c % 2][:, :, :], emb[c % 3][:, :, :], ACT.Relu).then_inc(msg_ready, 1)

                run_steps(act, K, U, [(3, root), (1, raw_out), (4, normalise), (2, e1_out), (7, message), (3, e2_out), (0, copy_attr)])

            @block.vector
            def _(dve):
                dve.memset(zero[:, :], 0.0).then_inc(zeroed, 1)

                def one_hot(i, c):
                    k = U * i + c
                    wait(dve, totalled, G * (k - 1))
                    for u in range(G):
                        last = dve.tensor_scalar(hot[c % 2][u][:, :], iota[:, 0:NT], e["tile"]["dst"][:, bass.ds(G * k + u, 1)],
                                                 None, ALU.is_equal)
                    last.then_inc(hot_made, 1)

                def read_rank(u):
                    def body(i, c):
                        n = G * (U * i + c) + u
                        dve.wait_ge(added, n + 1)
                        wait(dve, ranked, n - 1)
                        dve.scalar_tensor_tensor(out=picked[u % 2][:, :], in0=iota[:, 0:NT],
                                                 scalar=e["tile"]["dst"][:, bass.ds(n, 1)], in1=counted[:, 0:NT],
                                                 op0=ALU.is_equal, op1=ALU.mult,
                                                 accum_out=rank[:, bass.ds(n, 1)]).then_inc(ranked, 1)
                    return body

                def place(i, c):
                    k = U * i + c
                    wait(dve, scattered[c % 2], 16 * G * (3 * i + c // 2))
                    dve.wait_ge(ranked, G * (k + 1))
                    dve.scalar_tensor_tensor(out=place_now[c % 2][:, :], in0=rank[:, bass.ds(G * k, G)], scalar=float(NT),
                                             in1=e["tile"]["dst"][:, bass.ds(G * k, G)],
                                             op0=ALU.mult, op1=ALU.add).then_inc(placed, 1)

                def take_stats(i, c):
                    k = U * i + c
                    wait(dve, mv_done, k - 1)
                    dve.wait_ge(gathered[c % 6], 16 * G * (i + c // 6 + 1))
                    for u in range(G):
                        last = dve.bn_stats(stats[c % 2][:, u, :], xg[c % 6][:, u, :])
                    last.then_inc(stats_done, 1)

                def add(i, c):
                    k = U * i + c
                    dve.wait_ge(emb_scaled, k + 1)
                    dve.wait_ge(hs_ready, k + 1)
                    dve.tensor_tensor(emb[c % 3][:, :, :], emb[c % 3][:, :, :], hs[c % 3][:, :, :], ALU.add).then_inc(summed, 1)

                def aggregate(i, c):
                    k = U * i + c
                    wait(dve, nmr_done, k - 1)
                    dve.wait_ge(stats_done, k + 1)
                    dve.tensor_copy(anchor[:, :], eps[:, :])
                    for u in range(G):
                        last = dve.bn_aggr(mv[c % 2][:, u, :], stats[c % 2][:, u, :])
                    last.then_inc(mv_done, 1)

                def scale(i, c):
                    k = U * i + c
                    wait(dve, msg_ready, k - 2)
                    dve.wait_ge(emb_done, k + 1)
                    for u in range(G):
                        last = dve.scalar_tensor_tensor(out=emb[c % 3][:, u, :], in0=emb_ps[c % 2][u // 2][:, u % 2 * D:(u % 2 + 1) * D],
                                                        scalar=e["gate"][:, bass.ds(G * k + u, 1)], in1=e["leb"][:, :],
                                                        op0=ALU.mult, op1=ALU.add)
                    last.then_inc(emb_scaled, 1)

                def invert(i, c):
                    k = U * i + c
                    wait(dve, hs_ready, k - 1)
                    dve.wait_ge(std_done, k + 1)
                    dve.reciprocal(rstd[c % 2][:, :], std[c % 2][:, :]).then_inc(rstd_done, 1)

                def factors(i, c):
                    k = U * i + c
                    wait(dve, hs_ready, k - 1)
                    dve.wait_ge(rstd_done, k + 1)
                    dve.scalar_tensor_tensor(out=nmr[c % 2][:, :], in0=mv[c % 2][:, :, 0], scalar=-1.0,
                                             in1=rstd[c % 2][:, :], op0=ALU.mult, op1=ALU.mult).then_inc(nmr_done, 1)

                run_steps(dve, K, U, [(1, read_rank(0)), (5, scale), (1, read_rank(1)), (6, add), (1, read_rank(2)),
                                      (2, take_stats), (3, invert), (1, read_rank(3)), (0, one_hot), (3, factors),
                                      (2, aggregate), (1, place)])

            @block.sync
            def _(sp):
                rows = msg_rows[0:P * EC, :].rearrange("(p c) d -> p (c d)", c=EC)

                def store(i, c):
                    k = U * i + c
                    sp.wait_ge(msg_ready, k + 1)
                    sp.dma_start(rows[:, bass.ds(G * D * k, G * D)],
                                 msg[c % 2][:, :, :].rearrange("p g d -> p (g d)")).then_inc(stored[c % 2], 16)

                run_steps(sp, K, U, [(0, store)])
                sp.wait_ge(stored[0], 16 * ((K + 1) // 2))
                sp.wait_ge(stored[1], 16 * (K // 2))


def name_rows_of_y(nc, first, N, row_of):
    own = Phase(nc)
    with own:
        later = own.enter_context(nc.sbuf_tensor("later", list(row_of.shape), F32))
        compared = own.sem("compared")
        with nc.Block() as block:
            @block.vector
            def _(dve):
                dve.tensor_scalar(later[:, :], row_of[:, :], float(first), float(N), ALU.is_ge, ALU.mult).then_inc(compared, 1)
                dve.wait_ge(compared, 1)
                dve.tensor_tensor(row_of[:, :], row_of[:, :], later[:, :], ALU.add)


def crowded_tiles(nc, name, side, EC, crowd, iota, lane_of, row_of, table, shift, banks):
    own = Phase(nc)
    mean = name != "A"
    with own:
        def sb(n, shape, dt=F32):
            return own.enter_context(nc.sbuf_tensor(f"crowd{name}_{n}", shape, dt))

        def sem(n):
            return own.sem(f"crowd{name}_{n}")
        tile_i = sb("tile_i", [P, 1], I32)
        shift_i = sb("shift_i", [P, 1], I32)
        offset = sb("offset", [P, 1])
        place = sb("place", [P, 1])
        column = sb("column", [P, 1])
        anchor = sb("anchor", [P, 1])
        row_now = sb("row_now", [P, 1], I32)
        target = sb("target", [P, 1], I32)
        rows = sb("rows", [P, D])
        hot = sb("hot", [P, P])
        total = sb("total", [P, D])
        degree = sb("degree", [P, 2])
        ones = sb("ones", [P, 1])
        tick = sb("tick", [P, 2])
        sum_ps, deg_ps = banks[0], banks[1]
        ticked = sem("ticked")
        tile_free = sem("tile_free")
        tile_in = sem("tile_in")
        offset_ready = sem("offset_ready")
        column_ready = sem("column_ready")
        hot_made = sem("hot_made")
        row_copied = sem("row_copied")
        gathered = sem("gathered")
        product_done = sem("product_done")
        emptied = sem("emptied")
        added = sem("added")
        counted = sem("counted")
        ratio_ready = sem("ratio_ready")
        placed = sem("placed")
        target_copied = sem("target_copied")
        result_ready = sem("result_ready")
        result_out = sem("result_out")
        tiles = crowd["tiles"][side]
        most = crowd["most"]
        last_tile = lane_of[side].shape[1] - 1

        with nc.Block() as block:
            @block.scalar
            def _(act):
                count = act.value_load(crowd["count"][side][0:1, 0:1], min_val=0, max_val=most)
                with act.If(count > 0):
                    with act.Fori(0, count) as j:
                        act.wait_ge(tile_free, j + 1)
                        act.dma_start(tile_i[:, :], tiles[bass.ds(j, 1), :].partition_broadcast(P)
                                     .rearrange("p a b -> p (a b)")).then_inc(tile_in, 16)
                        if mean:
                            act.wait_ge(result_ready, j + 1)
                            act.dma_start(table[bass.ds(j * P, P), :], total[:, :]).then_inc(result_out, 16)

            @block.gpsimd
            def _(pool):
                pool.memset(tick[:, :], 0.0).then_inc(ticked, 1)
                pool.memset(rows[:, :], 0.0).then_inc(ticked, 1)
                pool.memset(shift_i[:, :], shift).then_inc(ticked, 1)
                pool.wait_ge(ticked, 3)
                count = pool.value_load(crowd["count"][side][0:1, 0:1], min_val=0, max_val=most)
                with pool.If(count > 0):
                    with pool.Fori(0, count) as j:
                        with pool.Fori(0, EC) as c:
                            n = j * EC + c
                            pool.tensor_tensor(row_now[:, :], crowd["entry"][side][:, bass.ds(c, 1), 1], shift_i[:, :],
                                               ALU.add).then_inc(row_copied, 1)
                            pool.wait_ge(row_copied, n + 1)
                            anchor_on_pool(pool, tick)
                            pool.indirect_dma_start(
                                out=rows[:, :], out_offset=None, in_=table,
                                in_offset=bass.IndirectOffsetOnAxis(ap=row_now[:, 0:1], axis=0),
                                bounds_check=table.shape[0] - 1, oob_is_err=False).then_inc(gathered, 16)
                            pool.wait_ge(product_done, n + 1)
                        if not mean:
                            t = pool.value_load(tiles[bass.ds(j, 1), :], min_val=0, max_val=last_tile)
                            pool.tensor_copy(target[:, :], row_of[side][:, bass.ds(t, 1)]).then_inc(target_copied, 1)
                            pool.wait_ge(target_copied, j + 1)
                            pool.wait_ge(result_ready, j + 1)
                            anchor_on_pool(pool, tick)
                            pool.indirect_dma_start(
                                out=table, out_offset=bass.IndirectOffsetOnAxis(ap=target[:, 0:1], axis=0),
                                in_=total[:, :], in_offset=None,
                                bounds_check=table.shape[0] - 1, oob_is_err=False).then_inc(result_out, 16)
                            pool.wait_ge(result_out, 16 * j + 16)

            @block.tensor
            def _(pe):
                count = pe.value_load(crowd["count"][side][0:1, 0:1], min_val=0, max_val=most)
                with pe.If(count > 0):
                    with pe.Fori(0, count) as j:
                        with pe.Fori(0, EC) as c:
                            n = j * EC + c
                            pe.wait_ge(hot_made, n + 1)
                            pe.wait_ge(gathered, 16 * n + 16)
                            pe.matmul(deg_ps[:, 0:1], hot[:, :], ones[:, 0:1], start=True, stop=True)
                            pe.matmul(sum_ps[:, 0:D], hot[:, :], rows[:, :], start=True, stop=True).then_inc(product_done, 1)
                            pe.wait_ge(added, n + 1)
                            pe.wait_ge(counted, n + 1)

            @block.vector
            def _(dve):
                dve.memset(ones[:, :], 1.0).then_inc(tile_free, 1)
                dve.tensor_copy(place[:, :], crowd["lane"][:, 0:1]).then_inc(placed, 1)
                count = dve.value_load(crowd["count"][side][0:1, 0:1], min_val=0, max_val=most)
                with dve.If(count > 0):
                    with dve.Fori(0, count) as j:
                        t = dve.value_load(tiles[bass.ds(j, 1), :], min_val=0, max_val=last_tile)
                        dve.wait_ge(tile_in, 16 * j + 16)
                        dve.tensor_scalar(offset[:, :], tile_i[:, :], float(P), None, ALU.mult).then_inc(offset_ready, 1)
                        dve.memset(total[:, :], 0.0).then_inc(emptied, 1)
                        dve.memset(degree[:, :], 0.0).then_inc(emptied, 1)
                        dve.wait_ge(offset_ready, j + 1)
                        dve.wait_ge(emptied, 2 * j + 2)
                        dve.tensor_copy(anchor[:, :], offset[:, :]).then_inc(tile_free, 1)
                        with dve.Fori(0, EC) as c:
                            n = j * EC + c
                            dve.tensor_tensor(column[:, :], crowd["key"][side][:, bass.ds(c, 1)], offset[:, :],
                                              ALU.subtract).then_inc(column_ready, 1)
                            dve.wait_ge(column_ready, n + 1)
                            dve.tensor_scalar(hot[:, :], iota[:, 0:P], column[:, 0:1], None, ALU.is_equal).then_inc(hot_made, 1)
                            dve.wait_ge(product_done, n + 1)
                            dve.tensor_tensor(degree[:, 0:1], deg_ps[:, 0:1], degree[:, 0:1], ALU.add).then_inc(counted, 1)
                            dve.tensor_tensor(total[:, :], sum_ps[:, 0:D], total[:, :], ALU.add).then_inc(added, 1)
                            dve.wait_ge(added, n + 1)
                            dve.wait_ge(counted, n + 1)
                        if mean:
                            dve.tensor_scalar(degree[:, 1:2], degree[:, 0:1], 1.0, None, ALU.max).then_inc(ratio_ready, 1)
                            dve.wait_ge(ratio_ready, 3 * j + 1)
                            dve.reciprocal(degree[:, 0:1], degree[:, 1:2]).then_inc(ratio_ready, 1)
                            dve.wait_ge(ratio_ready, 3 * j + 2)
                            dve.tensor_scalar(total[:, :], total[:, :], degree[:, 0:1], None, ALU.mult).then_inc(ratio_ready, 1)
                            dve.wait_ge(ratio_ready, 3 * j + 3)
                            dve.wait_ge(placed, j + 1)
                            dve.tensor_copy(row_of[side][:, bass.ds(t, 1)], place[:, :]).then_inc(target_copied, 1)
                            dve.wait_ge(target_copied, j + 1)
                            dve.tensor_scalar(place[:, :], place[:, :], float(P), None, ALU.add).then_inc(placed, 1)
                        dve.tensor_copy(lane_of[side][:, bass.ds(t, 1)], crowd["lane"][:, 0:1]).then_inc(result_ready, 1)
                        dve.wait_ge(result_out, 16 * j + 16)


def pair_rows(table, k):
    return table[bass.ds(256 * k, 256), :].rearrange("(p j) d -> p (j d)", j=2)


def last_rows(table, k, lanes):
    return table[256 * k:256 * k + 2 * lanes, :].rearrange("(p j) d -> p (j d)", j=2)


def gated_block(nc, N, K, TAIL, iota, ident, ones16, eps, w_sb, bias3, b2_wide, lng_sb, lnb_sb, lane_of, row_of,
                x, msg_rows, x1_rows, h2_rows, banks, e, slots, counted):
    U = 8
    NT = 2 * K
    own = Phase(nc)
    with own:
        def sb(name, shape, dt=F32):
            return own.enter_context(nc.sbuf_tensor(name, shape, dt))

        def ring(name, n, shape, dt=F32):
            return [sb(f"{name}{m}", shape, dt) for m in range(n)]

        def sem(name):
            return own.sem("A_" + name)
        xb = ring("xb", 8, [P, 512])
        mb = ring("mb", 8, [P, 2, D])
        rows_now = ring("rows_now", 8, [P, 2], I32)
        hot = ring("hotA", 2, [P, 2, P])
        h = ring("h", 2, [P, 512])
        ht = ring("ht", 2, [P, 2, 2, P])
        z = ring("z", 2, [P, 512])
        r = ring("r", 2, [P, 2, 2, P])
        x1 = ring("x1b", 4, [P, 512])
        h2 = ring("h2b", 4, [P, 512])
        tick = sb("tick", [P, 2])
        GX, GH, GY = 0, 1, 2
        st = ring("st", 2, [P, 6, 6])
        mv = ring("mv", 2, [P, 6, 2])
        sd = ring("sd", 2, [P, 6])
        rs = ring("rs", 2, [P, 6])
        nm = ring("nm", 2, [P, 6])
        LX, LH, LY = 0, 3, 6
        STEPS = K + LY
        ht_ps, h1_ps, o_ps, zt_ps = banks[0:2], banks[2:4], banks[4:6], banks[6]
        hot_src = ring("hot_src", 4, [P, NT], BF16)
        picked = ring("picked_src", 2, [P, NT], BF16)
        zero = sb("zero_src", [P, 512], BF16)
        rank = sb("rank_src", [P, K])
        tile, entry = e["tile"]["src"], e["entry"]["src"]
        place_now = ring("place_nowA", 4, [P, 1], I32)
        entry_now = ring("entry_nowA", 4, [P, 2], I32)

        x_in = [sem(f"x_in{m}") for m in range(8)]
        msg_in = [sem(f"msg_in{m}") for m in range(8)]
        stored = [sem(f"stored{m}") for m in range(4)]
        scattered = [sem(f"scattered{m}") for m in range(4)]
        cleared = sem("cleared")
        rows_copied = sem("rows_copied")
        entry_copied = sem("entry_copied")
        hot_made = sem("hot_made")
        st_done = {g: sem(f"st_done{g}") for g in (GX, GH, GY)}
        mv_set = sem("mv_set")
        mv_done = sem("mv_done")
        sd_done = sem("sd_done")
        rs_done = sem("rs_done")
        nm_done = sem("nm_done")
        h_ready = sem("h_ready")
        ht_done = sem("ht_done")
        ht_ready = sem("ht_ready")
        opened = sem("opened")
        o_biased = sem("o_biased")
        h1_done = sem("h1_done")
        z_ready = sem("z_ready")
        zt_done = sem("zt_done")
        r_ready = sem("r_ready")
        o_done = sem("o_done")
        x1_ready = sem("x1_ready")
        h2_ready = sem("h2_ready")
        zeroed = sem("zeroed_src")
        hot_src_made = sem("hot_src_made")
        added = sem("added_src")
        ranked = sem("ranked_src")
        totalled = sem("totalled_src")
        placed = sem("placed")

        with nc.Block() as block:
            @block.sync
            def _(sp):
                def load(i, c):
                    k = U * i + c
                    wait(sp, x1_ready, k - 7)
                    full = not (isinstance(k, int) and k == K - 1)
                    lanes = P if full else TAIL
                    sp.dma_start(xb[c % 8][0:lanes, :], pair_rows(x, k) if full else last_rows(x, k, lanes)).then_inc(x_in[c % 8], 16)

                def store(i, c):
                    k = U * i + c
                    sp.wait_ge(h2_ready, k + 1)
                    full = not (isinstance(k, int) and k == K - 1)
                    lanes = P if full else TAIL
                    for table, b in ((x1_rows, x1), (h2_rows, h2)):
                        sp.dma_start(pair_rows(table, k) if full else last_rows(table, k, lanes),
                                     b[c % 4][0:lanes, :]).then_inc(stored[c % 4], 16)

                run_steps(sp, K, U, [(0, load), (8, store)])
                for m in range(4):
                    sp.wait_ge(stored[m], 32 * ((K - m + 3) // 4))

            @block.gpsimd
            def _(pool):
                pool.memset(tick[:, :], 0.0).then_inc(cleared, 1)
                pool.wait_ge(cleared, 1)

                def copy_rows(i, c):
                    k = U * i + c
                    wait(pool, msg_in[c % 8], 32 * (i + c // 8))
                    pool.tensor_copy(rows_now[c % 8][:, :], row_of[:, bass.ds(2 * k, 2)]).then_inc(rows_copied, 1)

                def copy_entry(i, c):
                    n = U * i + c
                    wait(pool, scattered[c % 4], 16 * (2 * i + c // 4))
                    pool.tensor_copy(entry_now[c % 4][:, :],
                                     entry[:, bass.ds(n, 1), :].rearrange("p c w -> p (c w)")).then_inc(entry_copied, 1)

                def ready(i, c):
                    pool.wait_ge(placed, U * i + c + 1)
                    pool.wait_ge(entry_copied, U * i + c + 1)

                def gather(i, c):
                    k = U * i + c
                    wait(pool, ht_done, k - 7)
                    pool.wait_ge(rows_copied, k + 1)
                    if isinstance(k, int) and k < 8:
                        pool.memset(mb[c][:, :, :], 0.0).then_inc(cleared, 1)
                        pool.wait_ge(cleared, k + 2)
                    anchor_on_pool(pool, tick)
                    for j in range(2):
                        pool.indirect_dma_start(
                            out=mb[c % 8][:, j, :], out_offset=None, in_=msg_rows,
                            in_offset=bass.IndirectOffsetOnAxis(ap=rows_now[c % 8][:, j:j + 1], axis=0),
                            bounds_check=msg_rows.shape[0] - 1, oob_is_err=False).then_inc(msg_in[c % 8], 16)

                def scatter(i, c):
                    pool.indirect_dma_start(
                        out=slots, out_offset=bass.IndirectOffsetOnAxis(ap=place_now[c % 4][:, 0:1], axis=0),
                        in_=entry_now[c % 4][:, :], in_offset=None,
                        bounds_check=P * NT - 1, oob_is_err=False).then_inc(scattered[c % 4], 16)

                run_steps(pool, K, U, [(0, copy_rows), (5, copy_entry), (5, ready), (0, gather), (5, scatter)])
                for m in range(4):
                    pool.wait_ge(scattered[m], 16 * ((K - m + 3) // 4))

            @block.tensor
            def _(pe):
                def turn_and_sum(i, c):
                    k = U * i + c
                    pe.wait_ge(h_ready, k + 1)
                    pe.wait_ge(hot_made, k + 1)
                    pe.wait_ge(msg_in[c % 8], 32 * (i + c // 8 + 1))
                    wait(pe, ht_ready, k - 1)
                    for f in range(2):
                        for j in range(2):
                            to = ht_ps[c % 2][:, (2 * f + j) * P:(2 * f + j + 1) * P]
                            pe.matmul(to, h[c % 2][:, j * D + f * P:j * D + (f + 1) * P], ident[:, :],
                                      is_transpose=True, start=True, stop=False)
                            last = pe.matmul(to, mb[c % 8][:, j, f * P:(f + 1) * P], hot[c % 2][:, j, :],
                                             start=False, stop=True)
                    last.then_inc(ht_done, 1)

                def first(i, c):
                    k = U * i + c
                    pe.wait_ge(ht_ready, k + 1)
                    wait(pe, z_ready, k - 1)
                    for j in range(2):
                        part = h1_ps[c % 2][:, j * D:(j + 1) * D]
                        pe.matmul(part, ones16[:, :], bias3["b1"][:, :], start=True, stop=False)
                        for f in range(2):
                            last = pe.matmul(part, ht[c % 2][:, f, j, :], w_sb["w1"][:, f, :], start=False, stop=(f == 1))
                    last.then_inc(h1_done, 1)

                def turn(i, c):
                    k = U * i + c
                    pe.wait_ge(z_ready, k + 1)
                    wait(pe, r_ready, k)
                    for f in range(2):
                        for j in range(2):
                            last = pe.matmul(zt_ps[:, (2 * f + j) * P:(2 * f + j + 1) * P],
                                             z[c % 2][:, j * D + f * P:j * D + (f + 1) * P], ident[:, :],
                                             is_transpose=True, start=True, stop=True)
                    last.then_inc(zt_done, 1)

                def second(i, c):
                    k = U * i + c
                    pe.wait_ge(r_ready, k + 1)
                    pe.wait_ge(o_biased, k + 1)
                    for j in range(2):
                        for f in range(2):
                            last = pe.matmul(o_ps[c % 2][:, j * D:(j + 1) * D], r[c % 2][:, f, j, :], w_sb["w2"][:, f, :],
                                             start=False, stop=True, skip_group_check=True)
                    last.then_inc(o_done, 1)

                def count_earlier_lanes(i, c):
                    n = U * i + c
                    pe.wait_ge(hot_src_made, n + 1)
                    pe.matmul(counted[:, 0:NT], e["before"][:, :], hot_src[c % 4][:, :], start=False,
                              stop=True, skip_group_check=True).then_inc(added, 1)

                def count_the_rest(i, c):
                    n = U * i + c
                    pe.wait_ge(ranked, n + 1)
                    pe.matmul(counted[:, 0:NT], e["rest"][:, :], hot_src[c % 4][:, :], start=False,
                              stop=True, skip_group_check=True).then_inc(totalled, 1)

                pe.wait_ge(zeroed, 1)
                pe.matmul(counted[:, 0:NT], e["before"][:, :], zero[:, 0:NT], start=True, stop=True)
                for b in o_ps:
                    last = pe.matmul(b[:, :], ones16[:, :], zero[:, :], start=True, stop=True)
                last.then_inc(opened, 1)
                run_steps(pe, K, U, [(2, count_the_rest), (1, count_earlier_lanes), (2, turn_and_sum), (5, second), (4, turn), (2, first)])

            @block.scalar
            def _(act):
                def root(i, c):
                    s = U * i + c
                    wait(act, rs_done, s - 1)
                    act.wait_ge(mv_done, s + 1)
                    act.activation(sd[c % 2][:, :], mv[c % 2][:, :, 1], ACT.Sqrt, bias=eps[:, 0:1]).then_inc(sd_done, 1)

                def normalise(i, c, group, lag, func, to, of, done):
                    s = c + lag
                    act.wait_ge(nm_done, U * i + s + 1)
                    for j in range(2):
                        m = 2 * group + j
                        last = act.activation(to[:, j * D:(j + 1) * D], of[:, j * D:(j + 1) * D], func,
                                              bias=nm[s % 2][:, m:m + 1], scale=rs[s % 2][:, m:m + 1])
                    last.then_inc(done, 1)

                def h_out(i, c):
                    wait(act, ht_done, U * i + c - 1)
                    normalise(i, c, GX, LX, ACT.Relu, h[c % 2], xb[c % 8], h_ready)

                def ht_out(i, c):
                    k = U * i + c
                    wait(act, h1_done, k - 1)
                    act.wait_ge(ht_done, k + 1)
                    act.activation(ht[c % 2][:, :, :, :].rearrange("p f j n -> p (f j n)"), ht_ps[c % 2][:, :],
                                   ACT.Copy).then_inc(ht_ready, 1)

                def z_out(i, c):
                    wait(act, zt_done, U * i + c - 1)
                    normalise(i, c, GH, LH, ACT.Identity, z[c % 2], h1_ps[c % 2], z_ready)

                def r_out(i, c):
                    k = U * i + c
                    wait(act, o_done, k - 1)
                    act.wait_ge(zt_done, k + 1)
                    for f in range(2):
                        last = act.activation(r[c % 2][:, f, :, :].rearrange("p j n -> p (j n)"),
                                              zt_ps[:, f * D:(f + 1) * D], ACT.Relu,
                                              bias=lnb_sb[:, f:f + 1], scale=lng_sb[:, f:f + 1])
                    last.then_inc(r_ready, 1)

                def h2_out(i, c):
                    wait(act, stored[c % 4], 32 * (2 * i + c // 4))
                    normalise(i, c, GY, LY, ACT.Relu, h2[c % 4], x1[c % 4], h2_ready)

                def put_b2(i, c):
                    wait(act, x1_ready, U * i + c - 1)
                    act.activation(o_ps[c % 2][:, :], b2_wide[:, :], ACT.Copy).then_inc(o_biased, 1)

                act.wait_ge(opened, 1)
                run_steps(act, K, U, [(4, z_out), (1, h_out), (2, ht_out), (7, h2_out), (4, put_b2), (4, r_out), (0, root, STEPS)])

            @block.vector
            def _(dve):
                dve.memset(zero[:, :], 0.0).then_inc(zeroed, 1)
                for m in range(2):
                    dve.memset(mv[m][:, :, :], 1.0).then_inc(mv_set, 1)
                dve.wait_ge(mv_set, 2)

                def take_stats(i, c, group, lag, of):
                    for j in range(2):
                        last = dve.bn_stats(st[(c + lag) % 2][:, 2 * group + j, :], of[:, j * D:(j + 1) * D])
                    last.then_inc(st_done[group], 1)

                def stats_x(i, c):
                    dve.wait_ge(x_in[c % 8], 16 * (i + c // 8 + 1))
                    take_stats(i, c, GX, LX, xb[c % 8])

                def stats_h(i, c):
                    wait(dve, mv_done, U * i + c + LH - 1)
                    dve.wait_ge(h1_done, U * i + c + 1)
                    take_stats(i, c, GH, LH, h1_ps[c % 2])

                def stats_y(i, c):
                    dve.wait_ge(x1_ready, U * i + c + 1)
                    take_stats(i, c, GY, LY, x1[c % 4])

                def one_hot(i, c):
                    k = U * i + c
                    wait(dve, ht_done, k - 1)
                    for j in range(2):
                        if j == 1:
                            if isinstance(k, int):
                                for group, lag in ((GX, LX), (GH, LH), (GY, LY)):
                                    wait(dve, st_done[group], min(k + 1 - lag + 1, K))
                            else:
                                dve.wait_ge(st_done[GY], k + 1 - LY + 1)
                            wait(dve, nm_done, k + 1 - 1)
                        last = dve.tensor_scalar(hot[c % 2][:, j, :], iota[:, 0:P], lane_of[:, bass.ds(2 * k + j, 1)], None,
                                                 ALU.is_equal)
                    last.then_inc(hot_made, 1)

                def aggregate(i, c):
                    s = U * i + c
                    groups = [(g, lag) for g, lag in ((GX, LX), (GH, LH), (GY, LY))
                              if not isinstance(s, int) or 0 <= s - lag < K]
                    if isinstance(s, int):
                        for g, lag in groups:
                            dve.wait_ge(st_done[g], s - lag + 1)
                        wait(dve, nm_done, s - 1)
                    for g, _ in groups:
                        for j in range(2):
                            last = dve.bn_aggr(mv[c % 2][:, 2 * g + j, :], st[c % 2][:, 2 * g + j, :])
                    last.then_inc(mv_done, 1)

                def factors(i, c):
                    s = U * i + c
                    if isinstance(s, int):
                        for done, lag in ((h_ready, LX), (z_ready, LH), (h2_ready, LY)):
                            wait(dve, done, min(s - 1 - lag, K))
                    else:
                        dve.wait_ge(h2_ready, s - 1 - LY)
                        dve.wait_ge(h_ready, s - 1 - LX)
                        dve.wait_ge(z_ready, s - 1 - LH)
                    dve.wait_ge(sd_done, s + 1)
                    dve.reciprocal(rs[c % 2][:, :], sd[c % 2][:, :]).then_inc(rs_done, 1)
                    dve.wait_ge(rs_done, s + 1)
                    dve.scalar_tensor_tensor(out=nm[c % 2][:, :], in0=mv[c % 2][:, :, 0], scalar=-1.0,
                                             in1=rs[c % 2][:, :], op0=ALU.mult, op1=ALU.mult).then_inc(nm_done, 1)

                def residual(i, c):
                    k = U * i + c
                    wait(dve, stored[c % 4], 32 * (2 * i + c // 4))
                    wait(dve, h2_ready, k - 3)
                    dve.wait_ge(o_done, k + 1)
                    dve.tensor_tensor(x1[c % 4][:, :], o_ps[c % 2][:, :], xb[c % 8][:, :], ALU.add).then_inc(x1_ready, 1)

                def hot_chunk(i, c):
                    n = U * i + c
                    wait(dve, totalled, n - 3)
                    dve.tensor_scalar(hot_src[c % 4][:, :], iota[:, 0:NT], tile[:, bass.ds(n, 1)], None,
                                      ALU.is_equal).then_inc(hot_src_made, 1)

                def read_rank(i, c):
                    n = U * i + c
                    dve.wait_ge(added, n + 1)
                    wait(dve, ranked, n - 1)
                    dve.scalar_tensor_tensor(out=picked[c % 2][:, :], in0=iota[:, 0:NT], scalar=tile[:, bass.ds(n, 1)],
                                             in1=counted[:, 0:NT], op0=ALU.is_equal, op1=ALU.mult,
                                             accum_out=rank[:, bass.ds(n, 1)]).then_inc(ranked, 1)

                def place(i, c):
                    n = U * i + c
                    wait(dve, scattered[c % 4], 16 * (2 * i + c // 4))
                    dve.wait_ge(ranked, n + 1)
                    dve.scalar_tensor_tensor(out=place_now[c % 4][:, :], in0=rank[:, bass.ds(n, 1)],
                                             scalar=float(NT), in1=tile[:, bass.ds(n, 1)],
                                             op0=ALU.mult, op1=ALU.add).then_inc(placed, 1)

                run_steps(dve, K, U, [(LH, stats_h), (6, residual), (1, read_rank), (LX, stats_x), (LY, stats_y),
                                      (0, hot_chunk), (1, one_hot), (0, aggregate, STEPS), (1, place), (0, factors, STEPS)])


def mean_block(nc, name, N, K, TAIL, iota, ident, ones16, eps, w, bias, g_wide, b_wide, lane_of, row_of, rdeg,
               own_rows, table, residual_rows, result, banks):
    U = 6
    last_layer = residual_rows is not None
    own = Phase(nc)
    with own:
        def sb(n, shape, dt=F32):
            return own.enter_context(nc.sbuf_tensor(f"{name}_{n}", shape, dt))

        def ring(n, count, shape, dt=F32):
            return [sb(f"{n}{m}", shape, dt) for m in range(count)]

        def sem(n):
            return own.sem(f"{name}_{n}")
        hb = ring("hb", 6, [P, 512])
        nb = ring("nb", 6, [P, 2, D])
        rows_now = ring("rows_now", 6, [P, 2], I32)
        hot = ring("hot", 2, [P, 2, P])
        hm = ring("hm", 2, [P, 512])
        ht = ring("ht", 2, [P, 2, 2, P])
        tick = sb("tick", [P, 2])
        squares = ring("squares", 2, [P, 512])
        ss = ring("ss", 2, [P, 6])
        sd = ring("sd", 2, [P, 6])
        rs = ring("rs", 2, [P, 6])
        u = ring("u", 6, [P, 512])
        v = ring("v", 2, [P, 512])
        y = ring("y", 6, [P, 512])
        dg = ring("dg", 2, [P, 2])
        if last_layer:
            xb = ring("xb", 6, [P, 512])
            res = ring("res", 6, [P, 512])
        agg_ps, ht_ps, z_ps, deg_ps = banks[0:2], banks[2:4], banks[4:6], banks[6:8]

        h_in = [sem(f"h_in{m}") for m in range(6)]
        nb_in = [sem(f"nb_in{m}") for m in range(6)]
        stored = [sem(f"stored{m}") for m in range(6)]
        cleared = sem("cleared")
        rows_copied = sem("rows_copied")
        hot_made = sem("hot_made")
        agg_done = sem("agg_done")
        deg_raised = sem("deg_raised")
        rdeg_ready = sem("rdeg_ready")
        hm_ready = sem("hm_ready")
        ht_done = sem("ht_done")
        ht_ready = sem("ht_ready")
        z_done = sem("z_done")
        ss_set = sem("ss_set")
        ss_done = sem("ss_done")
        sd_done = sem("sd_done")
        rs_done = sem("rs_done")
        u_ready = sem("u_ready")
        v_ready = sem("v_ready")
        y_ready = sem("y_ready")
        if last_layer:
            x_in = [sem(f"x_in{m}") for m in range(6)]
            res_ready = sem("res_ready")

        with nc.Block() as block:
            @block.sync
            def _(sp):
                def load(i, c):
                    k = U * i + c
                    wait(sp, hm_ready, k - 5)
                    full = not (isinstance(k, int) and k == K - 1)
                    lanes = P if full else TAIL
                    sp.dma_start(hb[c % 6][0:lanes, :], pair_rows(own_rows, k) if full else last_rows(own_rows, k, lanes)).then_inc(h_in[c % 6], 16)

                def load_residual(i, c):
                    k = U * i + c
                    wait(sp, res_ready, k - 5)
                    full = not (isinstance(k, int) and k == K - 1)
                    lanes = P if full else TAIL
                    sp.dma_start(xb[c % 6][0:lanes, :],
                                 pair_rows(residual_rows, k) if full else last_rows(residual_rows, k, lanes)).then_inc(x_in[c % 6], 16)

                def store(i, c):
                    k = U * i + c
                    full = not (isinstance(k, int) and k == K - 1)
                    lanes = P if full else TAIL
                    sp.wait_ge(res_ready if last_layer else y_ready, k + 1)
                    b = res if last_layer else y
                    sp.dma_start(pair_rows(result, k) if full else last_rows(result, k, lanes),
                                 b[c % 6][0:lanes, :]).then_inc(stored[c % 6], 16)

                if last_layer:
                    run_steps(sp, K, U, [(0, load), (9, load_residual), (15, store)])
                else:
                    run_steps(sp, K, U, [(0, load), (14, store)])
                for m in range(6):
                    sp.wait_ge(stored[m], 16 * ((K - m + 5) // 6))

            @block.gpsimd
            def _(pool):
                pool.memset(tick[:, :], 0.0).then_inc(cleared, 1)
                pool.wait_ge(cleared, 1)

                def copy_rows(i, c):
                    k = U * i + c
                    wait(pool, nb_in[c % 6], 32 * (i + c // 6))
                    pool.tensor_copy(rows_now[c % 6][:, :], row_of[:, bass.ds(2 * k, 2)]).then_inc(rows_copied, 1)

                def gather(i, c):
                    k = U * i + c
                    wait(pool, agg_done, k - 5)
                    pool.wait_ge(rows_copied, k + 1)
                    if isinstance(k, int) and k < 6:
                        pool.memset(nb[c][:, :, :], 0.0).then_inc(cleared, 1)
                        pool.wait_ge(cleared, k + 2)
                    anchor_on_pool(pool, tick)
                    for j in range(2):
                        pool.indirect_dma_start(
                            out=nb[c % 6][:, j, :], out_offset=None, in_=table,
                            in_offset=bass.IndirectOffsetOnAxis(ap=rows_now[c % 6][:, j:j + 1], axis=0),
                            bounds_check=table.shape[0] - 1, oob_is_err=False).then_inc(nb_in[c % 6], 16)

                run_steps(pool, K, U, [(0, copy_rows), (0, gather)])

            @block.tensor
            def _(pe):
                def aggregate(i, c):
                    k = U * i + c
                    pe.wait_ge(hot_made, k + 1)
                    pe.wait_ge(nb_in[c % 6], 32 * (i + c // 6 + 1))
                    wait(pe, hm_ready, k - 1)
                    if not last_layer:
                        wait(pe, deg_raised, k - 1)
                        halves = hot[c % 2][:, :, :].bitcast(BF16).rearrange("p j (n w) -> p j n w", w=2)
                        for j in range(2):
                            pe.matmul(deg_ps[c % 2][:, 2 * j:2 * j + 1], halves[:, j, :, 1], ones16[:, 0:1], start=True, stop=True)
                    for j in range(2):
                        last = pe.matmul(agg_ps[c % 2][:, j * D:(j + 1) * D], hot[c % 2][:, j, :], nb[c % 6][:, j, :],
                                         start=True, stop=True)
                    last.then_inc(agg_done, 1)

                def turn(i, c):
                    k = U * i + c
                    pe.wait_ge(hm_ready, k + 1)
                    wait(pe, ht_ready, k - 1)
                    for f in range(2):
                        for j in range(2):
                            last = pe.matmul(ht_ps[c % 2][:, (2 * f + j) * P:(2 * f + j + 1) * P],
                                             hm[c % 2][:, j * D + f * P:j * D + (f + 1) * P], ident[:, :],
                                             is_transpose=True, start=True, stop=True)
                    last.then_inc(ht_done, 1)

                def layer(i, c):
                    k = U * i + c
                    pe.wait_ge(ht_ready, k + 1)
                    wait(pe, ss_done, k - 1)
                    for j in range(2):
                        part = z_ps[c % 2][:, j * D:(j + 1) * D]
                        pe.matmul(part, ones16[:, :], bias[:, :], start=True, stop=False)
                        for f in range(2):
                            last = pe.matmul(part, ht[c % 2][:, f, j, :], w[:, f, :], start=False, stop=(f == 1))
                    last.then_inc(z_done, 1)

                run_steps(pe, K, U, [(1, aggregate), (3, turn), (5, layer)])

            @block.scalar
            def _(act):
                def root(i, c):
                    k = U * i + c
                    if c % 3 != 2 and not (isinstance(k, int) and k == K - 1):
                        return
                    group = (U // 3) * i + c // 3
                    wait(act, rs_done, group - 1)
                    act.wait_ge(ss_done, k + 1)
                    act.activation(sd[c // 3 % 2][:, :], ss[c // 3 % 2][:, :], ACT.Sqrt, bias=eps[:, 0:1],
                                   scale=1.0 / D).then_inc(sd_done, 1)

                def square(i, c):
                    k = U * i + c
                    act.wait_ge(u_ready, k + 1)
                    wait(act, ss_done, k - 1)
                    wait(act, sd_done, (U // 3) * i + c // 3 - 1)
                    for j in range(2):
                        half = slice(j * D, (j + 1) * D)
                        m = 2 * (c % 3) + j
                        last = act.activation(squares[c % 2][:, half], z_ps[c % 2][:, half], ACT.Square,
                                              accum_out=ss[c // 3 % 2][:, m:m + 1])
                    last.then_inc(ss_done, 1)

                def ht_out(i, c):
                    k = U * i + c
                    wait(act, z_done, k - 1)
                    act.wait_ge(ht_done, k + 1)
                    act.activation(ht[c % 2][:, :, :, :].rearrange("p f j n -> p (f j n)"), ht_ps[c % 2][:, :],
                                   ACT.Copy).then_inc(ht_ready, 1)

                def silu(i, c):
                    k = U * i + c
                    if last_layer:
                        wait(act, res_ready, k - 5)
                    else:
                        wait(act, stored[c % 6], 16 * (i + c // 6))
                    act.wait_ge(v_ready, k + 1)
                    act.activation(y[c % 6][:, :], v[c % 2][:, :], ACT.Silu).then_inc(y_ready, 1)

                run_steps(act, K, U, [(4, ht_out), (SC + 1, silu), (7, root), (6, square)])

            @block.vector
            def _(dve):
                for m in range(2):
                    dve.memset(ss[m][:, :], 1.0).then_inc(ss_set, 1)

                def one_hot(i, c):
                    k = U * i + c
                    wait(dve, agg_done, k - 1)
                    for j in range(2):
                        last = dve.tensor_scalar(hot[c % 2][:, j, :], iota[:, 0:P], lane_of[:, bass.ds(2 * k + j, 1)], None,
                                                 ALU.is_equal)
                    last.then_inc(hot_made, 1)

                def degree(i, c):
                    k = U * i + c
                    dve.wait_ge(agg_done, k + 1)
                    wait(dve, rdeg_ready, k - 1)
                    dve.tensor_scalar(dg[c % 2][:, :], deg_ps[c % 2][:, 0:4:2], 1.0, None, ALU.max).then_inc(deg_raised, 1)

                def invert_degree(i, c):
                    k = U * i + c
                    dve.wait_ge(deg_raised, k + 1)
                    dve.reciprocal(rdeg[:, bass.ds(2 * k, 2)], dg[c % 2][:, :]).then_inc(rdeg_ready, 1)

                def mean(i, c):
                    k = U * i + c
                    dve.wait_ge(agg_done, k + 1)
                    dve.wait_ge(h_in[c % 6], 16 * (i + c // 6 + 1))
                    wait(dve, ht_done, k - 1)
                    if not last_layer:
                        dve.wait_ge(rdeg_ready, k + 1)
                    for j in range(2):
                        half = slice(j * D, (j + 1) * D)
                        last = dve.scalar_tensor_tensor(out=hm[c % 2][:, half], in0=agg_ps[c % 2][:, half],
                                                        scalar=rdeg[:, bass.ds(2 * k + j, 1)], in1=hb[c % 6][:, half],
                                                        op0=ALU.mult, op1=ALU.add)
                    last.then_inc(hm_ready, 1)

                def by_gain(i, c):
                    k = U * i + c
                    wait(dve, v_ready, k - 5)
                    dve.wait_ge(z_done, k + 1)
                    dve.tensor_tensor(u[c % 6][:, :], z_ps[c % 2][:, :], g_wide[:, :], ALU.mult).then_inc(u_ready, 1)

                def invert(i, c):
                    k = U * i + c
                    if c % 3 != 2 and not (isinstance(k, int) and k == K - 1):
                        return
                    group = (U // 3) * i + c // 3
                    wait(dve, v_ready, 3 * (group - 1))
                    dve.wait_ge(sd_done, group + 1)
                    dve.reciprocal(rs[c // 3 % 2][:, :], sd[c // 3 % 2][:, :]).then_inc(rs_done, 1)

                def scale(i, c):
                    k = U * i + c
                    wait(dve, y_ready, k - 1)
                    dve.wait_ge(u_ready, k + 1)
                    dve.wait_ge(rs_done, (U // 3) * i + c // 3 + 1)
                    for j in range(2):
                        half = slice(j * D, (j + 1) * D)
                        m = 2 * (c % 3) + j
                        last = dve.scalar_tensor_tensor(out=v[c % 2][:, half], in0=u[c % 6][:, half],
                                                        scalar=rs[c // 3 % 2][:, m:m + 1], in1=b_wide[:, :],
                                                        op0=ALU.mult, op1=ALU.add)
                    last.then_inc(v_ready, 1)

                def residual(i, c):
                    k = U * i + c
                    dve.wait_ge(y_ready, k + 1)
                    dve.wait_ge(x_in[c % 6], 16 * (i + c // 6 + 1))
                    wait(dve, stored[c % 6], 16 * (i + c // 6))
                    dve.tensor_tensor(res[c % 6][:, :], y[c % 6][:, :], xb[c % 6][:, :], ALU.add).then_inc(res_ready, 1)

                stages = [(6, by_gain)] + ([(2, degree)] if not last_layer else [(SC + 2, residual)])
                stages += [(0, one_hot), (8, invert)] + ([] if last_layer else [(2, invert_degree)])
                run_steps(dve, K, U, stages + [(2, mean), (SC, scale)])


_INS = ['x', 'src', 'dst', 'edge_attr_17', 'L0_gnn_ew1', 'L0_gnn_eb1', 'L0_gnn_ew2', 'L0_gnn_eb2', 'L0_gnn_lew',
        'L0_gnn_leb', 'L0_gnn_w1', 'L0_gnn_b1', 'L0_gnn_ln_g', 'L0_gnn_ln_b', 'L0_gnn_w2', 'L0_gnn_b2',
        'L1_gnn_W0', 'L1_gnn_b0', 'L1_gnn_g0', 'L1_gnn_beta0', 'L1_gnn_W1', 'L1_gnn_b1', 'L1_gnn_g1', 'L1_gnn_beta1']


def kernel(**inputs):
    import numpy as _np
    import concourse.bacc as _bacc
    from concourse import mybir as _mybir
    from concourse.bass_utils import run_bass_kernel_spmd as _run

    nc = _bacc.Bacc("TRN2", target_bir_lowering=False, num_devices=1)
    arrays, args = {}, []
    for name in _INS:
        a = _np.asarray(inputs[name])
        if name in ('L1_gnn_W0', 'L1_gnn_W1'):
            a = a.T
        a = _np.ascontiguousarray(a)
        arrays[f"in_{name}_dram"] = a
        args.append(nc.dram_tensor(f"in_{name}_dram", a.shape, _mybir.dt.from_np(a.dtype), kind="ExternalInput").ap())
    shape = _np.asarray(inputs['x']).shape
    args.append(nc.dram_tensor("out_0_dram", shape, _mybir.dt.from_np(_np.dtype('float32')), kind="ExternalOutput").ap())
    program(nc, *args)
    r = _run(nc, [arrays], core_ids=[0])
    return r.results[0]["out_0_dram"]
```
